# Optimizing a Trainium2 kernel written in Bass

```python
import numpy as np
import jax
import jax.numpy as jnp

def _softmax(x, axis=-1):
    return jax.nn.softmax(x, axis=axis)

def _gelu(x):
    return jax.nn.gelu(x, approximate=True)

def _silu(x):
    return jax.nn.silu(x)

def _sigmoid(x):
    return jax.nn.sigmoid(x)

def _layernorm(x, axis=-1, eps=1e-05):
    m = jnp.mean(x, axis=axis, keepdims=True)
    v = jnp.var(x, axis=axis, keepdims=True)
    return (x - m) / jnp.sqrt(v + eps)

def _scatter_add(tgt, idx, src, axis=0):
    return tgt.at[idx].add(src)

def _segment_sum(src, seg, n):
    return jax.ops.segment_sum(src, seg, n)
kernel_name = 'mk_decoder_preln_d4_seqx_r4_089770'

def setup_inputs(seed: int=0):
    np.random.seed(seed)
    _w = jnp.asarray

    def _rec_inputs():
        import jax
        import jax.numpy as jnp
        _rk = jax.random.key(seed)
        x = 0.0002417 + 0.9998 * jax.random.normal(jax.random.fold_in(_rk, 1), (4, 512, 256), jnp.float32)
        _lenS = 512 - jax.random.randint(jax.random.fold_in(_rk, 7), (4,), 0, max(1, 512 // 4) + 1, jnp.int32)
        _lenS2 = 512 - jax.random.randint(jax.random.fold_in(_rk, 8), (4,), 0, max(1, 512 // 4) + 1, jnp.int32)
        _ctx_1024P = jax.random.normal(jax.random.fold_in(_rk, 11), (4, 16, 256), jnp.float32)
        _ctx_1024c = jax.random.dirichlet(jax.random.fold_in(_rk, 511), 0.3 * jnp.ones((16,), jnp.float32), (4, 512))
        _ctx_1024t = jnp.einsum('bsk,bkd->bsd', _ctx_1024c, _ctx_1024P)
        _ctx_1024t = _ctx_1024t * jax.lax.rsqrt(jnp.mean(jnp.square(_ctx_1024t)) + 1e-12) * 0.953939
        ctx_1024 = 7.22013e-05 + 1.00017 * (_ctx_1024t + 0.3 * jax.random.normal(jax.random.fold_in(_rk, 611), (4, 512, 256), jnp.float32))
        _validS = jnp.arange(512)[None, :] < _lenS[:, None]
        _validS2 = jnp.arange(512)[None, :] < _lenS2[:, None]
        _causal = jnp.tril(jnp.ones((512, 512), dtype=bool))
        mask_1x1xSxS2_bf1 = jnp.ones((1, 1, 512, 512), dtype=bool)
        mask_BxSxS2_ik1 = jnp.where(jnp.broadcast_to(_validS2[:, None, :], (4, 512, 512)), 1, 0).astype(jnp.int32)
        mask_BxS2_bf0 = jnp.logical_not(jnp.ones((4, 512), dtype=bool))
        return (x, ctx_1024, mask_1x1xSxS2_bf1, mask_BxSxS2_ik1, mask_BxS2_bf0)
    x, ctx_1024, mask_1x1xSxS2_bf1, mask_BxSxS2_ik1, mask_BxS2_bf0 = _rec_inputs()

    def _L0_attn_setup():
        import jax, jax.numpy as jnp
        import numpy as np
        D_MODEL = 256
        N_HEADS = 16
        HEAD_D = D_MODEL // N_HEADS
        B, T = (4, 1024)
        ROPE_BASE = 10000.0

        def _rope(x):
            Bx, Tx, Dx = x.shape
            half = Dx // 2
            inv_freq = 1.0 / ROPE_BASE ** (jnp.arange(half, dtype=jnp.float32) / half)
            ang = jnp.arange(Tx, dtype=jnp.float32)[:, None] * inv_freq[None, :]
            cos, sin = (jnp.cos(ang), jnp.sin(ang))
            x1 = x[..., 0::2]
            x2 = x[..., 1::2]
            r1 = x1 * cos - x2 * sin
            r2 = x1 * sin + x2 * cos
            out = jnp.stack([r1, r2], axis=-1).reshape(Bx, Tx, Dx)
            return out
        key = jax.random.key(seed)
        k_x, k_q, k_k, k_v = jax.random.split(key, 4)
        x = jax.random.normal(k_x, (B, T, D_MODEL), dtype=jnp.float32)
        bound = np.sqrt(6.0 / (HEAD_D * N_HEADS))
        shp = (HEAD_D, HEAD_D, N_HEADS)
        w_q = jax.random.uniform(k_q, shp, jnp.float32, -bound, bound)
        w_k = jax.random.uniform(k_k, shp, jnp.float32, -bound, bound)
        w_v = jax.random.uniform(k_v, shp, jnp.float32, -bound, bound)
        return {'x': x, 'w_q': w_q, 'w_k': w_k, 'w_v': w_v}
    _L0_attn_all = _L0_attn_setup()
    _L0_attn_in = {k: v for k, v in _L0_attn_all.items() if k in ('w_q', 'w_k', 'w_v')}
    del _L0_attn_all

    def _L0_xattn_setup():
        import jax, jax.numpy as jnp
        import numpy as np
        EMBED = 256
        HEADS = 16
        HEAD_DIM = EMBED // HEADS
        key = jax.random.key(seed)
        ks = jax.random.split(key, 8)
        N, L = (4, 512)
        values = jax.random.normal(ks[0], (N, L, EMBED), dtype=jnp.float32)
        keys_ = jax.random.normal(ks[1], (N, L, EMBED), dtype=jnp.float32)
        queries = jax.random.normal(ks[2], (N, L, EMBED), dtype=jnp.float32)
        s = 1.0 / np.sqrt(HEAD_DIM)
        Wv = jax.random.normal(ks[3], (HEAD_DIM, HEAD_DIM), dtype=jnp.float32) * s
        Wk = jax.random.normal(ks[4], (HEAD_DIM, HEAD_DIM), dtype=jnp.float32) * s
        Wq = jax.random.normal(ks[5], (HEAD_DIM, HEAD_DIM), dtype=jnp.float32) * s
        Wo = jax.random.normal(ks[6], (EMBED, EMBED), dtype=jnp.float32) * (1.0 / np.sqrt(EMBED))
        bo = jnp.zeros((EMBED,), dtype=jnp.float32)
        return {'values': values, 'keys': keys_, 'queries': queries, 'Wv': Wv, 'Wk': Wk, 'Wq': Wq, 'Wo': Wo, 'bo': bo}
    _L0_xattn_all = _L0_xattn_setup()
    _L0_xattn_in = {k: v for k, v in _L0_xattn_all.items() if k in ('Wv', 'Wk', 'Wq', 'Wo', 'bo')}
    del _L0_xattn_all

    def _L0_ffn_setup():
        import jax, jax.numpy as jnp
        import numpy as np
        HIDDEN = 256
        HEAD_DIM = 64
        N_EXPERTS = 16
        MIN_EXPERTS = 2
        B, T = (4, 512)

        def _normalize(x, axis):
            n = jnp.sqrt(jnp.sum(x * x, axis=axis, keepdims=True))
            return x / jnp.maximum(n, 1e-12)

        def _ste(x):
            hard = jax.lax.stop_gradient((x > 0).astype(x.dtype))
            return hard + x - jax.lax.stop_gradient(x)

        def _gating(hidden_states, sim_matrix, gates):
            b, t, c = hidden_states.shape
            flat = hidden_states.reshape(b * t, c)
            logits = _normalize(flat, -1) @ _normalize(sim_matrix, 0) - jax.nn.sigmoid(gates)
            gated = jax.nn.relu(logits)
            mask = _ste(gated)
            inactive = jnp.sum(mask, axis=1) == 0
            _, fb_idx = jax.lax.top_k(logits, MIN_EXPERTS)
            fb = jnp.zeros_like(mask).at[jnp.arange(b * t)[:, None], fb_idx].set(1.0)
            fb_applied = inactive[:, None] & (fb > 0)
            mask = jnp.where(fb_applied, 1.0, mask)
            masked_logits = jnp.where(mask > 0, gated, -jnp.inf)
            return jax.nn.softmax(masked_logits, axis=-1).reshape(b, t, -1)
        key = jax.random.key(seed)
        ks = jax.random.split(key, 6)
        xav_qkv = float(np.sqrt(6.0 / (HIDDEN + HEAD_DIM)))
        return {'hidden_states': jax.random.normal(ks[0], (B, T, HIDDEN), dtype=jnp.float32), 'sim_matrix': jax.random.normal(ks[1], (HIDDEN, N_EXPERTS), dtype=jnp.float32), 'gates': jnp.zeros((N_EXPERTS,), dtype=jnp.float32), 'q_proj': jax.random.uniform(ks[2], (N_EXPERTS, HIDDEN, HEAD_DIM), jnp.float32, -xav_qkv, xav_qkv), 'k_proj': jax.random.uniform(ks[3], (N_EXPERTS, HIDDEN, HEAD_DIM), jnp.float32, -xav_qkv, xav_qkv), 'v_proj': jax.random.uniform(ks[4], (N_EXPERTS, HIDDEN, HEAD_DIM), jnp.float32, -xav_qkv, xav_qkv), 'o_proj': jax.random.uniform(ks[5], (N_EXPERTS, HEAD_DIM, HIDDEN), jnp.float32, -xav_qkv, xav_qkv)}
    _L0_ffn_all = _L0_ffn_setup()
    _L0_ffn_in = {k: v for k, v in _L0_ffn_all.items() if k in ('sim_matrix', 'gates', 'q_proj', 'k_proj', 'v_proj', 'o_proj')}
    del _L0_ffn_all

    def _L1_attn_setup():
        import jax, jax.numpy as jnp
        import numpy as np
        HEADS = 16
        EPS = 1e-08

        def _attention(x, Wq, Wkv, Wo, heads=HEADS, causal=True, eps=EPS):
            B, N, D = x.shape
            dh = D // heads
            q = x @ Wq.T
            k, v = jnp.split(x @ Wkv.T, 2, axis=-1)

            def split_heads(t):
                return t.reshape(B, N, heads, dh).transpose(0, 2, 1, 3)
            q, k, v = map(split_heads, (q, k, v))
            q = q * dh ** (-0.5)
            sim = jnp.einsum('bhid,bhjd->bhij', q, k)
            mask_value = -jnp.finfo(sim.dtype).max
            if causal:
                causal_mask = jnp.triu(jnp.ones((N, N), dtype=bool), 1)
                sim = jnp.where(causal_mask, mask_value, sim)
            m = jax.lax.stop_gradient(jnp.max(sim, axis=-1, keepdims=True))
            e = jnp.exp(sim - m)
            num = jnp.einsum('bhij,bhjd->bhid', e, v)
            den = jnp.sum(e, axis=-1, keepdims=True) + eps
            out = num / den
            out = out.transpose(0, 2, 1, 3).reshape(B, N, D)
            return out @ Wo.T
        key = jax.random.key(seed)
        k0, k1, k2, k3 = jax.random.split(key, 4)
        B, N, D = (2, 512, 256)
        x = jax.random.normal(k0, (B, N, D), jnp.float32)
        Wq = jax.random.normal(k1, (D, D), jnp.float32) * 0.02
        Wkv = jax.random.normal(k2, (2 * D, D), jnp.float32) * 0.02
        Wo = jax.random.normal(k3, (D, D), jnp.float32) * 0.02
        return {'x': x, 'Wq': Wq, 'Wkv': Wkv, 'Wo': Wo}
    _L1_attn_all = _L1_attn_setup()
    _L1_attn_in = {k: v for k, v in _L1_attn_all.items() if k in ('Wq', 'Wkv', 'Wo')}
    del _L1_attn_all

    def _L1_xattn_setup():
        import jax, jax.numpy as jnp
        import numpy as np
        B, S, D = (4, 512, 256)
        key = jax.random.key(seed)
        ks = jax.random.split(key, 12)
        scale = 1.0 / np.sqrt(D)
        return {'q': jax.random.normal(ks[0], (B, S, D), jnp.float32), 'k': jax.random.normal(ks[1], (B, S, D), jnp.float32), 'v': jax.random.normal(ks[2], (B, S, D), jnp.float32), 'mask': jnp.ones((1, 1, S, S), dtype=bool), 'Wq': jax.random.normal(ks[3], (D, D), jnp.float32) * scale, 'bq': jnp.zeros((D,), jnp.float32), 'Wk': jax.random.normal(ks[4], (D, D), jnp.float32) * scale, 'bk': jnp.zeros((D,), jnp.float32), 'Wv': jax.random.normal(ks[5], (D, D), jnp.float32) * scale, 'bv': jnp.zeros((D,), jnp.float32), 'Wo': jax.random.normal(ks[6], (D, D), jnp.float32) * scale, 'bo': jnp.zeros((D,), jnp.float32)}
    _L1_xattn_all = _L1_xattn_setup()
    _L1_xattn_in = {k: v for k, v in _L1_xattn_all.items() if k in ('Wq', 'bq', 'Wk', 'bk', 'Wv', 'bv', 'Wo', 'bo')}
    del _L1_xattn_all

    def _L1_ffn_setup():
        import jax, jax.numpy as jnp
        import numpy as np
        EPS = 1e-06
        LN_EPS = 1e-05

        def _absmean_core(W):
            gamma = jnp.mean(jnp.abs(W)) + EPS
            Ws = W / gamma
            Wq = jnp.sign(Ws) * jnp.minimum(jnp.round(jnp.abs(Ws)), 1.0)
            return (Wq, gamma)

        @jax.custom_vjp
        def absmean(W):
            return _absmean_core(W)[0]

        def _absmean_fwd(W):
            Wq, gamma = _absmean_core(W)
            return (Wq, gamma)

        def _absmean_bwd(gamma, g):
            return (g / gamma,)
        absmean.defvjp(_absmean_fwd, _absmean_bwd)

        def layernorm(x, w, b, eps=LN_EPS):
            mu = jnp.mean(x, axis=-1, keepdims=True)
            var = jnp.mean((x - mu) ** 2, axis=-1, keepdims=True)
            return (x - mu) * jax.lax.rsqrt(var + eps) * w + b
        key = jax.random.key(seed)
        k1, k2, k3 = jax.random.split(key, 3)
        d, h = (256, 1024)
        B, T = (8, 512)
        return {'x': jax.random.normal(k1, (B, T, d), jnp.float32), 'W_fc': jax.random.normal(k2, (h, d), jnp.float32), 'ln_w': jnp.ones((h,), jnp.float32), 'ln_b': jnp.zeros((h,), jnp.float32), 'W_proj': jax.random.normal(k3, (d, h), jnp.float32)}
    _L1_ffn_all = _L1_ffn_setup()
    _L1_ffn_in = {k: v for k, v in _L1_ffn_all.items() if k in ('W_fc', 'ln_w', 'ln_b', 'W_proj')}
    del _L1_ffn_all

    def _L2_attn_setup():
        import jax, jax.numpy as jnp
        import numpy as np
        H = 16

        def _kernel(x, gamma, beta):
            mean = x.mean(axis=-1, keepdims=True)
            std = jnp.std(x, axis=-1, ddof=1, keepdims=True)
            xn = (x - mean) / (std + 1e-06)
            return jnp.square(gamma * xn + beta)
        key = jax.random.key(seed)
        ks = jax.random.split(key, 9)
        B, T, C = (2, 512, 256)
        x = jax.random.normal(ks[0], (B, T, C), jnp.float32)
        Wqkv = jax.random.normal(ks[1], (C, 3 * C), jnp.float32) * 0.02
        bqkv = jnp.zeros((3 * C,), jnp.float32)
        gamma_q = jax.random.uniform(ks[2], (C,), jnp.float32)
        beta_q = jax.random.uniform(ks[3], (C,), jnp.float32)
        gamma_k = jax.random.uniform(ks[4], (C,), jnp.float32)
        beta_k = jax.random.uniform(ks[5], (C,), jnp.float32)
        Wo = jax.random.normal(ks[6], (C, C), jnp.float32) * 0.02
        bo = jnp.zeros((C,), jnp.float32)
        return {'x': x, 'Wqkv': Wqkv, 'bqkv': bqkv, 'gamma_q': gamma_q, 'beta_q': beta_q, 'gamma_k': gamma_k, 'beta_k': beta_k, 'Wo': Wo, 'bo': bo}
    _L2_attn_all = _L2_attn_setup()
    _L2_attn_in = {k: v for k, v in _L2_attn_all.items() if k in ('Wqkv', 'bqkv', 'gamma_q', 'beta_q', 'gamma_k', 'beta_k', 'Wo', 'bo')}
    del _L2_attn_all

    def _L2_xattn_setup():
        import jax, jax.numpy as jnp
        import numpy as np
        B, T, D = (4, 512, 256)
        H, DK, DV = (16, 64, 64)
        key = jax.random.key(seed)
        ks = jax.random.split(key, 12)
        s = 0.02
        return {'query': jax.random.normal(ks[0], (B, T, D), jnp.float32), 'key': jax.random.normal(ks[1], (B, T, D), jnp.float32), 'value': jax.random.normal(ks[2], (B, T, D), jnp.float32), 'mask': jax.random.randint(ks[3], (B, T, T), 0, 2, jnp.int32), 'Wq': jax.random.normal(ks[4], (H * DK, D), jnp.float32) * s, 'bq': jnp.zeros((H * DK,), jnp.float32), 'Wk': jax.random.normal(ks[5], (H * DK, D), jnp.float32) * s, 'bk': jnp.zeros((H * DK,), jnp.float32), 'Wv': jax.random.normal(ks[6], (H * DV, D), jnp.float32) * s, 'bv': jnp.zeros((H * DV,), jnp.float32), 'Wo': jax.random.normal(ks[7], (D, H * DV), jnp.float32) * s, 'bo': jnp.zeros((D,), jnp.float32)}
    _L2_xattn_all = _L2_xattn_setup()
    _L2_xattn_in = {k: v for k, v in _L2_xattn_all.items() if k in ('Wq', 'bq', 'Wk', 'bk', 'Wv', 'bv', 'Wo', 'bo')}
    del _L2_xattn_all

    def _L2_ffn_setup():
        import jax, jax.numpy as jnp
        import numpy as np
        B, T, D, F, E = (2, 256, 256, 1024, 8)
        EPS = 1e-06
        key = jax.random.key(seed)
        k = jax.random.split(key, 5)
        scale = 0.02
        return {'x': jax.random.normal(k[0], (B, T, D), dtype=jnp.float32), 'rms_w': jnp.ones((D,), dtype=jnp.float32), 'gate_w': jax.random.normal(k[1], (E, D), dtype=jnp.float32) * scale, 'W1': jax.random.normal(k[2], (E, D, F), dtype=jnp.float32) * scale, 'b1': jnp.zeros((E, F), dtype=jnp.float32), 'W2': jax.random.normal(k[3], (E, F, D), dtype=jnp.float32) * scale, 'b2': jnp.zeros((E, D), dtype=jnp.float32)}
    _L2_ffn_all = _L2_ffn_setup()
    _L2_ffn_in = {k: v for k, v in _L2_ffn_all.items() if k in ('rms_w', 'gate_w', 'W1', 'b1', 'W2', 'b2')}
    del _L2_ffn_all

    def _L3_attn_setup():
        import jax, jax.numpy as jnp
        import numpy as np
        NUM_HEADS = 16
        ROPE_BASE = 10000.0

        def _rotate_half(x):
            xr = x.reshape(*x.shape[:-1], -1, 2)
            x1, x2 = (xr[..., 0], xr[..., 1])
            return jnp.stack((-x2, x1), axis=-1).reshape(x.shape)

        def _rope(x):
            hd = x.shape[-1]
            n = x.shape[-2]
            inv_freq = 1.0 / ROPE_BASE ** (jnp.arange(0, hd, 2, dtype=jnp.float32) / hd)
            freqs = jnp.outer(jnp.arange(n, dtype=jnp.float32), inv_freq)
            freqs = jnp.repeat(freqs, 2, axis=-1)
            return x * jnp.cos(freqs) + _rotate_half(x) * jnp.sin(freqs)
        key = jax.random.key(seed)
        k0, k1, k2 = jax.random.split(key, 3)
        B, N, D = (2, 512, 256)
        X = jax.random.normal(k0, (B, N, D), jnp.float32)
        Wqkv = jax.random.normal(k1, (D, 3 * D), jnp.float32) * D ** (-0.5)
        Wout = jax.random.normal(k2, (D, D), jnp.float32) * D ** (-0.5)
        bout = jnp.zeros((D,), jnp.float32)
        return {'X': X, 'Wqkv': Wqkv, 'Wout': Wout, 'bout': bout}
    _L3_attn_all = _L3_attn_setup()
    _L3_attn_in = {k: v for k, v in _L3_attn_all.items() if k in ('Wqkv', 'Wout', 'bout')}
    del _L3_attn_all

    def _L3_xattn_setup():
        import jax, jax.numpy as jnp
        import numpy as np
        B, L1, L2, FULL, H = (8, 512, 512, 256, 256)
        NEG_INF = -1e+30
        key = jax.random.key(seed)
        k1, k2, k3, k4, k5 = jax.random.split(key, 5)
        xh1 = jax.random.normal(k1, (B, L1, FULL), dtype=jnp.float32)
        xh2 = jax.random.normal(k2, (B, L2, FULL), dtype=jnp.float32)
        x2 = jax.random.normal(k3, (B, L2, H), dtype=jnp.float32)
        x2_mask = jnp.zeros((B, L2), dtype=bool)
        W = jax.random.normal(k4, (FULL, FULL), dtype=jnp.float32) / np.sqrt(FULL)
        b = jnp.zeros((FULL,), dtype=jnp.float32)
        D = jnp.ones((1, FULL), dtype=jnp.float32)
        return {'xh1': xh1, 'xh2': xh2, 'x2': x2, 'x2_mask': x2_mask, 'W': W, 'b': b, 'D': D}
    _L3_xattn_all = _L3_xattn_setup()
    _L3_xattn_in = {k: v for k, v in _L3_xattn_all.items() if k in ('W', 'b', 'D')}
    del _L3_xattn_all

    def _L3_ffn_setup():
        import jax, jax.numpy as jnp
        import numpy as np
        TOP_K = 4
        key = jax.random.key(seed)
        ks = jax.random.split(key, 5)
        B, T, D = (2, 256, 256)
        P, PD = (64, 32)
        return {'x': jax.random.normal(ks[0], (B, T, D), dtype=jnp.float32), 'hasher_w': jax.random.normal(ks[1], (PD, D), dtype=jnp.float32) * 0.03, 'keys': jax.random.normal(ks[2], (P, PD), dtype=jnp.float32) * 0.1, 'values_down': jax.random.normal(ks[3], (P, D, PD), dtype=jnp.float32) * 0.01, 'values_up': jax.random.normal(ks[4], (P, PD, D), dtype=jnp.float32) * 0.01, 'scale': jnp.full((1,), 0.1, dtype=jnp.float32)}
    _L3_ffn_all = _L3_ffn_setup()
    _L3_ffn_in = {k: v for k, v in _L3_ffn_all.items() if k in ('hasher_w', 'keys', 'values_down', 'values_up', 'scale')}
    del _L3_ffn_all
    return {'x': x, 'ctx_1024': ctx_1024, 'mask_1x1xSxS2_bf1': mask_1x1xSxS2_bf1, 'mask_BxSxS2_ik1': mask_BxSxS2_ik1, 'mask_BxS2_bf0': mask_BxS2_bf0, 'L0_attn_w_q': _L0_attn_in['w_q'], 'L0_attn_w_k': _L0_attn_in['w_k'], 'L0_attn_w_v': _L0_attn_in['w_v'], 'L0_xattn_Wv': _L0_xattn_in['Wv'], 'L0_xattn_Wk': _L0_xattn_in['Wk'], 'L0_xattn_Wq': _L0_xattn_in['Wq'], 'L0_xattn_Wo': _L0_xattn_in['Wo'], 'L0_xattn_bo': _L0_xattn_in['bo'], 'L0_ffn_sim_matrix': _L0_ffn_in['sim_matrix'], 'L0_ffn_gates': _L0_ffn_in['gates'], 'L0_ffn_q_proj': _L0_ffn_in['q_proj'], 'L0_ffn_k_proj': _L0_ffn_in['k_proj'], 'L0_ffn_v_proj': _L0_ffn_in['v_proj'], 'L0_ffn_o_proj': _L0_ffn_in['o_proj'], 'L1_attn_Wq': _L1_attn_in['Wq'], 'L1_attn_Wkv': _L1_attn_in['Wkv'], 'L1_attn_Wo': _L1_attn_in['Wo'], 'L1_xattn_Wq': _L1_xattn_in['Wq'], 'L1_xattn_bq': _L1_xattn_in['bq'], 'L1_xattn_Wk': _L1_xattn_in['Wk'], 'L1_xattn_bk': _L1_xattn_in['bk'], 'L1_xattn_Wv': _L1_xattn_in['Wv'], 'L1_xattn_bv': _L1_xattn_in['bv'], 'L1_xattn_Wo': _L1_xattn_in['Wo'], 'L1_xattn_bo': _L1_xattn_in['bo'], 'L1_ffn_W_fc': _L1_ffn_in['W_fc'], 'L1_ffn_ln_w': _L1_ffn_in['ln_w'], 'L1_ffn_ln_b': _L1_ffn_in['ln_b'], 'L1_ffn_W_proj': _L1_ffn_in['W_proj'], 'L2_attn_Wqkv': _L2_attn_in['Wqkv'], 'L2_attn_bqkv': _L2_attn_in['bqkv'], 'L2_attn_gamma_q': _L2_attn_in['gamma_q'], 'L2_attn_beta_q': _L2_attn_in['beta_q'], 'L2_attn_gamma_k': _L2_attn_in['gamma_k'], 'L2_attn_beta_k': _L2_attn_in['beta_k'], 'L2_attn_Wo': _L2_attn_in['Wo'], 'L2_attn_bo': _L2_attn_in['bo'], 'L2_xattn_Wq': _L2_xattn_in['Wq'], 'L2_xattn_bq': _L2_xattn_in['bq'], 'L2_xattn_Wk': _L2_xattn_in['Wk'], 'L2_xattn_bk': _L2_xattn_in['bk'], 'L2_xattn_Wv': _L2_xattn_in['Wv'], 'L2_xattn_bv': _L2_xattn_in['bv'], 'L2_xattn_Wo': _L2_xattn_in['Wo'], 'L2_xattn_bo': _L2_xattn_in['bo'], 'L2_ffn_rms_w': _L2_ffn_in['rms_w'], 'L2_ffn_gate_w': _L2_ffn_in['gate_w'], 'L2_ffn_W1': _L2_ffn_in['W1'], 'L2_ffn_b1': _L2_ffn_in['b1'], 'L2_ffn_W2': _L2_ffn_in['W2'], 'L2_ffn_b2': _L2_ffn_in['b2'], 'L3_attn_Wqkv': _L3_attn_in['Wqkv'], 'L3_attn_Wout': _L3_attn_in['Wout'], 'L3_attn_bout': _L3_attn_in['bout'], 'L3_xattn_W': _L3_xattn_in['W'], 'L3_xattn_b': _L3_xattn_in['b'], 'L3_xattn_D': _L3_xattn_in['D'], 'L3_ffn_hasher_w': _L3_ffn_in['hasher_w'], 'L3_ffn_keys': _L3_ffn_in['keys'], 'L3_ffn_values_down': _L3_ffn_in['values_down'], 'L3_ffn_values_up': _L3_ffn_in['values_up'], 'L3_ffn_scale': _L3_ffn_in['scale']}

def reference(x, ctx_1024, mask_1x1xSxS2_bf1, mask_BxSxS2_ik1, mask_BxS2_bf0, L0_attn_w_q, L0_attn_w_k, L0_attn_w_v, L0_xattn_Wv, L0_xattn_Wk, L0_xattn_Wq, L0_xattn_Wo, L0_xattn_bo, L0_ffn_sim_matrix, L0_ffn_gates, L0_ffn_q_proj, L0_ffn_k_proj, L0_ffn_v_proj, L0_ffn_o_proj, L1_attn_Wq, L1_attn_Wkv, L1_attn_Wo, L1_xattn_Wq, L1_xattn_bq, L1_xattn_Wk, L1_xattn_bk, L1_xattn_Wv, L1_xattn_bv, L1_xattn_Wo, L1_xattn_bo, L1_ffn_W_fc, L1_ffn_ln_w, L1_ffn_ln_b, L1_ffn_W_proj, L2_attn_Wqkv, L2_attn_bqkv, L2_attn_gamma_q, L2_attn_beta_q, L2_attn_gamma_k, L2_attn_beta_k, L2_attn_Wo, L2_attn_bo, L2_xattn_Wq, L2_xattn_bq, L2_xattn_Wk, L2_xattn_bk, L2_xattn_Wv, L2_xattn_bv, L2_xattn_Wo, L2_xattn_bo, L2_ffn_rms_w, L2_ffn_gate_w, L2_ffn_W1, L2_ffn_b1, L2_ffn_W2, L2_ffn_b2, L3_attn_Wqkv, L3_attn_Wout, L3_attn_bout, L3_xattn_W, L3_xattn_b, L3_xattn_D, L3_ffn_hasher_w, L3_ffn_keys, L3_ffn_values_down, L3_ffn_values_up, L3_ffn_scale):
    import jax
    import jax.numpy as jnp

    def _L0_attn_ref(x, w_q, w_k, w_v):
        import jax, jax.numpy as jnp
        import numpy as np
        D_MODEL = 256
        N_HEADS = 16
        HEAD_D = D_MODEL // N_HEADS
        B, T = (4, 1024)
        ROPE_BASE = 10000.0

        def _rope(x):
            Bx, Tx, Dx = x.shape
            half = Dx // 2
            inv_freq = 1.0 / ROPE_BASE ** (jnp.arange(half, dtype=jnp.float32) / half)
            ang = jnp.arange(Tx, dtype=jnp.float32)[:, None] * inv_freq[None, :]
            cos, sin = (jnp.cos(ang), jnp.sin(ang))
            x1 = x[..., 0::2]
            x2 = x[..., 1::2]
            r1 = x1 * cos - x2 * sin
            r2 = x1 * sin + x2 * cos
            out = jnp.stack([r1, r2], axis=-1).reshape(Bx, Tx, Dx)
            return out
        Bx, Tx, Dx = x.shape
        d = Dx // N_HEADS
        xh = x.reshape(Bx, Tx, d, N_HEADS)
        q = jnp.einsum('btqh,qdh->btdh', xh, w_q).reshape(Bx, Tx, Dx)
        k = jnp.einsum('btkh,kdh->btdh', xh, w_k).reshape(Bx, Tx, Dx)
        v = jnp.einsum('btvh,vdh->btdh', xh, w_v).reshape(Bx, Tx, Dx)
        q = _rope(q)
        k = _rope(k)
        gamma = 1.0 / jnp.sqrt(jnp.float32(Dx))
        scores = jnp.einsum('bqd,bkd->bqk', q, k) * gamma
        causal = jnp.tril(jnp.ones((Tx, Tx), dtype=bool))
        scores = jnp.where(causal[None], scores, -jnp.inf)
        attn = jax.nn.softmax(scores, axis=-1)
        y = jnp.einsum('bqt,btd->bqd', attn, v)
        return y

    def _L0_xattn_ref(values, keys, queries, Wv, Wk, Wq, Wo, bo):
        import jax, jax.numpy as jnp
        import numpy as np
        EMBED = 256
        HEADS = 16
        HEAD_DIM = EMBED // HEADS
        N, L, _ = queries.shape
        v = values.reshape(N, -1, HEADS, HEAD_DIM)
        k = keys.reshape(N, -1, HEADS, HEAD_DIM)
        q = queries.reshape(N, L, HEADS, HEAD_DIM)
        v = jnp.einsum('nlhd,ed->nlhe', v, Wv)
        k = jnp.einsum('nlhd,ed->nlhe', k, Wk)
        q = jnp.einsum('nqhd,ed->nqhe', q, Wq)
        scores = jnp.einsum('nqhd,nkhd->nhqk', q, k) / jnp.sqrt(jnp.float32(EMBED))
        attn = jax.nn.softmax(scores, axis=-1)
        out = jnp.einsum('nhqk,nkhd->nqhd', attn, v).reshape(N, L, EMBED)
        return out @ Wo.T + bo

    def _L0_ffn_ref(hidden_states, sim_matrix, gates, q_proj, k_proj, v_proj, o_proj):
        import jax, jax.numpy as jnp
        import numpy as np
        HIDDEN = 256
        HEAD_DIM = 64
        N_EXPERTS = 16
        MIN_EXPERTS = 2
        B, T = (4, 512)

        def _normalize(x, axis):
            n = jnp.sqrt(jnp.sum(x * x, axis=axis, keepdims=True))
            return x / jnp.maximum(n, 1e-12)

        def _ste(x):
            hard = jax.lax.stop_gradient((x > 0).astype(x.dtype))
            return hard + x - jax.lax.stop_gradient(x)

        def _gating(hidden_states, sim_matrix, gates):
            b, t, c = hidden_states.shape
            flat = hidden_states.reshape(b * t, c)
            logits = _normalize(flat, -1) @ _normalize(sim_matrix, 0) - jax.nn.sigmoid(gates)
            gated = jax.nn.relu(logits)
            mask = _ste(gated)
            inactive = jnp.sum(mask, axis=1) == 0
            _, fb_idx = jax.lax.top_k(logits, MIN_EXPERTS)
            fb = jnp.zeros_like(mask).at[jnp.arange(b * t)[:, None], fb_idx].set(1.0)
            fb_applied = inactive[:, None] & (fb > 0)
            mask = jnp.where(fb_applied, 1.0, mask)
            masked_logits = jnp.where(mask > 0, gated, -jnp.inf)
            return jax.nn.softmax(masked_logits, axis=-1).reshape(b, t, -1)
        b, t, c = hidden_states.shape
        rw = _gating(hidden_states, sim_matrix, gates)
        q = jnp.einsum('bte,bted->btd', rw, jnp.einsum('btc,ecd->bted', hidden_states, q_proj))
        k = jnp.einsum('bte,bted->btd', rw, jnp.einsum('btc,ecd->bted', hidden_states, k_proj))
        v = jnp.einsum('bte,bted->btd', rw, jnp.einsum('btc,ecd->bted', hidden_states, v_proj))
        scale = 1.0 / jnp.sqrt(jnp.asarray(HEAD_DIM, dtype=q.dtype))
        scores = jnp.einsum('bqd,bkd->bqk', q, k) * scale
        causal = jnp.tril(jnp.ones((t, t), dtype=bool))
        scores = jnp.where(causal, scores, -jnp.inf)
        attn = jnp.einsum('bqk,bkd->bqd', jax.nn.softmax(scores, axis=-1), v)
        mixed = attn[:, :, None, :] * rw[..., None]
        return jnp.einsum('bted,edc->btc', mixed, o_proj)

    def _L1_attn_ref(x, Wq, Wkv, Wo):
        import jax, jax.numpy as jnp
        import numpy as np
        HEADS = 16
        EPS = 1e-08

        def _attention(x, Wq, Wkv, Wo, heads=HEADS, causal=True, eps=EPS):
            B, N, D = x.shape
            dh = D // heads
            q = x @ Wq.T
            k, v = jnp.split(x @ Wkv.T, 2, axis=-1)

            def split_heads(t):
                return t.reshape(B, N, heads, dh).transpose(0, 2, 1, 3)
            q, k, v = map(split_heads, (q, k, v))
            q = q * dh ** (-0.5)
            sim = jnp.einsum('bhid,bhjd->bhij', q, k)
            mask_value = -jnp.finfo(sim.dtype).max
            if causal:
                causal_mask = jnp.triu(jnp.ones((N, N), dtype=bool), 1)
                sim = jnp.where(causal_mask, mask_value, sim)
            m = jax.lax.stop_gradient(jnp.max(sim, axis=-1, keepdims=True))
            e = jnp.exp(sim - m)
            num = jnp.einsum('bhij,bhjd->bhid', e, v)
            den = jnp.sum(e, axis=-1, keepdims=True) + eps
            out = num / den
            out = out.transpose(0, 2, 1, 3).reshape(B, N, D)
            return out @ Wo.T
        return _attention(x, Wq, Wkv, Wo)

    def _L1_xattn_ref(q, k, v, mask, Wq, bq, Wk, bk, Wv, bv, Wo, bo):
        import jax, jax.numpy as jnp
        import numpy as np
        B, S, D = (4, 512, 256)
        query = q @ Wq + bq
        key = k @ Wk + bk
        value = v @ Wv + bv
        d_k = query.shape[-1]
        scores = jnp.einsum('bqd,bkd->bqk', query, key) / jnp.sqrt(jnp.float32(d_k))
        attn = jax.nn.softmax(scores, axis=-1)
        x = jnp.einsum('bqk,bkd->bqd', attn, value)
        b, s, d = x.shape
        x = jnp.swapaxes(x, 1, 2).reshape(b, s, d)
        return x @ Wo + bo

    def _L1_ffn_ref(x, W_fc, ln_w, ln_b, W_proj):
        import jax, jax.numpy as jnp
        import numpy as np
        EPS = 1e-06
        LN_EPS = 1e-05

        def _absmean_core(W):
            gamma = jnp.mean(jnp.abs(W)) + EPS
            Ws = W / gamma
            Wq = jnp.sign(Ws) * jnp.minimum(jnp.round(jnp.abs(Ws)), 1.0)
            return (Wq, gamma)

        @jax.custom_vjp
        def absmean(W):
            return _absmean_core(W)[0]

        def _absmean_fwd(W):
            Wq, gamma = _absmean_core(W)
            return (Wq, gamma)

        def _absmean_bwd(gamma, g):
            return (g / gamma,)
        absmean.defvjp(_absmean_fwd, _absmean_bwd)

        def layernorm(x, w, b, eps=LN_EPS):
            mu = jnp.mean(x, axis=-1, keepdims=True)
            var = jnp.mean((x - mu) ** 2, axis=-1, keepdims=True)
            return (x - mu) * jax.lax.rsqrt(var + eps) * w + b
        h = jnp.einsum('btd,hd->bth', x, absmean(W_fc))
        h = jax.nn.gelu(h, approximate=False)
        h = layernorm(h, ln_w, ln_b)
        return jnp.einsum('bth,dh->btd', h, absmean(W_proj))

    def _L2_attn_ref(x, Wqkv, bqkv, gamma_q, beta_q, gamma_k, beta_k, Wo, bo):
        import jax, jax.numpy as jnp
        import numpy as np
        H = 16

        def _kernel(x, gamma, beta):
            mean = x.mean(axis=-1, keepdims=True)
            std = jnp.std(x, axis=-1, ddof=1, keepdims=True)
            xn = (x - mean) / (std + 1e-06)
            return jnp.square(gamma * xn + beta)
        B, T, C = x.shape
        D = C // H
        qkv = x @ Wqkv + bqkv
        q, k, v = jnp.split(qkv, 3, axis=2)
        kerq = _kernel(q, gamma_q, beta_q)
        kerk = _kernel(k, gamma_k, beta_k)
        kerq = kerq.reshape(B, T, H, D).transpose(0, 2, 1, 3)
        kerk = kerk.reshape(B, T, H, D).transpose(0, 2, 1, 3)
        vh = v.reshape(B, T, H, D).transpose(0, 2, 1, 3)
        kv = jnp.cumsum(jnp.einsum('bhtf,bhtg->bhtfg', kerk, vh), axis=2)
        out = jnp.einsum('bhtf,bhtfg->bhtg', kerq, kv)
        Z = 1.0 / (jnp.einsum('bhtf,bhtf->bht', kerq, jnp.cumsum(kerk, axis=2)) + 1e-06)
        out = out * Z[..., None]
        out = out.transpose(0, 2, 1, 3).reshape(B, T, C)
        return out @ Wo + bo

    def _L2_xattn_ref(query, key, value, mask, Wq, bq, Wk, bk, Wv, bv, Wo, bo):
        import jax, jax.numpy as jnp
        import numpy as np
        B, T, D = (4, 512, 256)
        H, DK, DV = (16, 64, 64)
        b = query.shape[0]
        q = (query @ Wq.T + bq).reshape(b, -1, H, DK).transpose(0, 2, 1, 3)
        k = (key @ Wk.T + bk).reshape(b, -1, H, DK).transpose(0, 2, 1, 3)
        v = (value @ Wv.T + bv).reshape(b, -1, H, DV).transpose(0, 2, 1, 3)
        scores = jnp.einsum('bhqd,bhkd->bhqk', q, k) / jnp.sqrt(jnp.float32(DK))
        m = mask[:, None, :, :] == 0
        scores = jnp.where(m, jnp.float32(-1e+20), scores)
        attn = jax.nn.softmax(scores, axis=-1)
        attn = jnp.where(m, 0.0, attn)
        x = jnp.einsum('bhqk,bhkd->bhqd', attn, v)
        x = x.transpose(0, 2, 1, 3).reshape(b, -1, H * DV)
        return x @ Wo.T + bo

    def _L2_ffn_ref(x, rms_w, gate_w, W1, b1, W2, b2):
        import jax, jax.numpy as jnp
        import numpy as np
        B, T, D, F, E = (2, 256, 256, 1024, 8)
        EPS = 1e-06
        ms = jnp.mean(x * x, axis=-1, keepdims=True)
        xn = x * jax.lax.rsqrt(ms + EPS) * rms_w
        logits = jnp.einsum('btd,ed->bte', xn, gate_w)
        scores = jax.nn.softmax(logits, axis=-1)
        top1_idx = jnp.argmax(scores, axis=-1)
        top1_score = jnp.max(scores, axis=-1)
        out = jnp.zeros_like(xn)
        for e in range(E):
            h = jax.nn.silu(jnp.einsum('btd,df->btf', xn, W1[e]) + b1[e])
            ye = jnp.einsum('btf,fd->btd', h, W2[e]) + b2[e]
            out = jnp.where((top1_idx == e)[..., None], ye, out)
        return out * top1_score[..., None]

    def _L3_attn_ref(X, Wqkv, Wout, bout):
        import jax, jax.numpy as jnp
        import numpy as np
        NUM_HEADS = 16
        ROPE_BASE = 10000.0

        def _rotate_half(x):
            xr = x.reshape(*x.shape[:-1], -1, 2)
            x1, x2 = (xr[..., 0], xr[..., 1])
            return jnp.stack((-x2, x1), axis=-1).reshape(x.shape)

        def _rope(x):
            hd = x.shape[-1]
            n = x.shape[-2]
            inv_freq = 1.0 / ROPE_BASE ** (jnp.arange(0, hd, 2, dtype=jnp.float32) / hd)
            freqs = jnp.outer(jnp.arange(n, dtype=jnp.float32), inv_freq)
            freqs = jnp.repeat(freqs, 2, axis=-1)
            return x * jnp.cos(freqs) + _rotate_half(x) * jnp.sin(freqs)
        B, N, D = X.shape
        H = NUM_HEADS
        hd = D // H
        scale = hd ** (-0.5)
        qkv = X @ Wqkv
        q, k, v = jnp.split(qkv, 3, axis=-1)

        def to_heads(t):
            return t.reshape(B, N, H, hd).transpose(0, 2, 1, 3)
        Q, K, V = (to_heads(q), to_heads(k), to_heads(v))
        Q = _rope(Q)
        K = _rope(K)
        scores = jnp.einsum('bhnd,bhmd->bhnm', Q, K) * scale
        causal = jnp.tril(jnp.ones((N, N), dtype=bool))
        scores = jnp.where(causal, scores, -jnp.inf)
        attn = jax.nn.softmax(scores, axis=-1)
        out = jnp.einsum('bhnm,bhmd->bhnd', attn, V)
        out = out.transpose(0, 2, 1, 3).reshape(B, N, D)
        return out @ Wout + bout

    def _L3_xattn_ref(xh1, xh2, x2, x2_mask, W, b, D):
        import jax, jax.numpy as jnp
        import numpy as np
        B, L1, L2, FULL, H = (8, 512, 512, 256, 256)
        NEG_INF = -1e+30
        x1_key = jax.nn.relu(jnp.einsum('bsf,fg->bsg', xh1, W.T) + b)
        x2_key = jax.nn.relu(jnp.einsum('btf,fg->btg', xh2, W.T) + b)
        x2_key = x2_key * D[None, :, :]
        scores = jnp.einsum('bsf,btf->bst', x1_key, x2_key)
        scores = jnp.where(x2_mask[:, None, :], NEG_INF, scores)
        alpha = jax.nn.softmax(scores, axis=-1)
        seq_ave = jnp.einsum('bst,bth->bsh', alpha, x2)
        return seq_ave

    def _L3_ffn_ref(x, hasher_w, keys, values_down, values_up, scale):
        import jax, jax.numpy as jnp
        import numpy as np
        TOP_K = 4
        h = jnp.einsum('btd,pd->btp', x, hasher_w)
        sim = jnp.einsum('btp,np->btn', h, keys)
        vals, idx = jax.lax.top_k(sim, TOP_K)
        w = jax.nn.softmax(vals, axis=-1)
        out = jnp.zeros_like(x)
        for k in range(TOP_K):
            ik = idx[..., k]
            vd = values_down[ik]
            vu = values_up[ik]
            proj = jax.nn.silu(jnp.einsum('btd,btdp->btp', x, vd))
            o = jnp.einsum('btp,btpd->btd', proj, vu)
            out = out + o * w[..., k:k + 1]
        return x + out * scale
    x = x + _L0_attn_ref(_layernorm(x, axis=-1), L0_attn_w_q, L0_attn_w_k, L0_attn_w_v)
    x = x + _L0_xattn_ref(ctx_1024, ctx_1024, _layernorm(x, axis=-1), L0_xattn_Wv, L0_xattn_Wk, L0_xattn_Wq, L0_xattn_Wo, L0_xattn_bo)
    x = x + _L0_ffn_ref(_layernorm(x, axis=-1), L0_ffn_sim_matrix, L0_ffn_gates, L0_ffn_q_proj, L0_ffn_k_proj, L0_ffn_v_proj, L0_ffn_o_proj)
    x = x + _L1_attn_ref(_layernorm(x, axis=-1), L1_attn_Wq, L1_attn_Wkv, L1_attn_Wo)
    x = x + _L1_xattn_ref(_layernorm(x, axis=-1), ctx_1024, ctx_1024, mask_1x1xSxS2_bf1, L1_xattn_Wq, L1_xattn_bq, L1_xattn_Wk, L1_xattn_bk, L1_xattn_Wv, L1_xattn_bv, L1_xattn_Wo, L1_xattn_bo)
    x = x + _L1_ffn_ref(_layernorm(x, axis=-1), L1_ffn_W_fc, L1_ffn_ln_w, L1_ffn_ln_b, L1_ffn_W_proj)
    x = x + _L2_attn_ref(_layernorm(x, axis=-1), L2_attn_Wqkv, L2_attn_bqkv, L2_attn_gamma_q, L2_attn_beta_q, L2_attn_gamma_k, L2_attn_beta_k, L2_attn_Wo, L2_attn_bo)
    x = x + _L2_xattn_ref(_layernorm(x, axis=-1), ctx_1024, ctx_1024, mask_BxSxS2_ik1, L2_xattn_Wq, L2_xattn_bq, L2_xattn_Wk, L2_xattn_bk, L2_xattn_Wv, L2_xattn_bv, L2_xattn_Wo, L2_xattn_bo)
    x = x + _L2_ffn_ref(_layernorm(x, axis=-1), L2_ffn_rms_w, L2_ffn_gate_w, L2_ffn_W1, L2_ffn_b1, L2_ffn_W2, L2_ffn_b2)
    x = x + _L3_attn_ref(_layernorm(x, axis=-1), L3_attn_Wqkv, L3_attn_Wout, L3_attn_bout)
    x = x + _L3_xattn_ref(_layernorm(x, axis=-1), ctx_1024, ctx_1024, mask_BxS2_bf0, L3_xattn_W, L3_xattn_b, L3_xattn_D)
    x = x + _L3_ffn_ref(_layernorm(x, axis=-1), L3_ffn_hasher_w, L3_ffn_keys, L3_ffn_values_down, L3_ffn_values_up, L3_ffn_scale)
    return x

_drawn_inputs = setup_inputs


def setup_inputs(seed=0):
    import zlib

    import numpy as np

    out = dict(_drawn_inputs(seed))
    spreads = {'L0_xattn_bo': (0.0, 0.1),
     'L0_ffn_gates': (0.0, 0.1),
     'L1_xattn_bq': (0.0, 0.516),
     'L1_xattn_bk': (0.0, 2.0),
     'L1_xattn_bv': (0.0, 0.1),
     'L1_xattn_bo': (0.0, 0.1),
     'L1_ffn_ln_w': (1.0, 0.2),
     'L1_ffn_ln_b': (0.0, 0.1),
     'L2_attn_bqkv': (0.0, 0.8),
     'L2_attn_bo': (0.0, 0.8),
     'L2_xattn_bq': (0.0, 0.8),
     'L2_xattn_bk': (0.0, 2.0),
     'L2_xattn_bv': (0.0, 0.8),
     'L2_xattn_bo': (0.0, 0.8),
     'L2_ffn_rms_w': (1.0, 0.6),
     'L2_ffn_b1': (0.0, 0.8),
     'L2_ffn_b2': (0.0, 0.8),
     'L3_attn_bout': (0.0, 2.0),
     'L3_xattn_b': (0.0, 0.697),
     'L3_xattn_D': (1.0, 0.6)}
    factors = {'L0_attn_w_q': 5.205,
     'L0_attn_w_k': 4.429,
     'L1_attn_Wq': 8.0,
     'L2_attn_Wqkv': 8.0,
     'L2_attn_gamma_q': 8.0,
     'L2_attn_beta_q': 8.0,
     'L2_attn_gamma_k': 8.0,
     'L2_attn_beta_k': 8.0,
     'L2_attn_Wo': 8.0,
     'L2_xattn_Wq': 8.0,
     'L2_xattn_Wk': 8.0,
     'L2_xattn_Wv': 8.0,
     'L2_xattn_Wo': 8.0,
     'L2_ffn_gate_w': 8.0,
     'L2_ffn_W1': 8.0,
     'L2_ffn_W2': 8.0,
     'L3_attn_Wqkv': 4.174,
     'L3_attn_Wout': 4.368,
     'L3_ffn_hasher_w': 64.0,
     'L3_ffn_keys': 64.0,
     'L3_ffn_values_down': 64.0,
     'L3_ffn_values_up': 64.0}
    for name, (base, spread) in spreads.items():
        noise = np.random.default_rng([zlib.crc32(name.encode()), seed]).standard_normal(out[name].shape)
        drawn = base * np.exp(spread * noise) if base else spread * noise
        out[name] = jnp.asarray(drawn.astype(out[name].dtype))
    for name, factor in factors.items():
        out[name] = (out[name] * factor).astype(out[name].dtype)
    return out
```

```python
from contextlib import ExitStack, contextmanager

import concourse.bass as bass
import numpy as np
from concourse import mybir

F32 = mybir.dt.float32
BF16 = mybir.dt.bfloat16
I32 = mybir.dt.int32
U32 = mybir.dt.uint32
U8 = mybir.dt.uint8
ALU = mybir.AluOpType
ACT = mybir.ActivationFunctionType
AX = mybir.AxisListType

B, T, D, P = 4, 512, 256, 128
NT, NC = T // P, D // P
H, HD, PITCH = 16, D // 16, 32
GROUPS = H * PITCH // P
DK = 64
F = 1024
EXPERTS, HIDDEN_CHUNKS = 8, F // P
MIX, MIXD = 16, 64
SLOTS, SLOTD = 64, 32
BANK = 512
BANKS = 8
LN_EPS = 1e-5
MASKED = -1e30
ARENA = 12288
SEMS = 16

WIDTHS = {
    "L0_attn": [("wq", 512), ("wk", 512), ("wv", 512), ("cos", 512), ("sin", 512)],
    "L0_xattn": [("wq", 1024), ("wk", 1024), ("wv", 512), ("wo", 1024), ("bo", 256)],
    "L0_ffn": [("sim", 32), ("gates", 16), ("q", 2048), ("k", 2048), ("v", 2048), ("o", 2048)],
    "L1_attn": [("wq", 1024), ("wk", 1024), ("wv", 512), ("wo", 1024)],
    "L1_xattn": [("wq", 512), ("wk", 512), ("wv", 512), ("wo", 512), ("bq", 2), ("bk", 2),
                 ("bv", 256), ("bo", 256)],
    "L1_ffn": [("fc", 2048), ("proj", 2048), ("ln_w", 8), ("ln_b", 8)],
    "L2_attn": [("wqkv", 1536), ("bqkv", 768), ("gq", 4), ("hq", 4), ("gk", 4), ("hk", 4),
                ("wo", 1024), ("bo", 256)],
    "L2_xattn": [("wq", 2048), ("wk", 2048), ("wv", 2048), ("wo", 4096), ("bq", 16), ("bk", 16),
                 ("bv", 1024), ("bo", 256)],
    "L2_ffn": [("rms", 2), ("gate", 16), ("b1", 64), ("b2", 256)],
    "L3_attn": [("wq", 1024), ("wqr", 1024), ("wk", 1024), ("wkr", 1024), ("wv", 512), ("wo", 1024),
                ("cos", 512), ("sin", 512), ("bo", 256)],
    "L3_xattn": [("w", 512), ("b", 2), ("d", 2)],
    "L3_ffn": [("hash", 64), ("keys", 64), ("down", 4096), ("up", 4096), ("spread", 2048), ("scale", 1)],
}
CONSTS = [("ident", P), ("causal", BANK), ("den16", P), ("den64", P), ("aug", 1), ("iota", 64), ("ones", P),
          ("half", 16), ("minus_half", 16), ("causal_cols", P)]
SUBLAYERS = list(WIDTHS)


def offsets(fields):
    at, out = 0, {}
    for name, width in fields:
        out[name] = (at, width)
        at += width
    return out, at


class Net:

    def __init__(self, nc, ctx):
        self.nc, self.ctx = nc, ctx
        self.banks = [[ctx.enter_context(nc.semaphore(f"sem_{half}_{i}")) for i in range(SEMS)] for half in range(2)]
        self.turn = 0
        self.tensors = 0
        self.psum = ctx.enter_context(nc.psum_tensor("psum", [P, BANKS, BANK], F32))

    def sbuf(self, name, shape, dt=F32, ctx=None):
        self.tensors += 1
        return (ctx or self.ctx).enter_context(self.nc.sbuf_tensor(f"{name}_{self.tensors}", shape, dt))

    @contextmanager
    def block(self):
        mine, other = self.banks[self.turn], self.banks[1 - self.turn]
        self.turn = 1 - self.turn
        free = iter(mine)
        with self.nc.Block() as block:
            @block.gpsimd
            def _(pool):
                pool.sem_clear(range(other[0].num, other[-1].num + 1))
            yield block, lambda signals: next(free)



class Product:

    def __init__(self, engine, rows, cols, mms, out, finish, split=None):
        self.engine, self.rows, self.cols, self.mms = engine, rows, cols, mms
        self.out, self.finish, self.split = out, finish, split


def summed(terms):
    n = len(terms)
    return [(None, a, b, i == 0, i == n - 1, False) for i, (a, b) in enumerate(terms)]


def turned(tiles, ident):
    return [(slice(i * P, i * P + t.shape[0]), t, ident[0:t.shape[0], 0:t.shape[0]], True, True, True)
            for i, t in enumerate(tiles)]


def finished(eng, p, ps):
    src = ps[0:p.rows, 0:p.cols]
    if p.split:
        src = src.rearrange("p (a b) -> p a b", a=p.split)
    kind, *args = p.finish
    if kind == "act":
        func, bias, scale = args
        kw = {} if bias is None else {"bias": bias}
        return eng.activation(p.out, src, func, scale=scale, **kw)
    if kind == "copy":
        return eng.tensor_copy(p.out, src)
    if kind == "scalar":
        s1, s2, op0, op1 = args
        return eng.tensor_scalar(p.out, src, s1, s2, op0, op1)
    if kind == "tensor":
        other, op = args
        return eng.tensor_tensor(p.out, src, other, op)
    scalar, other, op0, op1 = args
    return eng.scalar_tensor_tensor(out=p.out, in0=src, scalar=scalar, in1=other, op0=op0, op1=op1)


COPY = ("act", ACT.Copy, None, 1.0)
VCOPY = ("copy",)


def products(net, table, name="products"):
    owner = [p.engine for p in table]
    with net.block() as (block, sem):
        product_done, act_done, dve_done = sem("product"), sem("finished"), sem("finished")

        @block.tensor
        def _(pe):
            for n, p in enumerate(table):
                if n >= BANKS:
                    last = n - BANKS
                    pe.wait_ge(act_done if owner[last] == "act" else dve_done, owner[:last + 1].count(owner[last]))
                bank = net.psum[:, n % BANKS, :]
                for where, lhsT, rhs, start, stop, turn in p.mms:
                    dst = bank[0:p.rows, where] if where is not None else bank[0:p.rows, 0:p.cols]
                    if turn:
                        mm = pe.transpose(dst, lhsT, rhs)
                    else:
                        mm = pe.matmul(dst, lhsT, rhs, start=start, stop=stop)
                mm.then_inc(product_done, 1)

        @block.scalar
        def _(act):
            for n, p in enumerate(table):
                if p.engine == "act":
                    act.wait_ge(product_done, n + 1)
                    finished(act, p, net.psum[:, n % BANKS, :]).then_inc(act_done, 1)

        @block.vector
        def _(dve):
            done = 0
            for n, p in enumerate(table):
                if p.engine == "dve":
                    dve.wait_ge(product_done, n + 1)
                    if p.finish[0] == "stt" and done:
                        dve.wait_ge(dve_done, done)
                    finished(dve, p, net.psum[:, n % BANKS, :]).then_inc(dve_done, 1)
                    done += 1


def cols_out(engine, w, width, src, m, out, finish=COPY, rows=P, n=T, bias=None):
    chunks = src.shape[1]
    terms = [(w[:, k * width + m:k * width + m + rows], src[:, k, :]) for k in range(chunks)]
    return Product(engine, rows, n, summed(terms), out, finish)


def rows_out(engine, src, t, w, width, at, n, out, finish=COPY, bias=None, ones=None, split=None):
    terms = [(src[:, k, t * P:(t + 1) * P], w[:, k * width + at:k * width + at + n]) for k in range(src.shape[1])]
    if bias is not None:
        terms.append((ones[0:1, :], bias[0:1, at:at + n]))
    return Product(engine, P, n, summed(terms), out, finish, split)



def layernorm(net, x, xn, xc):
    with ExitStack() as ctx:
        stats = net.sbuf("stats", [P, NT, 6], ctx=ctx)
        mv = net.sbuf("mean_var", [P, NT, 2], ctx=ctx)
        rstd = net.sbuf("rstd", [P, NT], ctx=ctx)
        with net.block() as (block, sem):
            stats_done, mv_done, rstd_done = sem("stats"), sem("mean and variance"), sem("1/std")
            xn_done, turned_done, guarded = sem("normalised tile"), sem("transposed chunk"), sem("variance + eps")

            @block.gpsimd
            def _(pool):
                pool.wait_ge(mv_done, NT)
                pool.tensor_scalar(rstd[:, :], mv[:, :, 1], LN_EPS, None, ALU.add, ALU.bypass).then_inc(guarded, 1)
                pool.wait_ge(guarded, 1)
                pool.tensor_tensor(rstd[:, :], rstd[:, :], net.minus_half[:, 0:NT], ALU.pow).then_inc(rstd_done, 1)

            @block.vector
            def _(dve):
                for t in range(NT):
                    dve.bn_stats(stats[:, t, :], x[:, t, :]).then_inc(stats_done, 1)
                for t in range(NT):
                    dve.wait_ge(stats_done, t + 1)
                    dve.bn_aggr(mv[:, t, :], stats[:, t, :]).then_inc(mv_done, 1)
                dve.wait_ge(rstd_done, 1)
                for t in range(NT):
                    dve.tensor_scalar(xn[:, t, :], x[:, t, :], mv[:, t, 0:1], rstd[:, t:t + 1],
                                      ALU.subtract, ALU.mult).then_inc(xn_done, 1)
                dve.wait_ge(turned_done, 2)
                dve.tensor_copy(xc[:, 1, :], net.psum[:, 1, :])

            @block.tensor
            def _(pe):
                for c in range(NC):
                    for t in range(NT):
                        pe.wait_ge(xn_done, t + 1)
                        mm = pe.transpose(net.psum[:, c, t * P:(t + 1) * P], xn[:, t, c * P:(c + 1) * P], net.ident)
                    mm.then_inc(turned_done, 1)

            @block.scalar
            def _(act):
                act.wait_ge(turned_done, 1)
                act.activation(xc[:, 0, :], net.psum[:, 0, :], ACT.Copy)



def wide_attention(net, q, k, values, width, causal, finish, keep=None, gone=None):
    masked = causal or keep is not None
    with ExitStack() as ctx:
        probs = net.sbuf("probs", [P, 2, T], ctx=ctx)
        scores = net.sbuf("scores", [P, 2, T], ctx=ctx) if masked else None
        kept = net.sbuf("kept", [P, 2, T], ctx=ctx) if keep is not None else None
        probs_t = net.sbuf("probs_t", [P, 2, T], ctx=ctx)
        nmax = net.sbuf("nmax", [P, NT], ctx=ctx)
        total = net.sbuf("total", [P, NT], ctx=ctx)
        inverse = net.sbuf("inverse", [P, NT], ctx=ctx)
        span = [(t + 1) * P if causal else T for t in range(NT)]
        with net.block() as (block, sem):
            scores_done, kept_done, max_done, probs_done = sem("scores"), sem("kept"), sem("maximum"), sem("exp")
            turned_done, copied_done, out_done = sem("transposed"), sem("transpose copied"), sem("p @ v")
            inverse_done, tile_done = sem("1/sum"), sem("tile written")

            @block.tensor
            def _(pe):
                def score(t):
                    if t >= 2:
                        if masked:
                            pe.wait_ge(max_done, t - 1)
                        else:
                            pe.wait_ge(probs_done, t - 1)
                    for i, (a, b) in enumerate(zip(q, k)):
                        mm = pe.matmul(net.psum[:, t % 2, 0:span[t]], a[:, t * P:(t + 1) * P], b[:, 0:span[t]],
                                       start=i == 0, stop=i == len(q) - 1)
                    mm.then_inc(scores_done, 1)

                score(0)
                for t in range(NT):
                    if t + 1 < NT:
                        score(t + 1)
                    pe.wait_ge(probs_done, t + 1)
                    if t >= 2:
                        pe.wait_ge(copied_done, t - 1)
                    for c in range(span[t] // P):
                        mm = pe.transpose(net.psum[:, 2 + t % 2, c * P:(c + 1) * P],
                                          probs[:, t % 2, c * P:(c + 1) * P], net.ident)
                    mm.then_inc(turned_done, 1)
                    pe.wait_ge(copied_done, t + 1)
                    if t >= 2:
                        pe.wait_ge(tile_done, t - 1)
                    n = span[t] // P
                    for c in range(n):
                        mm = pe.matmul(net.psum[:, 4 + t % 2, 0:width], probs_t[:, t % 2, c * P:(c + 1) * P],
                                       values(c), start=c == 0, stop=c == n - 1)
                    mm.then_inc(out_done, 1)

            @block.vector
            def _(dve):
                def maximum(t):
                    dve.wait_ge(scores_done, t + 1)
                    src = net.psum[:, t % 2, 0:span[t]]
                    if not masked:
                        dve.tensor_reduce(nmax[:, t:t + 1], src, AX.X, ALU.max, negate=True).then_inc(max_done, 1)
                        return
                    if t >= 2:
                        dve.wait_ge(probs_done, t - 1)
                    if keep is not None:
                        dve.tensor_tensor(kept[:, t % 2, :], src, keep, ALU.mult).then_inc(kept_done, 1)
                        dve.wait_ge(kept_done, t + 1)
                        src, mask = kept[:, t % 2, :], gone
                    else:
                        mask = net.causal[:, BANK - span[t]:BANK]
                    dve.tensor_tensor_reduce(scores[:, t % 2, 0:span[t]], src, mask, -1.0, 3e38, ALU.add, ALU.min,
                                             nmax[:, t:t + 1]).then_inc(max_done, 1)

                maximum(0)
                for t in range(NT):
                    if t + 1 < NT:
                        maximum(t + 1)
                    dve.wait_ge(turned_done, t + 1)
                    if t >= 2:
                        dve.wait_ge(out_done, t - 1)
                    dve.tensor_copy(probs_t[:, t % 2, 0:span[t]], net.psum[:, 2 + t % 2, 0:span[t]])\
                       .then_inc(copied_done, 1)
                    dve.wait_ge(probs_done, t + 1)
                    dve.reciprocal(inverse[:, t:t + 1], total[:, t:t + 1]).then_inc(inverse_done, 1)
                    dve.wait_ge(inverse_done, t + 1)
                    dve.wait_ge(out_done, t + 1)
                    finish(dve, t, net.psum[:, 4 + t % 2, 0:width], inverse[:, t:t + 1]).then_inc(tile_done, 1)

            @block.scalar
            def _(act):
                for t in range(NT):
                    act.wait_ge(max_done, t + 1)
                    if t >= 2:
                        act.wait_ge(turned_done, t - 1)
                    src = scores[:, t % 2, 0:span[t]] if masked else net.psum[:, t % 2, 0:span[t]]
                    act.activation(probs[:, t % 2, 0:span[t]], src, ACT.Exp, bias=nmax[:, t:t + 1],
                                   scale=-1.0 if masked else 1.0, accum_out=total[:, t:t + 1]).then_inc(probs_done, 1)



def many_heads(net, qc, kc, v, hd, o, causal=False, linear=False, mask_rows=None, mask_cols=None):
    packed = hd == HD
    future = causal and not linear
    cut = causal and linear
    groups = GROUPS if packed else 1
    rows = P if packed else hd + 1
    kt_n, steps = NT, 2 * NT

    def head(g, u):
        return (g, slice(u * PITCH, (u + 1) * PITCH)) if packed else (u, slice(0, rows))

    with ExitStack() as ctx:
        chunks = qc.shape[1]
        nmax = net.sbuf("nmax", [P, NT, 4, P], ctx=ctx)
        probs = net.sbuf("probs", [P, 2, 2, T], ctx=ctx)
        with net.block() as (block, sem):
            cleared, scores_done = sem("nmax zeroed"), sem("scores")
            max_done, turned_done, put_done = sem("maximum"), sem("-max transposed"), sem("-max in q")
            colscores_done, probs_done, cut_done = sem("transposed scores"), sem("exp"), sem("future cut off")
            pv_done, o_done, clamp_done = sem("p @ v of a step"), sem("output copied"), sem("-max clamped")
            units = 4 * NT
            turns = 1 if packed else 4

            @block.gpsimd
            def _(pool):
                if not linear:
                    pool.memset(nmax[:, :, :, :], 0.0).then_inc(cleared, 1)
                if cut:
                    for n in range(groups * steps):
                        pool.wait_ge(probs_done, n + 1)
                        kt = n % kt_n
                        d = probs[:, n % 2, :, kt * P:(kt + 1) * P]
                        pool.affine_select(out=d, in_=d, compare_op=ALU.is_ge, fill=0.0, base=0,
                                           pattern=[[0, 2], [1, P]], channel_multiplier=-1).then_inc(cut_done, 1)

            @block.tensor
            def _(pe):
                def score(g, n):
                    qt, u = n // 4, n % 4
                    s = g * units + n
                    if s >= 2:
                        pe.wait_ge(max_done, s - 1)
                    if g and n < 2:
                        pe.wait_ge(put_done, turns * g)
                    c, r = head(g, u)
                    w = (qt + 1) * P if causal else T
                    bank = net.psum[:, n % 2, 0:w]
                    mm = pe.matmul(bank, qc[r, c, qt * P:(qt + 1) * P], kc[r, c, 0:w], start=True,
                                   stop=mask_rows is None and not causal)
                    if mask_rows is not None:
                        mm = pe.matmul(bank, net.ident16, mask_rows[:, qt, :], start=False, stop=True)
                    if causal:
                        mm = pe.matmul(bank[:, qt * P:w], net.ident16, net.causal16, start=False, stop=True)
                    mm.then_inc(scores_done, 1)

                def put(g):
                    if packed:
                        pe.wait_ge(max_done, units * (g + 1))
                    else:
                        pe.wait_ge(clamp_done, 1)
                    for i in range(turns):
                        if i >= 2:
                            pe.wait_ge(put_done, turns * g + i - 1)
                        for t in range(NT):
                            mm = pe.transpose(net.psum[:, i % 2, t * P:(t + 1) * P], nmax[:, t, g if packed else i, :],
                                              net.ident)
                        mm.then_inc(turned_done, 1)

                def col_scores(n):
                    g, pair, kt = n // steps, n % steps // kt_n, n % kt_n
                    if not linear and n % steps == 0:
                        pe.wait_ge(put_done, turns * (g + 1))
                    if n >= 2:
                        pe.wait_ge(probs_done, n - 1)
                    lo = kt * P if causal else 0
                    for i in range(2):
                        c, r = head(g, 2 * pair + i)
                        bank = net.psum[:, 2 + 2 * (n % 2) + i, lo:T]
                        mm = pe.matmul(bank, kc[r, c, kt * P:(kt + 1) * P], qc[r, c, lo:T],
                                       start=True, stop=mask_cols is None and not future)
                        if future:
                            mm = pe.matmul(bank[:, 0:P], net.ident16, net.causal_cols16, start=False, stop=True)
                        if mask_cols is not None:
                            mm = pe.matmul(bank, net.ident16, mask_cols[:, kt, :], start=False, stop=True)
                    mm.then_inc(colscores_done, 1)

                def weigh(n):
                    g, pair, kt = n // steps, n % steps // kt_n, n % kt_n
                    pe.wait_ge(cut_done if cut else probs_done, n + 1)
                    if packed and n % steps == 0 and g >= 2:
                        pe.wait_ge(o_done, g - 1)
                    if not packed and n % kt_n == 0 and pair:
                        pe.wait_ge(o_done, 2 * pair)
                    lo = kt * P if causal else 0
                    for i in range(2):
                        u = 2 * pair + i
                        if packed:
                            dst = net.psum[u * PITCH:(u + 1) * PITCH, 6 + g % 2, lo:T]
                        else:
                            dst = net.psum[0:rows, 6 + i, lo:T]
                        mm = pe.matmul(dst, v(kt, 4 * g + u), probs[:, n % 2, i, lo:T], start=kt == 0,
                                       stop=kt == kt_n - 1, **({"tile_position": (0, u * PITCH)} if packed else {}))
                    mm.then_inc(pv_done, 1)

                if linear:
                    for n in range(groups * steps + 1):
                        if n < groups * steps:
                            col_scores(n)
                        if n:
                            weigh(n - 1)
                else:
                    for g in range(groups + 1):
                        for i in range(steps):
                            if g:
                                col_scores((g - 1) * steps + i)
                                if (g - 1) * steps + i:
                                    weigh((g - 1) * steps + i - 1)
                            if g < groups:
                                score(g, 2 * i)
                                score(g, 2 * i + 1)
                        if g < groups:
                            put(g)
                    weigh(groups * steps - 1)

            @block.vector
            def _(dve):
                def copy_out(g, i):
                    if packed:
                        dve.wait_ge(pv_done, steps * (g + 1))
                        dve.tensor_copy(o[:, g, :], net.psum[:, 6 + g % 2, :]).then_inc(o_done, 1)
                    else:
                        dve.wait_ge(pv_done, kt_n * (i // 2 + 1))
                        dve.tensor_copy(o[0:rows, i, :], net.psum[0:rows, 6 + i % 2, :]).then_inc(o_done, 1)

                if not linear:
                    dve.wait_ge(cleared, 1)
                    for g in range(groups):
                        for n in range(units):
                            s = g * units + n
                            dve.wait_ge(scores_done, s + 1)
                            qt, u = n // 4, n % 4
                            w = (qt + 1) * P if causal else T
                            at = nmax[:, qt, g, u * PITCH + hd:u * PITCH + hd + 1] if packed else \
                                nmax[:, qt, u, hd:hd + 1]
                            dve.tensor_reduce(at, net.psum[:, n % 2, 0:w], AX.X, ALU.max, negate=True)\
                               .then_inc(max_done, 1)
                        if not packed:
                            dve.wait_ge(max_done, units)
                            m = nmax[:, :, :, hd]
                            dve.tensor_scalar(m, m, 1e20, None, ALU.min).then_inc(clamp_done, 1)
                        for i in range(turns):
                            dve.wait_ge(turned_done, turns * g + i + 1)
                            dst = qc[0:rows, g if packed else i, :]
                            dve.tensor_tensor(dst, dst, net.psum[0:rows, i % 2, :], ALU.add).then_inc(put_done, 1)
                        if packed and g:
                            copy_out(g - 1, 0)
                if linear:
                    for g in range(groups - 1):
                        copy_out(g, 0)
                if packed:
                    copy_out(groups - 1, 0)
                else:
                    for i in range(4):
                        copy_out(0, i)

            @block.scalar
            def _(act):
                for n in range(groups * steps):
                    kt = n % kt_n
                    lo = kt * P if causal else 0
                    act.wait_ge(colscores_done, n + 1)
                    if n >= 2:
                        act.wait_ge(pv_done, n - 1)
                    act.activation(probs[:, n % 2, :, lo:T], net.psum[:, 2 + 2 * (n % 2):4 + 2 * (n % 2), lo:T],
                                   ACT.Copy if linear else ACT.Exp).then_inc(probs_done, 1)


def normalise(net, o, hd, guard, op):
    packed = hd == HD
    rows = P if packed else hd + 1
    with ExitStack() as ctx:
        inv = net.sbuf("inv", [P, 4, T], ctx=ctx)
        pick = net.den16 if packed else net.den64[0:rows, 0:hd]
        m = P if packed else hd
        products(net, [Product("dve", m, T, summed([(pick, o[0:rows, c, :])]), inv[0:m, c, :],
                               ("scalar", guard, None, op, ALU.bypass)) for c in range(4)])
        with net.block() as (block, sem):
            inverse_done = sem("1/sum")

            @block.vector
            def _(dve):
                for c in range(4):
                    dve.reciprocal(inv[0:m, c, :], inv[0:m, c, :]).then_inc(inverse_done, 1)
                for c in range(4):
                    dve.wait_ge(inverse_done, c + 1)
                    dve.tensor_tensor(o[0:m, c, :], o[0:m, c, :], inv[0:m, c, :], ALU.mult)


def add_output(net, x, src, chunks, rows, w, bias):
    table = []
    for t in range(NT):
        terms = [(src[0:rows, c, t * P:(t + 1) * P], w[0:rows, c * D:(c + 1) * D]) for c in range(chunks)]
        if bias is not None:
            terms.append((net.ones[0:1, :], bias[0:1, :]))
        table.append(Product("dve", P, D, summed(terms), x[:, t, :], ("tensor", x[:, t, :], ALU.add)))
    products(net, table)


def alternate(n):
    return "dve" if n % 2 else "act"


def copied(engine):
    return COPY if engine == "act" else VCOPY



def values_with_ones(net, v):
    with net.block() as (block, sem):
        zeroed = sem("zeroed")

        @block.gpsimd
        def _(pool):
            pool.memset(v[:, :, :, :], 0.0).then_inc(zeroed, 1)
            pool.wait_ge(zeroed, 1)
            pool.memset(v[:, :, :, HD:HD + 1], 1.0)


def fill_values(net, v, src, w, bias=None):
    return [rows_out(alternate(t), src, t, w, D, 0, D, v[:, t, :, 0:HD], copied(alternate(t)), bias, net.ones, split=H)
            for t in range(NT)]


def narrow_attention(net, W, x, qsrc, ksrc, scale, causal, bias, guard, qk=None, linear=False, fill=None):
    with ExitStack() as ctx:
        qc = net.sbuf("qc", [P, GROUPS, T], ctx=ctx)
        kc = net.sbuf("kc", [P, GROUPS, T], ctx=ctx)
        v = net.sbuf("v", [P, NT, H, PITCH], ctx=ctx)
        o = net.sbuf("o", [P, GROUPS, T], ctx=ctx)
        values_with_ones(net, v)
        if fill is None:
            table = fill_values(net, v, ksrc, W["wv"])
        else:
            table = []
        if qk is None:
            for g in range(GROUPS):
                table.append(cols_out("act", W["wq"], GROUPS * P, qsrc, g * P, qc[:, g, :], ("act", ACT.Copy, None, scale)))
                table.append(cols_out("dve", W["wk"], GROUPS * P, ksrc, g * P, kc[:, g, :],
                                      ("scalar", net.aug, None, ALU.add, ALU.bypass)))
        else:
            table += qk(qc, kc, v)
        products(net, table)
        if fill is not None:
            fill(qc, kc, v)
        many_heads(net, qc, kc, lambda kt, h: v[:, kt, h, :], HD, o, causal=causal, linear=linear)
        normalise(net, o, HD, guard, ALU.add)
        add_output(net, x, o, GROUPS, P, W["wo"], bias)


def L0_attn(net, W, x, xn, xc, **_):
    with ExitStack() as ctx:
        q = net.sbuf("q", [P, NC, T], ctx=ctx)
        k = net.sbuf("k", [P, NC, T], ctx=ctx)
        v = net.sbuf("v", [P, NT, D], ctx=ctx)
        tmp = net.sbuf("tmp", [P, 8, T], ctx=ctx)
        table = []
        for i, (dst, w) in enumerate(((q, W["wq"]), (k, W["wk"]))):
            for c in range(NC):
                for j, tab in enumerate((W["cos"], W["sin"])):
                    table.append(cols_out("dve", w, D, xc, c * P, tmp[:, 4 * i + 2 * c + j, :], ("tensor", tab, ALU.mult)))
        table += [rows_out("act", xc, t, W["wv"], D, 0, D, v[:, t, :]) for t in range(NT)]
        products(net, table)
        with net.block() as (block, sem):
            rotated = sem("rotated")

            @block.vector
            def _(dve):
                for i, dst in enumerate((q, k)):
                    a = tmp[:, 4 * i:4 * i + 4, :]
                    dve.tensor_tensor(dst[:, 0, :], a[:, 0, :], a[:, 3, :], ALU.subtract).then_inc(rotated, 1)
                    dve.tensor_tensor(dst[:, 1, :], a[:, 1, :], a[:, 2, :], ALU.add).then_inc(rotated, 1)

            @block.scalar
            def _(act):
                act.wait_ge(rotated, 2)
                act.activation(q[:, :, :], q[:, :, :], ACT.Copy, scale=D ** -0.5)

        def finish(dve, t, ps, inverse):
            return dve.scalar_tensor_tensor(out=x[:, t, :], in0=ps, scalar=inverse, in1=x[:, t, :],
                                            op0=ALU.mult, op1=ALU.add)
        wide_attention(net, [q[:, c, :] for c in range(NC)], [k[:, c, :] for c in range(NC)],
                       lambda c: v[:, c, :], D, True, finish)


def L0_xattn(net, W, x, xn, xc, cc, **_):
    narrow_attention(net, W, x, xc, cc, D ** -0.5, False, W["bo"], 0.0)


def L0_ffn(net, W, x, xn, xc, **_):
    with ExitStack() as ctx:
        sb = lambda name, shape, dt=F32: net.sbuf(name, shape, dt, ctx=ctx)
        gate = sb("gate", [P, NT, MIX])
        xsq, ssum = sb("xsq", [P, D]), sb("ssum", [P, NT])
        simsq, simn, siminv = sb("simsq", [P, 2 * MIX]), sb("simn", [P, 2 * MIX]), sb("siminv", [P, MIX])
        sig, raw, logit = sb("sig", [P, MIX]), sb("raw", [P, NT, MIX]), sb("logit", [P, NT, MIX])
        g, a, e = sb("g", [P, NT, MIX]), sb("a", [P, NT, MIX]), sb("e", [P, NT, MIX])
        top, index, indexf = sb("top", [P, NT, 8]), sb("index", [P, NT, 8], U32), sb("indexf", [P, NT, 8])
        anyon, mx, tot = sb("anyon", [P, NT]), sb("mx", [P, NT]), sb("tot", [P, NT])
        fb, fb2 = sb("fb", [P, NT, MIX]), sb("fb2", [P, NT, MIX])
        with net.block() as (block, sem):
            step, colsum_done, sim_done, raw_done, exped, sig_done = (sem("step"), sem("column sums"), sem("similarity"),
                                                                      sem("products"), sem("exp"), sem("sigmoid"))

            floor_done, root_done = sem("sums of squares kept above zero"), sem("1/norms")

            @block.gpsimd
            def _(pool):
                pool.wait_ge(floor_done, 1)
                pool.tensor_tensor(siminv[:, :], siminv[:, :], net.minus_half, ALU.pow).then_inc(root_done, 1)
                pool.tensor_tensor(ssum[:, :], ssum[:, :], net.minus_half[:, 0:NT], ALU.pow).then_inc(root_done, 1)

            @block.scalar
            def _(act):
                act.activation(sig[:, :], W["gates"], ACT.Sigmoid).then_inc(sig_done, 1)
                act.wait_ge(exped, 1)
                act.activation(e[:, :, :], e[:, :, :], ACT.Exp).then_inc(exped, 1)

            @block.tensor
            def _(pe):
                pe.wait_ge(step, 1)
                for c in range(NC):
                    mm = pe.matmul(net.psum[:, 0, 0:MIX], net.ones_pp, simsq[:, c * MIX:(c + 1) * MIX], start=c == 0, stop=c == 1)
                mm.then_inc(colsum_done, 1)
                pe.wait_ge(sim_done, 1)
                for t in range(NT):
                    for c in range(NC):
                        mm = pe.matmul(net.psum[:, 1, t * MIX:(t + 1) * MIX], xc[:, c, t * P:(t + 1) * P],
                                       simn[:, c * MIX:(c + 1) * MIX], start=c == 0, stop=c == 1)
                mm.then_inc(raw_done, 1)

            @block.vector
            def _(dve):
                n = 0

                def then(ins):
                    nonlocal n
                    n += 1
                    ins.then_inc(step, 1)
                    dve.wait_ge(step, n)

                then(dve.tensor_tensor(simsq[:, :], W["sim"], W["sim"], ALU.mult))
                for t in range(NT):
                    then(dve.tensor_tensor_reduce(xsq[:, :], xn[:, t, :], xn[:, t, :], 1.0, 0.0, ALU.mult, ALU.add,
                                                  ssum[:, t:t + 1]))
                then(dve.tensor_scalar(ssum[:, :], ssum[:, :], 1e-24, None, ALU.max))
                dve.wait_ge(colsum_done, 1)
                dve.tensor_scalar(siminv[:, :], net.psum[:, 0, 0:MIX], 1e-24, None, ALU.max).then_inc(floor_done, 1)
                dve.wait_ge(root_done, 2)
                for c in range(NC):
                    ins = dve.tensor_tensor(simn[:, c * MIX:(c + 1) * MIX], W["sim"][:, c * MIX:(c + 1) * MIX],
                                            siminv[:, :], ALU.mult)
                    if c == 0:
                        then(ins)
                ins.then_inc(sim_done, 1)
                dve.wait_ge(raw_done, 1)
                then(dve.tensor_tensor(raw[:, :, :], net.psum[:, 1, 0:NT * MIX].rearrange("p (t e) -> p t e", t=NT),
                                       ssum[:, :].unsqueeze(2).broadcast_to([P, NT, MIX]), ALU.mult))
                dve.wait_ge(sig_done, 1)
                then(dve.tensor_tensor(logit[:, :, :], raw[:, :, :],
                                       sig[:, :].unsqueeze(1).broadcast_to([P, NT, MIX]), ALU.subtract))
                then(dve.tensor_scalar(g[:, :, :], logit[:, :, :], 0.0, None, ALU.max))
                then(dve.tensor_scalar(a[:, :, :], logit[:, :, :], 0.0, None, ALU.is_gt))
                then(dve.tensor_reduce(anyon[:, :], a[:, :, :], AX.X, ALU.max))
                then(dve.tensor_reduce(mx[:, :], g[:, :, :], AX.X, ALU.max))
                for t in range(NT):
                    then(dve.max(top[:, t, :], logit[:, t, :]))
                    then(dve.max_index(index[:, t, :], top[:, t, :], logit[:, t, :]))
                then(dve.tensor_copy(indexf[:, :, :], index[:, :, :]))
                for dst, i in ((fb, 0), (fb2, 1)):
                    then(dve.tensor_tensor(dst[:, :, :], net.iota[:, 0:MIX].unsqueeze(1).broadcast_to([P, NT, MIX]),
                                           indexf[:, :, i:i + 1].broadcast_to([P, NT, MIX]), ALU.is_equal))
                then(dve.tensor_tensor(fb[:, :, :], fb[:, :, :], fb2[:, :, :], ALU.add))
                then(dve.tensor_scalar(anyon[:, :], anyon[:, :], -1.0, 1.0, ALU.mult, ALU.add))
                then(dve.tensor_tensor(fb[:, :, :], fb[:, :, :], anyon[:, :].unsqueeze(2).broadcast_to([P, NT, MIX]), ALU.mult))
                then(dve.tensor_tensor(a[:, :, :], a[:, :, :], fb[:, :, :], ALU.add))
                dve.tensor_tensor(e[:, :, :], g[:, :, :], mx[:, :].unsqueeze(2).broadcast_to([P, NT, MIX]),
                                  ALU.subtract).then_inc(exped, 1)
                dve.wait_ge(exped, 2)
                then(dve.tensor_tensor(e[:, :, :], e[:, :, :], a[:, :, :], ALU.mult))
                then(dve.tensor_reduce(tot[:, :], e[:, :, :], AX.X, ALU.add))
                then(dve.reciprocal(tot[:, :], tot[:, :]))
                then(dve.tensor_tensor(gate[:, :, :], e[:, :, :], tot[:, :].unsqueeze(2).broadcast_to([P, NT, MIX]), ALU.mult))

        qkv = sb("qkv", [P, NT, 3, MIXD])
        weighed = sb("weighed", [P, 2, MIX, MIXD])
        half = MIX // 2
        with net.block() as (block, sem):
            product_done, weighed_done, summed_done = sem("products"), sem("weighed"), sem("summed")
            jobs = [(t, j) for t in range(NT) for j in range(3)]

            @block.tensor
            def _(pe):
                for n, (t, j) in enumerate(jobs):
                    if n >= 4:
                        pe.wait_ge(weighed_done, 2 * (n - 3))
                    for h in range(2):
                        for c in range(NC):
                            at = c * MIX * MIXD + h * half * MIXD
                            mm = pe.matmul(net.psum[:, 2 * (n % 4) + h, :], xc[:, c, t * P:(t + 1) * P],
                                           W["qkv"[j]][:, at:at + half * MIXD], start=c == 0, stop=c == 1)
                        mm.then_inc(product_done, 1)

            @block.vector
            def _(dve):
                for n, (t, j) in enumerate(jobs):
                    for h in range(2):
                        dve.wait_ge(product_done, 2 * n + h + 1)
                        dve.tensor_tensor(weighed[:, n % 2, h * half:(h + 1) * half, :],
                                          net.psum[:, 2 * (n % 4) + h, :].rearrange("p (e d) -> p e d", d=MIXD),
                                          gate[:, t, h * half:(h + 1) * half].unsqueeze(2).broadcast_to([P, half, MIXD]),
                                          ALU.mult).then_inc(weighed_done, 1)
                    dve.wait_ge(weighed_done, 2 * n + 2)
                    dve.tensor_reduce(qkv[:, t, j, :], weighed[:, n % 2, :, :].rearrange("p e d -> p d e"), AX.X, ALU.add)\
                       .then_inc(summed_done, 1)
        qk = sb("qk", [MIXD, 2, T])
        products(net, [Product("act", MIXD, T, turned([qkv[:, t, j, :] for t in range(NT)], net.ident), qk[:, j, :],
                               ("act", ACT.Copy, None, MIXD ** -0.5 if j == 0 else 1.0)) for j in range(2)])
        attn = sb("attn", [P, NT, MIXD])

        def finish(dve, t, ps, inverse):
            return dve.tensor_scalar(attn[:, t, :], ps, inverse, None, ALU.mult)
        wide_attention(net, [qk[:, 0, :]], [qk[:, 1, :]], lambda c: qkv[:, c, 2, :], MIXD, True, finish)
        mixed = sb("mixed", [P, 2, MIX, MIXD])
        mixed_c = sb("mixed_c", [P, 8, T])
        with net.block() as (block, sem):
            mixed_done, turned_done, copied_done = sem("mixed"), sem("transposed"), sem("copied")

            @block.vector
            def _(dve):
                for t in range(NT):
                    if t >= 2:
                        dve.wait_ge(turned_done, 2 * (t - 1))
                    dve.tensor_tensor(mixed[:, t % 2, :, :], attn[:, t, :].unsqueeze(1).broadcast_to([P, MIX, MIXD]),
                                      gate[:, t, :].unsqueeze(2).broadcast_to([P, MIX, MIXD]), ALU.mult).then_inc(mixed_done, 1)

            @block.tensor
            def _(pe):
                for t in range(NT):
                    pe.wait_ge(mixed_done, t + 1)
                    flat = mixed[:, t % 2, :, :].rearrange("p e d -> p (e d)")
                    for h in range(2):
                        for c in range(4):
                            mm = pe.transpose(net.psum[:, 2 * t + h, c * P:(c + 1) * P],
                                              flat[:, (4 * h + c) * P:(4 * h + c + 1) * P], net.ident)
                        mm.then_inc(turned_done, 1)

            @block.scalar
            def _(act):
                for t in range(NT):
                    for h in range(2):
                        act.wait_ge(turned_done, 2 * t + h + 1)
                        act.activation(mixed_c[:, 4 * h:4 * h + 4, t * P:(t + 1) * P],
                                       net.psum[:, 2 * t + h, :].rearrange("p (c n) -> p c n", c=4), ACT.Copy)\
                           .then_inc(copied_done, 1)
        add_output(net, x, mixed_c, 8, P, W["o"], None)


def L1_attn(net, W, x, xn, xc, **_):
    narrow_attention(net, W, x, xc, xc, HD ** -0.5, True, None, 1e-8)


def L1_xattn(net, W, x, xn, xc, cc, **_):
    with ExitStack() as ctx:
        q = net.sbuf("q", [P, NC, T], ctx=ctx)
        k = net.sbuf("k", [P, NC, T], ctx=ctx)
        v = net.sbuf("v", [P, NT, D], ctx=ctx)
        o = net.sbuf("o", [P, NC, D, 2], ctx=ctx)
        table = []
        for c in range(NC):
            table.append(cols_out("dve", W["wq"], D, xc, c * P, q[:, c, :], ("scalar", W["bq"][:, c:c + 1], D ** -0.5, ALU.add, ALU.mult)))
            table.append(cols_out("act", W["wk"], D, cc, c * P, k[:, c, :], ("act", ACT.Identity, W["bk"][:, c:c + 1], 1.0)))
        table += [rows_out(alternate(t), cc, t, W["wv"], D, 0, D, v[:, t, :], copied(alternate(t)), W["bv"], net.ones) for t in range(NT)]
        products(net, table)

        def finish(dve, t, ps, inverse):
            return dve.tensor_scalar(o[:, t % 2, :, t // 2], ps, inverse, None, ALU.mult)
        wide_attention(net, [q[:, c, :] for c in range(NC)], [k[:, c, :] for c in range(NC)],
                       lambda c: v[:, c, :], D, False, finish)
        add_output(net, x, o[:, :, :, :].rearrange("p c f r -> p c (f r)"), NC, P, W["wo"], W["bo"])


def ternary(net, W):
    with ExitStack() as ctx:
        part = net.sbuf("part", [P, 2], ctx=ctx)
        gamma = net.sbuf("gamma", [P, 2], ctx=ctx)
        edge = net.sbuf("edge", [P, 2, 2], ctx=ctx)
        low = net.sbuf("low", [P, F * D // P], ctx=ctx)
        with net.block() as (block, sem):
            step, sum_done = sem("step"), sem("sum over partitions")

            @block.tensor
            def _(pe):
                pe.wait_ge(step, 2)
                pe.matmul(net.psum[:, 0, 0:2], net.ones_pp, part[:, :], start=True, stop=True).then_inc(sum_done, 1)

            @block.vector
            def _(dve):
                n = 0

                def then(ins):
                    nonlocal n
                    n += 1
                    ins.then_inc(step, 1)
                    dve.wait_ge(step, n)
                for i, w in enumerate((W["fc"], W["proj"])):
                    then(dve.tensor_reduce(part[:, i:i + 1], w, AX.X, ALU.add, apply_absolute_value=True))
                dve.wait_ge(sum_done, 1)
                then(dve.tensor_scalar(gamma[:, :], net.psum[:, 0, 0:2], 1.0 / (F * D), 1e-6, ALU.mult, ALU.add))
                then(dve.tensor_scalar(edge[:, 0, :], gamma[:, :], 0.5, None, ALU.mult))
                then(dve.tensor_scalar(edge[:, 1, :], gamma[:, :], -0.5, None, ALU.mult))
                for i, w in enumerate((W["fc"], W["proj"])):
                    then(dve.tensor_scalar(low[:, :], w, edge[:, 1, i:i + 1], None, ALU.is_lt))
                    then(dve.scalar_tensor_tensor(out=w, in0=w, scalar=edge[:, 0, i:i + 1], in1=low[:, :],
                                                  op0=ALU.is_gt, op1=ALU.subtract))


def L1_ffn(net, W, x, xn, xc, **_):
    ternary(net, W)
    with ExitStack() as ctx:
        h = net.sbuf("h", [P, NT, F], ctx=ctx)
        hc = net.sbuf("hc", [P, F // P, T], ctx=ctx)
        table = []
        for t in range(NT):
            for half in range(2):
                table.append(rows_out("act", xc, t, W["fc"], F, half * BANK, BANK, h[:, t, half * BANK:(half + 1) * BANK],
                                      ("act", ACT.Gelu, None, 1.0)))
        products(net, table)
        stats = net.sbuf("stats", [P, NT, 2, 6], ctx=ctx)
        mv = net.sbuf("mean_var", [P, NT, 2], ctx=ctx)
        rstd = net.sbuf("rstd", [P, NT], ctx=ctx)
        with net.block() as (block, sem):
            stats_done, mv_done, rstd_done, guarded = sem("stats"), sem("mean and variance"), sem("1/std"), sem("variance + eps")

            @block.gpsimd
            def _(pool):
                pool.wait_ge(mv_done, NT)
                pool.tensor_scalar(rstd[:, :], mv[:, :, 1], LN_EPS, None, ALU.add, ALU.bypass).then_inc(guarded, 1)
                pool.wait_ge(guarded, 1)
                pool.tensor_tensor(rstd[:, :], rstd[:, :], net.minus_half[:, 0:NT], ALU.pow).then_inc(rstd_done, 1)

            @block.vector
            def _(dve):
                for t in range(NT):
                    for half in range(2):
                        dve.bn_stats(stats[:, t, half, :], h[:, t, half * BANK:(half + 1) * BANK]).then_inc(stats_done, 1)
                for t in range(NT):
                    dve.wait_ge(stats_done, 2 * t + 2)
                    dve.bn_aggr(mv[:, t, :], stats[:, t, :, :].rearrange("p a b -> p (a b)")).then_inc(mv_done, 1)
                dve.wait_ge(rstd_done, 1)
                for t in range(NT):
                    dve.tensor_scalar(h[:, t, :], h[:, t, :], mv[:, t, 0:1], rstd[:, t:t + 1], ALU.subtract, ALU.mult)
        table = []
        for c in range(F // P):
            w, b = W["ln_w"][:, c:c + 1], W["ln_b"][:, c:c + 1]
            fin = ("act", ACT.Identity, b, w) if c % 2 == 0 else ("scalar", w, b, ALU.mult, ALU.add)
            table.append(Product(alternate(c), P, T, turned([h[:, t, c * P:(c + 1) * P] for t in range(NT)], net.ident),
                                 hc[:, c, :], fin))
        products(net, table)
        add_output(net, x, hc, F // P, P, W["proj"], None)


def L2_attn(net, W, x, xn, xc, **_):
    def fill(qc, kc, v):
        with ExitStack() as ctx:
            qk = net.sbuf("qk", [P, NT, 2, D], ctx=ctx)
            wide = net.sbuf("wide", [P, NT, 2, H, PITCH], ctx=ctx)
            table = []
            for t in range(NT):
                table.append(rows_out("act", xc, t, W["wqkv"], 3 * D, 0, 2 * D, qk[:, t, :, :].rearrange("p a b -> p (a b)"),
                                      COPY, W["bqkv"], net.ones))
                table.append(rows_out("dve", xc, t, W["wqkv"], 3 * D, 2 * D, D, v[:, t, :, 0:HD], VCOPY, W["bqkv"],
                                      net.ones, split=H))
            products(net, table)
            stats = net.sbuf("stats", [P, NT, 2, 6], ctx=ctx)
            mv = net.sbuf("mean_var", [P, NT, 2, 2], ctx=ctx)
            rstd = net.sbuf("rstd", [P, NT, 2], ctx=ctx)
            with net.block() as (block, sem):
                stats_done, mv_done, rstd_done, zeroed, scaled = (sem("stats"), sem("mean and variance"), sem("1/std"),
                                                                  sem("zeroed"), sem("variance scaled"))

                @block.gpsimd
                def _(pool):
                    pool.memset(wide[:, :, :, :, :], 0.0).then_inc(zeroed, 1)
                    pool.wait_ge(mv_done, 2 * NT)
                    pool.tensor_scalar(rstd[:, :, :], mv[:, :, :, 1], D / (D - 1), None, ALU.mult, ALU.bypass).then_inc(scaled, 1)
                    pool.wait_ge(scaled, 1)
                    pool.tensor_tensor(rstd[:, :, :], rstd[:, :, :], net.half[:, 0:2 * NT].rearrange("p (t j) -> p t j", j=2),
                                       ALU.pow).then_inc(rstd_done, 1)

                @block.vector
                def _(dve):
                    for t in range(NT):
                        for j in range(2):
                            dve.bn_stats(stats[:, t, j, :], qk[:, t, j, :]).then_inc(stats_done, 1)
                    for t in range(NT):
                        for j in range(2):
                            dve.wait_ge(stats_done, 2 * t + j + 1)
                            dve.bn_aggr(mv[:, t, j, :], stats[:, t, j, :]).then_inc(mv_done, 1)
                    dve.wait_ge(rstd_done, 1)
                    dve.tensor_scalar(rstd[:, :, :], rstd[:, :, :], 1e-6, None, ALU.add).then_inc(rstd_done, 1)
                    dve.wait_ge(rstd_done, 2)
                    dve.reciprocal(rstd[:, :, :], rstd[:, :, :]).then_inc(rstd_done, 1)
                    dve.wait_ge(rstd_done, 3)
                    dve.wait_ge(zeroed, 1)
                    for t in range(NT):
                        for j in range(2):
                            dve.tensor_scalar(wide[:, t, j, :, 0:HD], qk[:, t, j, :].rearrange("p (h d) -> p h d", h=H),
                                              mv[:, t, j, 0:1], rstd[:, t, j:j + 1], ALU.subtract, ALU.mult)
            table = []
            for j, (dst, gain, offset) in enumerate(((qc, W["gq"], W["hq"]), (kc, W["gk"], W["hk"]))):
                for g in range(GROUPS):
                    tiles = [wide[:, t, j, 4 * g:4 * g + 4, :].rearrange("p h d -> p (h d)") for t in range(NT)]
                    table.append(Product("act", P, T, turned(tiles, net.ident), dst[:, g, :],
                                         ("act", ACT.Square, offset[:, g:g + 1], gain[:, g:g + 1])))
            products(net, table)
    narrow_attention(net, W, x, xc, xc, 1.0, True, W["bo"], 1e-6, linear=True, fill=fill, qk=lambda *a: [])


def L2_xattn(net, W, x, xn, xc, cc, mask, mask_t, b, **_):
    with ExitStack() as ctx:
        sb = lambda name, shape, dt=F32: net.sbuf(name, shape, dt, ctx=ctx)
        mrows, mcols = sb("mrows", [P, NT, T], BF16), sb("mcols", [P, NT, T], BF16)
        with ExitStack() as inner:
            raw = net.sbuf("raw", [P, 2, NT, T], I32, ctx=inner)
            with net.block() as (block, sem):
                loaded = sem("mask")

                @block.sync
                def _(sp):
                    sp.dma_start(raw[:, 0, :, :], mask[b].rearrange("(t p) k -> p t k", p=P)).then_inc(loaded, 16)
                    sp.dma_start(raw[:, 1, :, :], mask_t[b].rearrange("(t p) k -> p t k", p=P)).then_inc(loaded, 16)

                @block.vector
                def _(dve):
                    dve.wait_ge(loaded, 32)
                    dve.tensor_scalar(mrows[:, :, :], raw[:, 0, :, :], 0, MASKED, ALU.is_equal, ALU.mult)
                    dve.tensor_scalar(mcols[:, :, :], raw[:, 1, :, :], 0, MASKED, ALU.is_equal, ALU.mult)
        qc, kc = sb("qc", [P, 4, T]), sb("kc", [P, 4, T])
        v, o = sb("v", [P, NT, 4, DK + 1]), sb("o", [P, 4, T])
        for four in range(4):
            with net.block() as (block, sem):
                @block.gpsimd
                def _(pool):
                    pool.memset(v[:, :, :, DK:DK + 1], 1.0)

                @block.vector
                def _(dve):
                    dve.memset(qc[DK:DK + 1, :, :], 0.0)
                    dve.memset(kc[DK:DK + 1, :, :], 1.0)
            table = []
            for u in range(4):
                h = 4 * four + u
                table.append(cols_out("dve", W["wq"], F, xc, h * DK, qc[0:DK, u, :],
                                      ("scalar", W["bq"][0:DK, h:h + 1], DK ** -0.5, ALU.add, ALU.mult), rows=DK))
                table.append(cols_out("act", W["wk"], F, cc, h * DK, kc[0:DK, u, :],
                                      ("act", ACT.Identity, W["bk"][0:DK, h:h + 1], 1.0), rows=DK))
            table += [rows_out(alternate(t), cc, t, W["wv"], F, four * D, D, v[:, t, :, 0:DK], copied(alternate(t)),
                               W["bv"], net.ones, split=4) for t in range(NT)]
            products(net, table)
            many_heads(net, qc, kc, lambda kt, u: v[:, kt, u, :], DK, o, mask_rows=mrows, mask_cols=mcols)
            normalise(net, o, DK, 1e-30, ALU.max)
            add_output(net, x, o, 4, DK, W["wo"][:, four * 4 * D:(four + 1) * 4 * D], W["bo"] if four == 0 else None)


def L2_ffn(net, W, x, xn, xc, w1, w2, arena, **_):
    with ExitStack() as ctx:
        sb = lambda name, shape, dt=F32: net.sbuf(name, shape, dt, ctx=ctx)
        xr, xrc = sb("xr", [P, NT, D]), sb("xrc", [P, NC, T])
        sq, ms = sb("sq", [P, D]), sb("ms", [P, NT])
        logit, top, index, indexf = sb("logit", [P, NT, 8]), sb("top", [P, NT, 8]), sb("index", [P, NT, 8], U32), sb("indexf", [P, NT])
        e, tot, gate, gate_c = sb("e", [P, NT, 8]), sb("tot", [P, NT]), sb("gate", [P, NT, 8]), sb("gate_c", [EXPERTS, T])
        with net.block() as (block, sem):
            step, mean_done, root_done = sem("step"), sem("mean square"), sem("1/root")

            @block.gpsimd
            def _(pool):
                pool.wait_ge(mean_done, 1)
                pool.tensor_tensor(ms[:, :], ms[:, :], net.minus_half[:, 0:NT], ALU.pow).then_inc(root_done, 1)

            @block.vector
            def _(dve):
                n = 0

                def then(ins):
                    nonlocal n
                    n += 1
                    ins.then_inc(step, 1)
                    dve.wait_ge(step, n)
                for t in range(NT):
                    then(dve.tensor_tensor_reduce(sq[:, :], xn[:, t, :], xn[:, t, :], 1.0, 0.0, ALU.mult, ALU.add, ms[:, t:t + 1]))
                dve.tensor_scalar(ms[:, :], ms[:, :], 1.0 / D, 1e-6, ALU.mult, ALU.add).then_inc(mean_done, 1)
                dve.wait_ge(root_done, 1)
                for t in range(NT):
                    then(dve.tensor_scalar(xr[:, t, :], xn[:, t, :], ms[:, t:t + 1], None, ALU.mult))
        products(net, [Product("dve", P, T, turned([xr[:, t, c * P:(c + 1) * P] for t in range(NT)], net.ident), xrc[:, c, :],
                               ("scalar", W["rms"][:, c:c + 1], None, ALU.mult, ALU.bypass)) for c in range(NC)])
        products(net, [rows_out("dve", xrc, t, W["gate"], 8, 0, 8, logit[:, t, :], VCOPY) for t in range(NT)])
        with net.block() as (block, sem):
            step, shifted, exped, ready, turned_done = (sem("step"), sem("logits - max"), sem("exp"), sem("gates"),
                                                        sem("gates transposed"))

            @block.vector
            def _(dve):
                n = 0

                def then(ins):
                    nonlocal n
                    n += 1
                    ins.then_inc(step, 1)
                    dve.wait_ge(step, n)
                for t in range(NT):
                    then(dve.max(top[:, t, :], logit[:, t, :]))
                    then(dve.max_index(index[:, t, :], top[:, t, :], logit[:, t, :]))
                dve.tensor_tensor(e[:, :, :], logit[:, :, :], top[:, :, 0:1].broadcast_to([P, NT, 8]),
                                  ALU.subtract).then_inc(shifted, 1)
                then(dve.tensor_copy(indexf[:, :], index[:, :, 0]))
                dve.wait_ge(exped, 1)
                then(dve.tensor_reduce(tot[:, :], e[:, :, :], AX.X, ALU.add))
                then(dve.reciprocal(tot[:, :], tot[:, :]))
                then(dve.tensor_tensor(gate[:, :, :], net.iota[:, 0:8].unsqueeze(1).broadcast_to([P, NT, 8]),
                                       indexf[:, :].unsqueeze(2).broadcast_to([P, NT, 8]), ALU.is_equal))
                dve.tensor_tensor(gate[:, :, :], gate[:, :, :], tot[:, :].unsqueeze(2).broadcast_to([P, NT, 8]), ALU.mult)\
                   .then_inc(ready, 1)
                dve.wait_ge(turned_done, 1)
                dve.tensor_copy(gate_c[:, :], net.psum[0:EXPERTS, 0, :])

            @block.scalar
            def _(act):
                act.wait_ge(shifted, 1)
                act.activation(e[:, :, :], e[:, :, :], ACT.Exp).then_inc(exped, 1)

            @block.tensor
            def _(pe):
                pe.wait_ge(ready, 1)
                for t in range(NT):
                    mm = pe.transpose(net.psum[0:EXPERTS, 0, t * P:(t + 1) * P], gate[:, t, :], net.ident)
                mm.then_inc(turned_done, 1)
        products(net, [Product("dve", P, D, summed([(gate_c[:, t * P:(t + 1) * P], W["b2"][0:EXPERTS, :])]), x[:, t, :],
                               ("tensor", x[:, t, :], ALU.add)) for t in range(NT)])
        hidden = sb("hidden", [P, 2, HIDDEN_CHUNKS, T])
        base = ARENA - 8192
        slot = [arena[:, base + 4096 * i:base + 4096 * (i + 1)] for i in range(2)]
        with net.block() as (block, sem):
            loaded = [sem("expert's weights in slot 0"), sem("expert's weights in slot 1")]
            up_done, act_done, down_done, added = sem("up product"), sem("silu"), sem("down product"), sem("added to x")

            @block.sync
            def _(sp):
                for n in range(EXPERTS):
                    if n >= 2:
                        sp.wait_ge(down_done, NT * (n - 1))
                    sp.dma_start(slot[n % 2][:, 0:2048], w1[n]).then_inc(loaded[n % 2], 16)
                    sp.dma_start(slot[n % 2][:, 2048:4096], w2[n]).then_inc(loaded[n % 2], 16)

            @block.tensor
            def _(pe):
                def up(n):
                    pe.wait_ge(loaded[n % 2], 32 * (n // 2 + 1))
                    for f in range(HIDDEN_CHUNKS):
                        m = n * HIDDEN_CHUNKS + f
                        if m >= 4:
                            pe.wait_ge(act_done, m - 3)
                        for c in range(NC):
                            at = c * F + f * P
                            mm = pe.matmul(net.psum[:, m % 4, :], slot[n % 2][:, at:at + P], xrc[:, c, :],
                                           start=c == 0, stop=c == 1)
                        mm.then_inc(up_done, 1)

                def down(n):
                    pe.wait_ge(act_done, HIDDEN_CHUNKS * (n + 1))
                    for t in range(NT):
                        m = n * NT + t
                        if m >= 4:
                            pe.wait_ge(added, m - 3)
                        for f in range(HIDDEN_CHUNKS):
                            at = 2048 + f * D
                            mm = pe.matmul(net.psum[:, 4 + m % 4, 0:D], hidden[:, n % 2, f, t * P:(t + 1) * P],
                                           slot[n % 2][:, at:at + D], start=f == 0, stop=f == HIDDEN_CHUNKS - 1)
                        mm.then_inc(down_done, 1)
                up(0)
                for n in range(EXPERTS):
                    if n + 1 < EXPERTS:
                        up(n + 1)
                    down(n)

            @block.scalar
            def _(act):
                for n in range(EXPERTS):
                    if n >= 2:
                        act.wait_ge(down_done, NT * (n - 1))
                    for f in range(HIDDEN_CHUNKS):
                        m = n * HIDDEN_CHUNKS + f
                        act.wait_ge(up_done, m + 1)
                        act.activation(hidden[:, n % 2, f, :], net.psum[:, m % 4, :], ACT.Silu,
                                       bias=W["b1"][:, m:m + 1]).then_inc(act_done, 1)

            @block.vector
            def _(dve):
                for n in range(EXPERTS):
                    for t in range(NT):
                        m = n * NT + t
                        dve.wait_ge(down_done, m + 1)
                        if m >= NT:
                            dve.wait_ge(added, m - NT + 1)
                        dve.scalar_tensor_tensor(out=x[:, t, :], in0=net.psum[:, 4 + m % 4, 0:D], scalar=gate[:, t, n:n + 1],
                                                 in1=x[:, t, :], op0=ALU.mult, op1=ALU.add).then_inc(added, 1)


def L3_attn(net, W, x, xn, xc, **_):
    def fill(qc, kc, v):
        with ExitStack() as ctx:
            a, r = net.sbuf("a", [P, GROUPS, T], ctx=ctx), net.sbuf("r", [P, GROUPS, T], ctx=ctx)
            for dst, w, wr in ((qc, W["wq"], W["wqr"]), (kc, W["wk"], W["wkr"])):
                table = []
                for g in range(GROUPS):
                    table.append(cols_out("dve", w, GROUPS * P, xc, g * P, a[:, g, :], ("tensor", W["cos"], ALU.mult)))
                    table.append(cols_out("dve", wr, GROUPS * P, xc, g * P, r[:, g, :], ("tensor", W["sin"], ALU.mult)))
                products(net, table)
                with net.block() as (block, sem):
                    added = sem("rotated")

                    @block.vector
                    def _(dve):
                        if dst is kc:
                            dve.scalar_tensor_tensor(out=dst[:, :, :], in0=a[:, :, :], scalar=net.aug, in1=r[:, :, :],
                                                     op0=ALU.add, op1=ALU.add)
                        else:
                            dve.tensor_tensor(a[:, :, :], a[:, :, :], r[:, :, :], ALU.add).then_inc(added, 1)

                    @block.scalar
                    def _(act):
                        if dst is qc:
                            act.wait_ge(added, 1)
                            act.activation(dst[:, :, :], a[:, :, :], ACT.Copy, scale=HD ** -0.5)
            products(net, fill_values(net, v, xc, W["wv"]))
    narrow_attention(net, W, x, xc, xc, 1.0, True, W["bo"], 0.0, fill=fill, qk=lambda *a: [])


def L3_xattn(net, W, x, xn, xc, ct, cc, kmask, b, **_):
    with ExitStack() as ctx:
        sb = lambda name, shape, dt=F32: net.sbuf(name, shape, dt, ctx=ctx)
        q, k = sb("q", [P, NC, T]), sb("k", [P, NC, T])
        raw, keep, gone = sb("raw", [P, T // 4], I32), sb("keep", [P, T]), sb("gone", [P, T])
        table = []
        for c in range(NC):
            table.append(cols_out("act", W["w"], D, xc, c * P, q[:, c, :], ("act", ACT.Relu, W["b"][:, c:c + 1], 1.0)))
            table.append(cols_out("dve", W["w"], D, cc, c * P, k[:, c, :], ("scalar", W["b"][:, c:c + 1], 0.0, ALU.add, ALU.max)))
        products(net, table)
        with net.block() as (block, sem):
            loaded = sem("mask")

            @block.sync
            def _(sp):
                sp.dma_start(raw[:, :], kmask[b].partition_broadcast(P)).then_inc(loaded, 16)

            @block.vector
            def _(dve):
                for c in range(NC):
                    dve.tensor_scalar(k[:, c, :], k[:, c, :], W["d"][:, c:c + 1], None, ALU.mult)
                dve.wait_ge(loaded, 16)
                dve.tensor_scalar(keep[:, :], raw[:, :].bitcast(U8), 0, None, ALU.is_equal)
                dve.tensor_scalar(gone[:, :], raw[:, :].bitcast(U8), 0, MASKED, ALU.not_equal, ALU.mult)

        def finish(dve, t, ps, inverse):
            return dve.scalar_tensor_tensor(out=x[:, t, :], in0=ps, scalar=inverse, in1=x[:, t, :],
                                            op0=ALU.mult, op1=ALU.add)
        wide_attention(net, [q[:, c, :] for c in range(NC)], [k[:, c, :] for c in range(NC)],
                       lambda c: ct[:, c, :], D, False, finish, keep=keep[:, :], gone=gone[:, :])


def L3_ffn(net, W, x, xn, xc, **_):
    with ExitStack() as ctx:
        sb = lambda name, shape, dt=F32: net.sbuf(name, shape, dt, ctx=ctx)
        hc, sim = sb("hc", [SLOTD, 1, T]), sb("sim", [P, NT, SLOTS])
        top, index, indexf = sb("top", [P, NT, 8]), sb("index", [P, NT, 8], U32), sb("indexf", [P, NT, 8])
        e, tot, gate, hit = sb("e", [P, NT, 4]), sb("tot", [P, NT]), sb("gate", [P, NT, SLOTS]), sb("hit", [P, NT, SLOTS])
        gate_c = sb("gate_c", [SLOTS, T])
        products(net, [Product("act", SLOTD, T, summed([(W["hash"][:, c * SLOTD:(c + 1) * SLOTD], xc[:, c, :]) for c in range(NC)]),
                               hc[:, 0, :], COPY)])
        products(net, [Product("act", P, SLOTS, summed([(hc[:, 0, t * P:(t + 1) * P], W["keys"][0:SLOTD, :])]), sim[:, t, :], COPY)
                       for t in range(NT)])
        with net.block() as (block, sem):
            step, shifted, exped, ready, turned_done = (sem("step"), sem("values - max"), sem("exp"), sem("gates"),
                                                        sem("gates transposed"))

            @block.vector
            def _(dve):
                n = 0

                def then(ins):
                    nonlocal n
                    n += 1
                    ins.then_inc(step, 1)
                    dve.wait_ge(step, n)
                for t in range(NT):
                    then(dve.max(top[:, t, :], sim[:, t, :]))
                    then(dve.max_index(index[:, t, :], top[:, t, :], sim[:, t, :]))
                dve.tensor_tensor(e[:, :, :], top[:, :, 0:4], top[:, :, 0:1].broadcast_to([P, NT, 4]),
                                  ALU.subtract).then_inc(shifted, 1)
                then(dve.tensor_copy(indexf[:, :, :], index[:, :, :]))
                dve.wait_ge(exped, 1)
                then(dve.tensor_reduce(tot[:, :], e[:, :, :], AX.X, ALU.add))
                then(dve.reciprocal(tot[:, :], tot[:, :]))
                then(dve.tensor_tensor(e[:, :, :], e[:, :, :], tot[:, :].unsqueeze(2).broadcast_to([P, NT, 4]), ALU.mult))
                iota = net.iota[:, :].unsqueeze(1).broadcast_to([P, NT, SLOTS])
                for i in range(4):
                    dst = gate if i == 0 else hit
                    then(dve.tensor_tensor(dst[:, :, :], iota, indexf[:, :, i:i + 1].broadcast_to([P, NT, SLOTS]), ALU.is_equal))
                    then(dve.tensor_tensor(dst[:, :, :], dst[:, :, :], e[:, :, i:i + 1].broadcast_to([P, NT, SLOTS]), ALU.mult))
                    if i:
                        ins = dve.tensor_tensor(gate[:, :, :], gate[:, :, :], hit[:, :, :], ALU.add)
                        if i < 3:
                            then(ins)
                ins.then_inc(ready, 1)
                dve.wait_ge(turned_done, 1)
                dve.tensor_copy(gate_c[:, :], net.psum[0:SLOTS, 0, :])

            @block.scalar
            def _(act):
                act.wait_ge(shifted, 1)
                act.activation(e[:, :, :], e[:, :, :], ACT.Exp).then_inc(exped, 1)

            @block.tensor
            def _(pe):
                pe.wait_ge(ready, 1)
                for t in range(NT):
                    mm = pe.transpose(net.psum[0:SLOTS, 0, t * P:(t + 1) * P], gate[:, t, :], net.ident)
                mm.then_inc(turned_done, 1)
        silu = sb("silu", [P, 2, T])
        proj = sb("proj", [P, SLOTS * SLOTD // P, T])
        chunks = SLOTS * SLOTD // P
        with net.block() as (block, sem):
            down_done, spread_done, silu_done, weighed = sem("down product"), sem("gates spread"), sem("silu"), sem("weighed")

            @block.tensor
            def _(pe):
                for n in range(chunks):
                    if n >= 2:
                        pe.wait_ge(weighed, n - 1)
                    for c in range(NC):
                        at = c * SLOTS * SLOTD + n * P
                        mm = pe.matmul(net.psum[:, n % 2, :], W["down"][:, at:at + P], xc[:, c, :], start=c == 0, stop=c == 1)
                    mm.then_inc(down_done, 1)
                    pe.matmul(net.psum[:, 2 + n % 2, :], W["spread"][0:SLOTS, n * P:(n + 1) * P], gate_c[:, :],
                              start=True, stop=True).then_inc(spread_done, 1)

            @block.scalar
            def _(act):
                for n in range(chunks):
                    act.wait_ge(down_done, n + 1)
                    if n >= 2:
                        act.wait_ge(weighed, n - 1)
                    act.activation(silu[:, n % 2, :], net.psum[:, n % 2, :], ACT.Silu).then_inc(silu_done, 1)

            @block.vector
            def _(dve):
                for n in range(chunks):
                    dve.wait_ge(silu_done, n + 1)
                    dve.wait_ge(spread_done, n + 1)
                    dve.tensor_tensor(proj[:, n, :], silu[:, n % 2, :], net.psum[:, 2 + n % 2, :], ALU.mult).then_inc(weighed, 1)
        out = sb("out", [P, NT, D])
        table = []
        for t in range(NT):
            terms = [(proj[:, c, t * P:(t + 1) * P], W["up"][:, c * D:(c + 1) * D]) for c in range(chunks)]
            table.append(Product("dve", P, D, summed(terms), out[:, t, :], ("stt", W["scale"], xn[:, t, :], ALU.mult, ALU.add)))
        products(net, table)
        with net.block() as (block, sem):
            @block.vector
            def _(dve):
                dve.tensor_tensor(x[:, :, :], x[:, :, :], out[:, :, :], ALU.add)


BODIES = dict(L0_attn=L0_attn, L0_xattn=L0_xattn, L0_ffn=L0_ffn, L1_attn=L1_attn, L1_xattn=L1_xattn, L1_ffn=L1_ffn,
              L2_attn=L2_attn, L2_xattn=L2_xattn, L2_ffn=L2_ffn, L3_attn=L3_attn, L3_xattn=L3_xattn, L3_ffn=L3_ffn)


def decoder(nc, x_d, ctx_d, mask_d, mask_t_d, kmask_d, w1_d, w2_d, consts_d, packs_d, out_d, batches=B, sublayers=SUBLAYERS):
    with ExitStack() as ctx:
        net = Net(nc, ctx)
        spots, width = offsets(CONSTS)
        consts = net.sbuf("consts", [P, width])
        (net.ident, net.causal, net.den16, net.den64, net.aug, net.iota, net.ones, net.half, net.minus_half,
         net.causal_cols) = (consts[:, at:at + n] for at, n in spots.values())
        net.ones_pp = net.ones
        narrow = net.sbuf("narrow", [P, 3, P], BF16)
        net.ident16, net.causal16, net.causal_cols16 = (narrow[:, i, :] for i in range(3))
        arenas = [net.sbuf("arena0", [P, ARENA]), net.sbuf("arena1", [P, ARENA])]
        x, xn, xc = net.sbuf("x", [P, NT, D]), net.sbuf("xn", [P, NT, D]), net.sbuf("xc", [P, NC, T])
        ct, cc = net.sbuf("ct", [P, NT, D]), net.sbuf("cc", [P, NC, T])
        with net.block() as (block, sem):
            loaded = sem("constants")

            @block.sync
            def _(sp):
                sp.dma_start(consts[:, :], consts_d).then_inc(loaded, 16)
                sp.wait_ge(loaded, 16)

            @block.vector
            def _(dve):
                dve.wait_ge(loaded, 16)
                dve.tensor_copy(net.ident16, net.ident)
                dve.tensor_copy(net.causal16, net.causal[:, BANK - P:BANK])
                dve.tensor_copy(net.causal_cols16, net.causal_cols)
        blocks_start = net.turn
        with nc.Fori(0, batches) as b:
            with net.block() as (block, sem):
                x_loaded, ctx_loaded = sem("x"), sem("context")

                @block.sync
                def _(sp):
                    sp.dma_start(x[:, :, :], x_d[b].rearrange("(t p) d -> p t d", p=P)).then_inc(x_loaded, 16)
                    sp.dma_start(ct[:, :, :], ctx_d[b].rearrange("(t p) d -> p t d", p=P)).then_inc(ctx_loaded, 16)
                    first = packs_d[sublayers[0]]
                    sp.dma_start(arenas[0][:, 0:first.shape[1]], first).then_inc(x_loaded, 16)
                    sp.wait_ge(x_loaded, 32)
                    sp.wait_ge(ctx_loaded, 16)
            products(net, [Product(alternate(c), P, T, turned([ct[:, t, c * P:(c + 1) * P] for t in range(NT)], net.ident),
                                   cc[:, c, :], copied(alternate(c))) for c in range(NC)])
            for s, name in enumerate(sublayers):
                arena = arenas[s % 2]
                W = {field: arena[:, at:at + n] for field, (at, n) in offsets(WIDTHS[name])[0].items()}
                with ExitStack() as prefetch:
                    layernorm(net, x, xn, xc)
                    BODIES[name](net, W, x=x, xn=xn, xc=xc, ct=ct, cc=cc, mask=mask_d, mask_t=mask_t_d, kmask=kmask_d,
                                 w1=w1_d, w2=w2_d, arena=arena, b=b)
                    if s + 1 < len(sublayers):
                        nxt = packs_d[sublayers[s + 1]]
                        with net.block() as (block, sem):
                            loaded = sem("weights")

                            @block.sync
                            def _(sp):
                                sp.dma_start(arenas[(s + 1) % 2][:, 0:nxt.shape[1]], nxt).then_inc(loaded, 16)
                                sp.wait_ge(loaded, 16)
            with net.block() as (block, sem):
                stored = sem("output")

                @block.sync
                def _(sp):
                    sp.dma_start(out_d[b].rearrange("(t p) d -> p t d", p=P), x[:, :, :]).then_inc(stored, 16)
                    sp.wait_ge(stored, 16)
            if net.turn != blocks_start:
                with net.block() as (block, sem):
                    pass



def by_chunk(w):
    k, n = w.shape
    return w.reshape(k // P, P, n).transpose(1, 0, 2).reshape(P, -1)


def on_rows(a, rows=P):
    out = np.zeros((P, a.shape[-1]), np.float32)
    out[:a.shape[0]] = a
    return out


def apart(w):
    out = np.zeros((w.shape[0], H, PITCH), np.float32)
    out[:, :, :HD] = w.reshape(w.shape[0], H, HD)
    return out.reshape(w.shape[0], H * PITCH)


def apart_rows(w):
    return np.ascontiguousarray(apart(np.ascontiguousarray(w.T)).T)


def blocks_of(w):
    out = np.zeros((H, HD, H, HD), np.float32)
    for h in range(H):
        out[h, :, h, :] = w
    return out.reshape(D, D)


def by_head(w):
    out = np.zeros((HD, H, HD, H), np.float32)
    for h in range(H):
        out[:, h, :, h] = w[:, :, h]
    return out.reshape(D, D)


def pack(i):
    f32 = np.float32
    evens = np.r_[0:D:2, 1:D:2]
    half = D // 2
    inv = (1.0 / 10000.0 ** (np.arange(half, dtype=f32) / f32(half))).astype(f32)
    ang = (np.arange(T, dtype=f32)[None, :] * inv[:, None]).astype(f32)
    inv3 = (1.0 / 10000.0 ** (np.arange(0, HD, 2, dtype=f32) / f32(HD))).astype(f32)
    ang3 = np.repeat((np.arange(T, dtype=f32)[None, :] * inv3[:, None]).astype(f32), 2, axis=0)
    sign = np.tile(np.array([-1.0, 1.0], f32), HD // 2)[:, None]
    cos3, sin3 = np.zeros((4, PITCH, T), f32), np.zeros((4, PITCH, T), f32)
    cos3[:, :HD], sin3[:, :HD] = np.cos(ang3), np.sin(ang3) * sign
    swap = np.arange(D).reshape(-1, 2)[:, ::-1].reshape(-1)
    qkv3 = i["L3_attn_Wqkv"]
    cols = lambda v: np.ascontiguousarray(v.reshape(-1, P).T)
    heads = lambda v: np.ascontiguousarray(apart(v.reshape(1, D)).reshape(GROUPS, P).T)
    dk = lambda v: on_rows(v.reshape(H, DK).T)
    spread = np.zeros((SLOTS, SLOTS * SLOTD), f32)
    for s in range(SLOTS):
        spread[s, s * SLOTD:(s + 1) * SLOTD] = 1.0
    packs = {
        "L0_attn": dict(wq=by_chunk(by_head(i["L0_attn_w_q"])[:, evens]), wk=by_chunk(by_head(i["L0_attn_w_k"])[:, evens]),
                        wv=by_chunk(by_head(i["L0_attn_w_v"])), cos=np.cos(ang), sin=np.sin(ang)),
        "L0_xattn": dict(wq=by_chunk(apart(blocks_of(i["L0_xattn_Wq"].T))), wk=by_chunk(apart(blocks_of(i["L0_xattn_Wk"].T))),
                         wv=by_chunk(blocks_of(i["L0_xattn_Wv"].T)), wo=by_chunk(apart_rows(i["L0_xattn_Wo"].T)),
                         bo=on_rows(i["L0_xattn_bo"][None])),
        "L0_ffn": dict(sim=by_chunk(i["L0_ffn_sim_matrix"]), gates=np.tile(i["L0_ffn_gates"][None], (P, 1)),
                       **{j: by_chunk(i[f"L0_ffn_{j}_proj"].transpose(1, 0, 2).reshape(D, MIX * MIXD)) for j in "qkv"},
                       o=by_chunk(i["L0_ffn_o_proj"].reshape(MIX * MIXD, D))),
        "L1_attn": dict(wq=by_chunk(apart(i["L1_attn_Wq"].T)), wk=by_chunk(apart(i["L1_attn_Wkv"][:D].T)),
                        wv=by_chunk(i["L1_attn_Wkv"][D:].T), wo=by_chunk(apart_rows(i["L1_attn_Wo"].T))),
        "L1_xattn": dict(**{f"w{j}": by_chunk(i[f"L1_xattn_W{j}"]) for j in "qkvo"}, bq=cols(i["L1_xattn_bq"]),
                         bk=cols(i["L1_xattn_bk"]), bv=on_rows(i["L1_xattn_bv"][None]), bo=on_rows(i["L1_xattn_bo"][None])),
        "L1_ffn": dict(fc=by_chunk(i["L1_ffn_W_fc"].T), proj=by_chunk(i["L1_ffn_W_proj"].T), ln_w=cols(i["L1_ffn_ln_w"]),
                       ln_b=cols(i["L1_ffn_ln_b"])),
        "L2_attn": dict(wqkv=by_chunk(i["L2_attn_Wqkv"]), bqkv=on_rows(i["L2_attn_bqkv"][None]), gq=heads(i["L2_attn_gamma_q"]),
                        hq=heads(i["L2_attn_beta_q"]), gk=heads(i["L2_attn_gamma_k"]), hk=heads(i["L2_attn_beta_k"]),
                        wo=by_chunk(apart_rows(i["L2_attn_Wo"])), bo=on_rows(i["L2_attn_bo"][None])),
        "L2_xattn": dict(wq=by_chunk(i["L2_xattn_Wq"].T), wk=by_chunk(i["L2_xattn_Wk"].T), wv=by_chunk(i["L2_xattn_Wv"].T),
                         wo=on_rows(i["L2_xattn_Wo"].T.reshape(H, DK, D).transpose(1, 0, 2).reshape(DK, H * D)),
                         bq=dk(i["L2_xattn_bq"]), bk=dk(i["L2_xattn_bk"]), bv=on_rows(i["L2_xattn_bv"][None]),
                         bo=on_rows(i["L2_xattn_bo"][None])),
        "L2_ffn": dict(rms=cols(i["L2_ffn_rms_w"]), gate=by_chunk(i["L2_ffn_gate_w"].T),
                       b1=np.ascontiguousarray(i["L2_ffn_b1"].reshape(EXPERTS * HIDDEN_CHUNKS, P).T), b2=on_rows(i["L2_ffn_b2"])),
        "L3_attn": dict(wq=by_chunk(apart(qkv3[:, :D])), wqr=by_chunk(apart(qkv3[:, :D][:, swap])),
                        wk=by_chunk(apart(qkv3[:, D:2 * D])), wkr=by_chunk(apart(qkv3[:, D:2 * D][:, swap])),
                        wv=by_chunk(qkv3[:, 2 * D:]), wo=by_chunk(apart_rows(i["L3_attn_Wout"])),
                        cos=cos3.reshape(P, T), sin=sin3.reshape(P, T), bo=on_rows(i["L3_attn_bout"][None])),
        "L3_xattn": dict(w=by_chunk(i["L3_xattn_W"].T), b=cols(i["L3_xattn_b"]), d=cols(i["L3_xattn_D"][0])),
        "L3_ffn": dict(hash=by_chunk(i["L3_ffn_hasher_w"].T), keys=on_rows(i["L3_ffn_keys"].T),
                       down=by_chunk(i["L3_ffn_values_down"].transpose(1, 0, 2).reshape(D, SLOTS * SLOTD)),
                       up=by_chunk(i["L3_ffn_values_up"].reshape(SLOTS * SLOTD, D)), spread=on_rows(spread),
                       scale=np.tile(i["L3_ffn_scale"][None], (P, 1))),
    }
    out = {}
    for name, fields in WIDTHS.items():
        parts = [packs[name][field] for field, _ in fields]
        assert [p.shape for p in parts] == [(P, n) for _, n in fields], (name, [p.shape for p in parts])
        out[name] = np.ascontiguousarray(np.concatenate(parts, 1), dtype=f32)
    return out


def constants():
    f32 = np.float32
    causal = np.zeros((P, BANK), f32)
    causal[:, BANK - P:] = np.where(np.arange(P)[None, :] > np.arange(P)[:, None], f32(MASKED), f32(0))
    den16 = np.zeros((P, P), f32)
    for h in range(4):
        den16[h * PITCH + HD, h * PITCH:(h + 1) * PITCH] = 1.0
    den64 = np.zeros((P, P), f32)
    den64[DK] = 1.0
    aug = np.zeros((P, 1), f32)
    aug[HD::PITCH] = 1.0
    fields = dict(ident=np.eye(P, dtype=f32), causal=causal, den16=den16, den64=den64, aug=aug,
                  iota=np.tile(np.arange(64, dtype=f32)[None], (P, 1)), ones=np.ones((P, P), f32),
                  half=np.full((P, 16), 0.5, f32), minus_half=np.full((P, 16), -0.5, f32),
                  causal_cols=np.ascontiguousarray(causal[:, BANK - P:].T))
    return np.concatenate([fields[name] for name, _ in CONSTS], 1)


def host_arrays(inputs):
    i = {name: np.asarray(a) for name, a in inputs.items()}
    arrays = {
        "x": i["x"], "context": i["ctx_1024"], "mask": i["mask_BxSxS2_ik1"],
        "mask_t": np.ascontiguousarray(i["mask_BxSxS2_ik1"].transpose(0, 2, 1)),
        "key_mask": np.ascontiguousarray(i["mask_BxS2_bf0"]).view(np.int32),
        "w1": np.stack([by_chunk(w) for w in i["L2_ffn_W1"]]), "w2": np.stack([by_chunk(w) for w in i["L2_ffn_W2"]]),
        "consts": constants(),
    }
    return arrays, pack(i)


def kernel(**inputs):
    import concourse.bacc as _bacc
    from concourse.bass_utils import run_bass_kernel_spmd as _run

    arrays, packs = host_arrays(inputs)
    nc = _bacc.Bacc("TRN2", target_bir_lowering=False, num_devices=1)
    feed, aps = {}, {}
    for name, a in {**arrays, **{f"pack_{k}": v for k, v in packs.items()}}.items():
        feed[f"in_{name}"] = np.ascontiguousarray(a)
        aps[name] = nc.dram_tensor(f"in_{name}", a.shape, mybir.dt.from_np(a.dtype), kind="ExternalInput").ap()
    out = nc.dram_tensor("out", (B, T, D), F32, kind="ExternalOutput").ap()
    decoder(nc, aps["x"], aps["context"], aps["mask"], aps["mask_t"], aps["key_mask"], aps["w1"], aps["w2"],
            aps["consts"], {k: aps[f"pack_{k}"] for k in packs}, out)
    r = _run(nc, [feed], core_ids=[0])
    return r.results[0]["out"]
```

```python
from contextlib import ExitStack, contextmanager

import concourse.bass as bass
import numpy as np
from concourse import mybir

F32 = mybir.dt.float32
BF16 = mybir.dt.bfloat16
F32R = mybir.dt.float32r
I32 = mybir.dt.int32
U32 = mybir.dt.uint32
U8 = mybir.dt.uint8
ALU = mybir.AluOpType
ACT = mybir.ActivationFunctionType
AX = mybir.AxisListType

B, T, D, P = 4, 512, 256, 128
NT, NC = T // P, D // P
H, HD, PITCH = 16, D // 16, 32
GROUPS = H * PITCH // P
PAIRS = H // 2
STACK = 4 * HD
SPARE = 3 * HD
DK = 64
F = 1024
EXPERTS, HIDDEN_CHUNKS = 8, F // P
MIX, MIXD = 16, 64
SLOTS, SLOTD = 64, 32
BANK = 512
BANKS = 8
LN_EPS = 1e-5
MASKED = -1e30
ARENA = 11552
SEMS = 16

WIDTHS = {
    "L0_attn": [("wq", 512), ("wk", 512), ("wv", 512), ("cos", 512), ("sin", 512)],
    "L0_xattn": [("wq", 2048), ("wk", 2048), ("wv", 512), ("wo", 1024), ("bo", 256)],
    "L0_ffn": [("sim", 32), ("gates", 16), ("q", 2048), ("k", 2048), ("v", 2048), ("o", 2048)],
    "L1_attn": [("wq", 2048), ("wk", 2048), ("wv", 512), ("wo", 1024)],
    "L1_xattn": [("wq", 512), ("wk", 512), ("wv", 512), ("wo", 512), ("bq", 2), ("bk", 2),
                 ("bv", 256), ("bo", 256)],
    "L1_ffn": [("fc", 2048), ("proj", 2048), ("ln_w", 8), ("ln_b", 8)],
    "L2_attn": [("wqkv", 1536), ("bqkv", 768), ("gq", 8), ("hq", 8), ("gk", 8), ("hk", 8),
                ("wo", 1024), ("bo", 256)],
    "L2_xattn": [("wq", 2048), ("wk", 2048), ("wv", 2048), ("wo", 2048), ("bq", 8), ("bk", 8),
                 ("bv", 1024), ("bo", 256)],
    "L2_ffn": [("rms", 2), ("gate", 16), ("b1", 64), ("b2", 256)],
    "L3_attn": [("wq", 2048), ("wqr", 2048), ("wk", 2048), ("wkr", 2048), ("wv", 512), ("wo", 1024),
                ("cos", 512), ("sin", 512), ("bo", 256)],
    "L3_xattn": [("w", 512), ("b", 2), ("d", 2)],
    "L3_ffn": [("hash", 64), ("keys", 64), ("down", 4096), ("up", 4096), ("spread", 2048), ("scale", 1)],
}
CONSTS = [("ident", P), ("causal", BANK), ("den16", P), ("guard8", 1), ("guard6", 1), ("ones_k", 1), ("parts_q", 1), ("parts_k", 1), ("iota", 64), ("ones", P),
          ("half", 16), ("minus_half", 16), ("causal_cols", P)]
SUBLAYERS = list(WIDTHS)


def offsets(fields):
    at, out = 0, {}
    for name, width in fields:
        out[name] = (at, width)
        at += width
    return out, at


class Net:

    def __init__(self, nc, ctx):
        self.nc, self.ctx = nc, ctx
        self.banks = [[ctx.enter_context(nc.semaphore(f"sem_{half}_{i}")) for i in range(SEMS)] for half in range(2)]
        self.turn = 0
        self.tensors = 0
        self.psum = ctx.enter_context(nc.psum_tensor("psum", [P, BANKS, BANK], F32))

    def sbuf(self, name, shape, dt=F32, ctx=None):
        self.tensors += 1
        return (ctx or self.ctx).enter_context(self.nc.sbuf_tensor(f"{name}_{self.tensors}", shape, dt))

    @contextmanager
    def block(self):
        mine, other = self.banks[self.turn], self.banks[1 - self.turn]
        self.turn = 1 - self.turn
        free = iter(mine)
        with self.nc.Block() as block:
            @block.gpsimd
            def _(pool):
                pool.sem_clear(range(other[0].num, other[-1].num + 1))
            yield block, lambda signals: next(free)



class Product:

    def __init__(self, engine, rows, cols, mms, out, finish, split=None):
        self.engine, self.rows, self.cols, self.mms = engine, rows, cols, mms
        self.out, self.finish, self.split = out, finish, split


def summed(terms):
    n = len(terms)
    return [(None, a, b, i == 0, i == n - 1, False) for i, (a, b) in enumerate(terms)]


def turned(tiles, ident):
    return [(slice(i * P, i * P + t.shape[0]), t, ident[0:t.shape[0], 0:t.shape[0]], True, True, True)
            for i, t in enumerate(tiles)]


def finished(eng, p, ps):
    src = ps[0:p.rows, 0:p.cols]
    if p.split:
        src = src.rearrange("p (a b) -> p a b", a=p.split)
    kind, *args = p.finish
    if kind == "act":
        func, bias, scale = args
        kw = {} if bias is None else {"bias": bias}
        return eng.activation(p.out, src, func, scale=scale, **kw)
    if kind == "copy":
        return eng.tensor_copy(p.out, src)
    if kind == "scalar":
        s1, s2, op0, op1 = args
        return eng.tensor_scalar(p.out, src, s1, s2, op0, op1)
    if kind == "tensor":
        other, op = args
        return eng.tensor_tensor(p.out, src, other, op)
    scalar, other, op0, op1 = args
    return eng.scalar_tensor_tensor(out=p.out, in0=src, scalar=scalar, in1=other, op0=op0, op1=op1)


COPY = ("act", ACT.Copy, None, 1.0)
VCOPY = ("copy",)


def products(net, table, name="products"):
    owner = [p.engine for p in table]
    with net.block() as (block, sem):
        product_done, act_done, dve_done = sem("product"), sem("finished"), sem("finished")

        @block.tensor
        def _(pe):
            for n, p in enumerate(table):
                if n >= BANKS:
                    last = n - BANKS
                    pe.wait_ge(act_done if owner[last] == "act" else dve_done, owner[:last + 1].count(owner[last]))
                bank = net.psum[:, n % BANKS, :]
                for where, lhsT, rhs, start, stop, turn in p.mms:
                    dst = bank[0:p.rows, where] if where is not None else bank[0:p.rows, 0:p.cols]
                    if turn:
                        mm = pe.transpose(dst, lhsT, rhs)
                    else:
                        mm = pe.matmul(dst, lhsT, rhs, start=start, stop=stop)
                mm.then_inc(product_done, 1)

        @block.scalar
        def _(act):
            for n, p in enumerate(table):
                if p.engine == "act":
                    act.wait_ge(product_done, n + 1)
                    finished(act, p, net.psum[:, n % BANKS, :]).then_inc(act_done, 1)

        @block.vector
        def _(dve):
            done = 0
            for n, p in enumerate(table):
                if p.engine == "dve":
                    dve.wait_ge(product_done, n + 1)
                    if p.finish[0] == "stt" and done:
                        dve.wait_ge(dve_done, done)
                    finished(dve, p, net.psum[:, n % BANKS, :]).then_inc(dve_done, 1)
                    done += 1


def cols_out(engine, w, width, src, m, out, finish=COPY, rows=P, n=T, bias=None):
    chunks = src.shape[1]
    terms = [(w[:, k * width + m:k * width + m + rows], src[:, k, :]) for k in range(chunks)]
    return Product(engine, rows, n, summed(terms), out, finish)


def rows_out(engine, src, t, w, width, at, n, out, finish=COPY, bias=None, split=None):
    terms = [(src[:, k, t * P:(t + 1) * P], w[:, k * width + at:k * width + at + n]) for k in range(src.shape[1])]
    if bias is not None:
        row = bias[:, at:at + n]
        engine, finish = "dve", ("tensor", row.rearrange("p (a b) -> p a b", a=split) if split else row, ALU.add)
    return Product(engine, P, n, summed(terms), out, finish, split)



def layernorm(net, x, xn, xc, bias=None, fetch=None, need=None):
    with ExitStack() as ctx:
        stats = net.sbuf("stats", [P, NT, 6], ctx=ctx)
        mv = net.sbuf("mean_var", [P, NT, 2], ctx=ctx)
        rstd = net.sbuf("rstd", [P, NT], ctx=ctx)
        with net.block() as (block, sem):
            stats_done, mv_done, rstd_done = sem("stats"), sem("mean and variance"), sem("1/std")
            xn_done, turned_done, guarded = sem("normalised tile"), sem("transposed chunk"), sem("variance + eps")

            @block.gpsimd
            def _(pool):
                pool.wait_ge(mv_done, NT)
                pool.tensor_scalar(rstd[:, :], mv[:, :, 1], LN_EPS, None, ALU.add, ALU.bypass).then_inc(guarded, 1)
                pool.wait_ge(guarded, 1)
                pool.tensor_tensor(rstd[:, :], rstd[:, :], net.minus_half[:, 0:NT], ALU.pow).then_inc(rstd_done, 1)
                if bias is not None:
                    if need is not None:
                        pool.wait_ge(need[0], need[1])
                    pool.wait_ge(xn_done, NT)
                    pool.tensor_tensor(x[:, :, :], x[:, :, :], bias.unsqueeze(1).broadcast_to([P, NT, D]), ALU.add)

            @block.sync
            def _(sp):
                if fetch is not None:
                    sp.dma_start(fetch[1], fetch[2]).then_inc(fetch[0], 16)
                if need is not None:
                    sp.wait_ge(need[0], need[1])

            @block.vector
            def _(dve):
                for t in range(NT):
                    dve.bn_stats(stats[:, t, :], x[:, t, :]).then_inc(stats_done, 1)
                for t in range(NT):
                    dve.wait_ge(stats_done, t + 1)
                    dve.bn_aggr(mv[:, t, :], stats[:, t, :]).then_inc(mv_done, 1)
                dve.wait_ge(rstd_done, 1)
                for t in range(NT):
                    dve.tensor_scalar(xn[:, t, :], x[:, t, :], mv[:, t, 0:1], rstd[:, t:t + 1],
                                      ALU.subtract, ALU.mult).then_inc(xn_done, 1)
                dve.wait_ge(turned_done, 2)
                dve.tensor_copy(xc[:, 1, :], net.psum[:, 1, :])

            @block.tensor
            def _(pe):
                for c in range(NC):
                    for t in range(NT):
                        pe.wait_ge(xn_done, t + 1)
                        mm = pe.transpose(net.psum[:, c, t * P:(t + 1) * P], xn[:, t, c * P:(c + 1) * P], net.ident)
                    mm.then_inc(turned_done, 1)

            @block.scalar
            def _(act):
                act.wait_ge(turned_done, 1)
                act.activation(xc[:, 0, :], net.psum[:, 0, :], ACT.Copy)



def wide_attention(net, q, k, values, width, causal, finish, keep=None, gone=None):
    masked = causal or keep is not None
    with ExitStack() as ctx:
        probs = net.sbuf("probs", [P, 2, T], ctx=ctx)
        scores = net.sbuf("scores", [P, 2, T], ctx=ctx) if masked else None
        kept = net.sbuf("kept", [P, 2, T], ctx=ctx) if keep is not None else None
        probs_t = net.sbuf("probs_t", [P, 2, T], ctx=ctx)
        nmax = net.sbuf("nmax", [P, NT], ctx=ctx)
        total = net.sbuf("total", [P, NT], ctx=ctx)
        inverse = net.sbuf("inverse", [P, NT], ctx=ctx)
        span = [(t + 1) * P if causal else T for t in range(NT)]
        with net.block() as (block, sem):
            scores_done, kept_done, max_done, probs_done = sem("scores"), sem("kept"), sem("maximum"), sem("exp")
            turned_done, copied_done, out_done = sem("transposed"), sem("transpose copied"), sem("p @ v")
            inverse_done, tile_done = sem("1/sum"), sem("tile written")

            @block.tensor
            def _(pe):
                def score(t):
                    if t >= 2:
                        if masked:
                            pe.wait_ge(max_done, t - 1)
                        else:
                            pe.wait_ge(probs_done, t - 1)
                    for i, (a, b) in enumerate(zip(q, k)):
                        mm = pe.matmul(net.psum[:, t % 2, 0:span[t]], a[:, t * P:(t + 1) * P], b[:, 0:span[t]],
                                       start=i == 0, stop=i == len(q) - 1)
                    mm.then_inc(scores_done, 1)

                score(0)
                for t in range(NT):
                    if t + 1 < NT:
                        score(t + 1)
                    pe.wait_ge(probs_done, t + 1)
                    if t >= 2:
                        pe.wait_ge(copied_done, t - 1)
                    for c in range(span[t] // P):
                        mm = pe.transpose(net.psum[:, 2 + t % 2, c * P:(c + 1) * P],
                                          probs[:, t % 2, c * P:(c + 1) * P], net.ident)
                    mm.then_inc(turned_done, 1)
                    pe.wait_ge(copied_done, t + 1)
                    if t >= 2:
                        pe.wait_ge(tile_done, t - 1)
                    n = span[t] // P
                    for c in range(n):
                        mm = pe.matmul(net.psum[:, 4 + t % 2, 0:width], probs_t[:, t % 2, c * P:(c + 1) * P],
                                       values(c), start=c == 0, stop=c == n - 1)
                    mm.then_inc(out_done, 1)

            @block.vector
            def _(dve):
                def maximum(t):
                    dve.wait_ge(scores_done, t + 1)
                    src = net.psum[:, t % 2, 0:span[t]]
                    if not masked:
                        dve.tensor_reduce(nmax[:, t:t + 1], src, AX.X, ALU.max, negate=True).then_inc(max_done, 1)
                        return
                    if t >= 2:
                        dve.wait_ge(probs_done, t - 1)
                    if keep is not None:
                        dve.tensor_tensor(kept[:, t % 2, :], src, keep, ALU.mult).then_inc(kept_done, 1)
                        dve.wait_ge(kept_done, t + 1)
                        src, mask = kept[:, t % 2, :], gone
                    else:
                        mask = net.causal[:, BANK - span[t]:BANK]
                    dve.tensor_tensor_reduce(scores[:, t % 2, 0:span[t]], src, mask, -1.0, 3e38, ALU.add, ALU.min,
                                             nmax[:, t:t + 1]).then_inc(max_done, 1)

                maximum(0)
                for t in range(NT):
                    if t + 1 < NT:
                        maximum(t + 1)
                    dve.wait_ge(turned_done, t + 1)
                    if t >= 2:
                        dve.wait_ge(out_done, t - 1)
                    dve.tensor_copy(probs_t[:, t % 2, 0:span[t]], net.psum[:, 2 + t % 2, 0:span[t]])\
                       .then_inc(copied_done, 1)
                    dve.wait_ge(probs_done, t + 1)
                    dve.reciprocal(inverse[:, t:t + 1], total[:, t:t + 1]).then_inc(inverse_done, 1)
                    dve.wait_ge(inverse_done, t + 1)
                    dve.wait_ge(out_done, t + 1)
                    finish(dve, t, net.psum[:, 4 + t % 2, 0:width], inverse[:, t:t + 1]).then_inc(tile_done, 1)

            @block.scalar
            def _(act):
                for t in range(NT):
                    act.wait_ge(max_done, t + 1)
                    if t >= 2:
                        act.wait_ge(turned_done, t - 1)
                    src = scores[:, t % 2, 0:span[t]] if masked else net.psum[:, t % 2, 0:span[t]]
                    act.activation(probs[:, t % 2, 0:span[t]], src, ACT.Exp, bias=nmax[:, t:t + 1],
                                   scale=-1.0 if masked else 1.0, accum_out=total[:, t:t + 1]).then_inc(probs_done, 1)



def many_heads(net, passes, put_in, v, hd, o, pairs, scale, guard=None, causal=False, linear=False, mask_rows=None, mask_cols=None):
    packed = hd == HD
    future = causal and not linear
    cut = causal and linear
    lag = 2 if packed else 1
    turns = 1 if packed else 2
    at = SPARE
    tiles, steps = 2 * NT, NT
    width = hd + 1
    turn_bank = 7 if packed else 0

    with ExitStack() as ctx:
        if not linear:
            nmax = net.sbuf("nmax", [P, pairs, NT, 2], ctx=ctx)
            spread = net.sbuf("spread", [P, 2, turns, NT, P], ctx=ctx)
        if not packed:
            inverse = net.sbuf("inverse", [P, 2, NT], ctx=ctx)
        probs = net.sbuf("probs", [P, 2, 2, T], ctx=ctx)
        with net.block() as (block, sem):
            cleared, scores_done, max_done = sem("spread zeroed"), sem("scores"), sem("maximum")
            high_done, split_done = sem("high part of -max"), sem("low part of -max")
            turned_done, put_done = sem("-max transposed"), sem("-max in q")
            colscores_done, probs_done, cut_done = sem("transposed scores"), sem("exp"), sem("future cut off")
            pv_done, o_done = sem("p @ v of a step"), sem("output copied")
            sums_read, inverted = sem("sums kept above zero"), sem("1/sum")

            @block.gpsimd
            def _(pool):
                if not linear:
                    pool.memset(spread[:, :, :, :, :], 0.0).then_inc(cleared, 1)
                if cut:
                    for n in range(pairs * steps):
                        pool.wait_ge(probs_done, n + 1)
                        kt = n % steps
                        d = probs[:, n % 2, :, kt * P:(kt + 1) * P]
                        pool.affine_select(out=d, in_=d, compare_op=ALU.is_ge, fill=0.0, base=0,
                                           pattern=[[0, 2], [1, P]], channel_multiplier=-1).then_inc(cut_done, 1)

            @block.tensor
            def _(pe):
                def score(p, n):
                    qt, s = n // 2, p * tiles + n
                    if s >= 2:
                        pe.wait_ge(max_done, s - 1)
                    if not packed and p and n == 0:
                        pe.wait_ge(put_done, turns * p)
                    if not packed and p and n == 1:
                        pe.wait_ge(put_done, turns * p)
                    w = (qt + 1) * P if causal else T
                    bank = net.psum[:, n % 2, 0:w]
                    terms = passes(2 * p + n % 2)
                    last = len(terms) - 1
                    for i, (k, q) in enumerate(terms):
                        mm = pe.matmul(bank, q[:, qt * P:(qt + 1) * P], k[:, 0:w], start=i == 0,
                                       stop=i == last and mask_rows is None and not causal)
                    if mask_rows is not None:
                        mm = pe.matmul(bank, net.ident16, mask_rows[:, qt, :], start=False, stop=True)
                    if causal:
                        mm = pe.matmul(bank[:, qt * P:w], net.ident16, net.causal16, start=False, stop=True)
                    mm.then_inc(scores_done, 1)

                def put(p):
                    pe.wait_ge(split_done, p + 1)
                    if packed and p:
                        pe.wait_ge(put_done, p)
                    for i in range(turns):
                        for t in range(NT):
                            mm = pe.transpose(net.psum[:, turn_bank + i, t * P:(t + 1) * P], spread[:, p % 2, i, t, :],
                                              net.ident)
                        mm.then_inc(turned_done, 1)

                def col_scores(n):
                    p, kt = n // steps, n % steps
                    if not linear and kt == 0:
                        pe.wait_ge(put_done, turns * (p + 1))
                    if n >= 2:
                        pe.wait_ge(probs_done, n - 1)
                    lo = kt * P if causal else 0
                    for j in range(2):
                        bank = net.psum[:, 2 + 2 * (n % 2) + j, lo:T]
                        terms = passes(2 * p + j)
                        last = len(terms) - 1
                        for i, (k, q) in enumerate(terms):
                            mm = pe.matmul(bank, k[:, kt * P:(kt + 1) * P], q[:, lo:T], start=i == 0,
                                           stop=i == last and mask_cols is None and not future)
                        if future:
                            mm = pe.matmul(bank[:, 0:P], net.ident16, net.causal_cols16, start=False, stop=True)
                        if mask_cols is not None:
                            mm = pe.matmul(bank, net.ident16, mask_cols[:, kt, :], start=False, stop=True)
                    mm.then_inc(colscores_done, 1)

                def weigh(n):
                    p, kt = n // steps, n % steps
                    pe.wait_ge(cut_done if cut else probs_done, n + 1)
                    if packed and kt == 0 and p % 2 == 0 and p:
                        pe.wait_ge(o_done, p // 2)
                    if not packed and kt == 0 and p:
                        pe.wait_ge(o_done, 2 * p)
                    lo = kt * P if causal else 0
                    for j in range(2):
                        if packed:
                            u = (2 * p + j) % 4
                            mm = pe.matmul(net.psum[u * PITCH:(u + 1) * PITCH, 6, lo:T], v(kt, 2 * p + j), probs[:, n % 2, j, lo:T],
                                           start=kt == 0, stop=kt == steps - 1, tile_position=(0, u * PITCH))
                        else:
                            for t in range(NT):
                                mm = pe.matmul(net.psum[:, 6 + j, t * width:(t + 1) * width], probs[:, n % 2, j, t * P:(t + 1) * P],
                                               v(kt, 2 * p + j), start=kt == 0 and t == 0, stop=kt == steps - 1 and t == NT - 1)
                    mm.then_inc(pv_done, 1)

                if linear:
                    for n in range(pairs * steps):
                        col_scores(n)
                        if n:
                            weigh(n - 1)
                else:
                    for p in range(pairs + lag):
                        for i in range(steps):
                            if p >= lag:
                                col_scores((p - lag) * steps + i)
                                if (p - lag) * steps + i:
                                    weigh((p - lag) * steps + i - 1)
                            if p < pairs:
                                score(p, 2 * i)
                                score(p, 2 * i + 1)
                            if packed and 1 <= p <= pairs and i == 0:
                                put(p - 1)
                        if not packed and p < pairs:
                            put(p)
                weigh(pairs * steps - 1)

            @block.vector
            def _(dve):
                def maximum(p, n):
                    qt, s = n // 2, p * tiles + n
                    w = (qt + 1) * P if causal else T
                    dve.wait_ge(scores_done, s + 1)
                    dve.tensor_reduce(nmax[:, p, qt, n % 2:n % 2 + 1], net.psum[:, n % 2, 0:w], AX.X, ALU.max,
                                      negate=True).then_inc(max_done, 1)

                def split(p):
                    dve.wait_ge(max_done, tiles * (p + 1))
                    m = nmax[:, p, :, :]
                    if not packed:
                        dve.tensor_scalar(m, m, 1e20, None, ALU.min).then_inc(high_done, 1)
                        dve.wait_ge(high_done, 3 * p + 1)
                    if p >= 2:
                        dve.wait_ge(turned_done, turns * (p - 1))
                    if packed:
                        both = spread[:, p % 2, 0, :, :].rearrange("p t (j c) -> p t j c", j=2)
                        dve.tensor_copy(both[:, :, :, at].bitcast(F32R), m).then_inc(high_done, 1)
                        dve.wait_ge(high_done, p + 1)
                        dve.tensor_tensor(both[:, :, :, at + 1], m, both[:, :, :, at], ALU.subtract).then_inc(split_done, 1)
                        return
                    for j in range(2):
                        c = (1 - j) * hd
                        dve.tensor_copy(spread[:, p % 2, j, :, c].bitcast(F32R), m[:, :, j]).then_inc(high_done, 1)
                    dve.wait_ge(high_done, 3 * (p + 1))
                    for j in range(2):
                        c = (1 - j) * hd
                        ins = dve.tensor_tensor(spread[:, p % 2, j, :, c + 1], m[:, :, j], spread[:, p % 2, j, :, c], ALU.subtract)
                    ins.then_inc(split_done, 1)

                def put(p):
                    for i in range(turns):
                        dve.wait_ge(turned_done, turns * p + i + 1)
                        tile, where = put_in(p * turns + i)
                        dve.tensor_tensor(tile[where, :], tile[where, :].bitcast(F32), net.psum[where, turn_bank + i, :],
                                          ALU.add).then_inc(put_done, 1)

                def copy_out(p):
                    dve.wait_ge(pv_done, steps * (p + 1))
                    if packed:
                        if guard is None:
                            ins = dve.tensor_copy(o[:, p // 2, :], net.psum[:, 6, :])
                        else:
                            ins = dve.tensor_scalar(o[:, p // 2, :], net.psum[:, 6, :], guard, None, ALU.add)
                        ins.then_inc(o_done, 1)
                    else:
                        if p:
                            dve.wait_ge(o_done, 2 * p)
                        out = net.psum[:, 6:8, 0:NT * width].rearrange("p j (t d) -> p j t d", t=NT)
                        dve.tensor_scalar(inverse[:, :, :], out[:, :, :, hd], 1e-30, None, ALU.max).then_inc(sums_read, 1)
                        dve.wait_ge(sums_read, p + 1)
                        dve.reciprocal(inverse[:, :, :], inverse[:, :, :]).then_inc(inverted, 1)
                        dve.wait_ge(inverted, p + 1)
                        for j in range(2):
                            dve.tensor_tensor(o[:, :, 2 * p + j, :], out[:, j, :, 0:hd],
                                              inverse[:, j, :].unsqueeze(2).broadcast_to([P, NT, hd]), ALU.mult).then_inc(o_done, 1)

                if linear:
                    for p in range(1, pairs - 1, 2):
                        copy_out(p)
                else:
                    dve.wait_ge(cleared, 1)
                    for p in range(pairs + lag):
                        for n in range(tiles):
                            if p < pairs:
                                maximum(p, n)
                            if packed and n == 1 and p >= lag + 2 and (p - lag) % 2 == 0:
                                copy_out(p - lag - 1)
                            if not packed and n == 1 and p >= lag + 1:
                                copy_out(p - lag - 1)
                            if packed and n == 3 and 1 <= p <= pairs:
                                put(p - 1)
                        if p < pairs:
                            split(p)
                            if not packed:
                                put(p)
                copy_out(pairs - 1)

            @block.scalar
            def _(act):
                for n in range(pairs * steps):
                    kt = n % steps
                    lo = kt * P if causal else 0
                    act.wait_ge(colscores_done, n + 1)
                    if n >= 2:
                        act.wait_ge(pv_done, n - 1)
                    act.activation(probs[:, n % 2, :, lo:T], net.psum[:, 2 + 2 * (n % 2):4 + 2 * (n % 2), lo:T],
                                   ACT.Copy if linear else ACT.Exp, scale=scale).then_inc(probs_done, 1)


def stack_parts(net, jobs, aug):
    rope = jobs[0][1] is not None
    square = jobs[0][2] is not None
    with ExitStack() as ctx:
        high = net.sbuf("high", [P, 2, T], F32R, ctx=ctx)
        value = net.sbuf("value", [P, 2, T], ctx=ctx)
        rotated = net.sbuf("rotated", [P, 2, T], ctx=ctx) if rope else None
        with net.block() as (block, sem):
            product_done, value_done, high_done, parts_done = sem("product"), sem("value"), sem("high"), sem("parts")
            cos_done, sin_done = sem("times cosine"), sem("times sine")

            @block.tensor
            def _(pe):
                for n, (terms, turned_terms, sq, is_k, dst) in enumerate(jobs):
                    if n >= 4:
                        pe.wait_ge(parts_done, n - 3)
                    for which, group in enumerate((terms, turned_terms)):
                        if group is None:
                            continue
                        for where, lhsT, rhs, start, stop, turn in group:
                            bank = net.psum[:, 2 * (n % 4) + which, :]
                            if turn:
                                mm = pe.transpose(bank[:, where], lhsT, rhs)
                            else:
                                mm = pe.matmul(bank, lhsT, rhs, start=start, stop=stop)
                    mm.then_inc(product_done, 1)

            def source(n):
                return value[:, n % 2, :] if rope or square else net.psum[:, 2 * (n % 4), :]

            @block.gpsimd
            def _(pool):
                if rope:
                    for n in range(len(jobs)):
                        pool.wait_ge(cos_done, n + 1)
                        pool.wait_ge(sin_done, n + 1)
                        pool.tensor_tensor(value[:, n % 2, :], value[:, n % 2, :], rotated[:, n % 2, :], ALU.add)\
                            .then_inc(value_done, 1)

            @block.scalar
            def _(act):
                for n, (terms, turned_terms, sq, is_k, dst) in enumerate(jobs):
                    if n >= 2:
                        act.wait_ge(parts_done, n - 1)
                    if square:
                        act.wait_ge(product_done, n + 1)
                        act.activation(value[:, n % 2, :], net.psum[:, 2 * (n % 4), :], ACT.Square, bias=sq[1], scale=sq[0])\
                           .then_inc(value_done, 1)
                    act.wait_ge(value_done if rope or square else product_done, n + 1)
                    kw = {"bias": aug["ones"]} if is_k else {}
                    act.activation(high[:, n % 2, :], source(n), ACT.Identity, **kw).then_inc(high_done, 1)

            @block.vector
            def _(dve):
                def times(n):
                    dve.wait_ge(product_done, n + 1)
                    if n >= 2:
                        dve.wait_ge(parts_done, n - 1)
                    dve.tensor_tensor(value[:, n % 2, :], net.psum[:, 2 * (n % 4), :], rope_cos, ALU.mult).then_inc(cos_done, 1)
                    dve.tensor_tensor(rotated[:, n % 2, :], net.psum[:, 2 * (n % 4) + 1, :], rope_sin, ALU.mult)\
                       .then_inc(sin_done, 1)
                rope_cos, rope_sin = aug["cos"], aug["sin"]
                if rope:
                    times(0)
                for n, (terms, turned_terms, sq, is_k, dst) in enumerate(jobs):
                    if rope and n + 1 < len(jobs):
                        times(n + 1)
                    dve.wait_ge(high_done, n + 1)
                    sign = aug["k"] if is_k else aug["q"]
                    src, h = source(n), high[:, n % 2, :].bitcast(F32)
                    for i, (where, out) in enumerate(dst):
                        ins = dve.scalar_tensor_tensor(out=out, in0=h[where, :], scalar=sign[where, :], in1=src[where, :],
                                                       op0=ALU.mult, op1=ALU.add)
                    ins.then_inc(parts_done, 1)


def normalise(net, o):
    with ExitStack() as ctx:
        inv = net.sbuf("inv", [P, GROUPS, T], ctx=ctx)
        with net.block() as (block, sem):
            sums_done, inverse_done = sem("sums on their heads' partitions"), sem("1/sum")

            @block.tensor
            def _(pe):
                for c in range(GROUPS):
                    pe.matmul(net.psum[:, c, :], net.den16, o[:, c, :], start=True, stop=True).then_inc(sums_done, 1)

            @block.vector
            def _(dve):
                for c in range(GROUPS):
                    dve.wait_ge(sums_done, c + 1)
                    dve.reciprocal(inv[:, c, :], net.psum[:, c, :]).then_inc(inverse_done, 1)

            @block.gpsimd
            def _(pool):
                for c in range(GROUPS):
                    pool.wait_ge(inverse_done, c + 1)
                    pool.tensor_tensor(o[:, c, :], o[:, c, :], inv[:, c, :], ALU.mult)


def add_output(net, x, src, chunks, rows, w):
    table = []
    for t in range(NT):
        terms = [(src[0:rows, c, t * P:(t + 1) * P], w[0:rows, c * D:(c + 1) * D]) for c in range(chunks)]
        table.append(Product("dve", P, D, summed(terms), x[:, t, :], ("tensor", x[:, t, :], ALU.add)))
    products(net, table)


def alternate(n):
    return "dve" if n % 2 else "act"


def copied(engine):
    return COPY if engine == "act" else VCOPY



def narrow_attention(net, W, x, qsrc, ksrc, scale, causal, guard, linear=False, jobs=None, before=None, vbias=None, vwidth=D, vat=0):
    with ExitStack() as ctx:
        qs = net.sbuf("qs", [P, PAIRS, T], F32R, ctx=ctx)
        ks = net.sbuf("ks", [P, H, T], F32R, ctx=ctx)
        v = net.sbuf("v", [P, NT, H, PITCH], ctx=ctx)
        with net.block() as (block, sem):
            zeroed = sem("zeroed")

            @block.gpsimd
            def _(pool):
                pool.memset(v[:, :, :, :], 0.0).then_inc(zeroed, 1)
                for j in range(2):
                    pool.wait_ge(zeroed, j + 1)
                    empty = slice((1 - j) * STACK, (2 - j) * STACK)
                    pool.memset(ks[empty, j:H:2, :].bitcast(F32), 0.0).then_inc(zeroed, 1)
                pool.wait_ge(zeroed, 3)
                pool.memset(v[:, :, :, HD:HD + 1], 1.0)
        wv = W["wqkv"] if vat else W["wv"]
        products(net, [rows_out(alternate(t), ksrc, t, wv, vwidth, vat, D, v[:, t, :, 0:HD], copied(alternate(t)), vbias,
                                split=H) for t in range(NT)])
        if jobs is None:
            def jobs(j, p, _):
                w, src = (W["wk"], ksrc) if j else (W["wq"], qsrc)
                return stacked_terms(w, src, p), None, None
        halves = [slice(j * STACK, (j + 1) * STACK) for j in range(2)]
        with ExitStack() as stacking:
            fourfold = net.sbuf("fourfold", [P, NT, H, 4, HD], ctx=stacking) if before is not None else None
            tables = [[(*jobs(0, p, fourfold), False, [(slice(0, P), qs[:, p, :])]) for p in range(PAIRS)],
                      [(*jobs(1, p, fourfold), True, [(half, ks[half, 2 * p + j, :]) for j, half in enumerate(halves)])
                       for p in range(PAIRS)]]
            if before is None:
                tables = [tables[0] + tables[1]]
            for j, table in enumerate(tables):
                if before is not None:
                    before(j, fourfold)
                stack_parts(net, table, dict(ones=net.ones_k, q=net.parts_q, k=net.parts_k, cos=W.get("cos"),
                                             sin=W.get("sin")))
        o = net.sbuf("o", [P, GROUPS, T], ctx=ctx)
        many_heads(net, lambda h: [(ks[:, h, :], qs[:, h // 2, :])], lambda i: (qs[:, i, :], slice(0, P)),
                   lambda kt, h: v[:, kt, h, :], HD, o, PAIRS, scale, guard=guard, causal=causal, linear=linear)
        normalise(net, o)
        add_output(net, x, o, GROUPS, P, W["wo"])


def stacked_terms(w, src, p):
    width = H * STACK
    return summed([(w[:, c * width + p * P:c * width + (p + 1) * P], src[:, c, :]) for c in range(NC)])


def L0_attn(net, W, x, xn, xc, **_):
    with ExitStack() as ctx:
        q = net.sbuf("q", [P, NC, T], ctx=ctx)
        k = net.sbuf("k", [P, NC, T], ctx=ctx)
        v = net.sbuf("v", [P, NT, D], ctx=ctx)
        tmp = net.sbuf("tmp", [P, 8, T], ctx=ctx)
        table = []
        for i, (dst, w) in enumerate(((q, W["wq"]), (k, W["wk"]))):
            for c in range(NC):
                for j, tab in enumerate((W["cos"], W["sin"])):
                    table.append(cols_out("dve", w, D, xc, c * P, tmp[:, 4 * i + 2 * c + j, :], ("tensor", tab, ALU.mult)))
        table += [rows_out("act", xc, t, W["wv"], D, 0, D, v[:, t, :]) for t in range(NT)]
        products(net, table)
        with net.block() as (block, sem):
            rotated = sem("rotated")

            @block.vector
            def _(dve):
                for i, dst in enumerate((q, k)):
                    a = tmp[:, 4 * i:4 * i + 4, :]
                    dve.tensor_tensor(dst[:, 0, :], a[:, 0, :], a[:, 3, :], ALU.subtract).then_inc(rotated, 1)
                    dve.tensor_tensor(dst[:, 1, :], a[:, 1, :], a[:, 2, :], ALU.add).then_inc(rotated, 1)

            @block.scalar
            def _(act):
                act.wait_ge(rotated, 2)
                act.activation(q[:, :, :], q[:, :, :], ACT.Copy, scale=D ** -0.5)

        def finish(dve, t, ps, inverse):
            return dve.scalar_tensor_tensor(out=x[:, t, :], in0=ps, scalar=inverse, in1=x[:, t, :],
                                            op0=ALU.mult, op1=ALU.add)
        wide_attention(net, [q[:, c, :] for c in range(NC)], [k[:, c, :] for c in range(NC)],
                       lambda c: v[:, c, :], D, True, finish)


def L0_xattn(net, W, x, xn, xc, cc, **_):
    narrow_attention(net, W, x, xc, cc, D ** -0.5, False, None)


def L0_ffn(net, W, x, xn, xc, **_):
    with ExitStack() as ctx:
        sb = lambda name, shape, dt=F32: net.sbuf(name, shape, dt, ctx=ctx)
        gate = sb("gate", [P, NT, MIX])
        xsq, ssum = sb("xsq", [P, D]), sb("ssum", [P, NT])
        simsq, simn, siminv = sb("simsq", [P, 2 * MIX]), sb("simn", [P, 2 * MIX]), sb("siminv", [P, MIX])
        sig, raw, logit = sb("sig", [P, MIX]), sb("raw", [P, NT, MIX]), sb("logit", [P, NT, MIX])
        g, a, e = sb("g", [P, NT, MIX]), sb("a", [P, NT, MIX]), sb("e", [P, NT, MIX])
        top, index, indexf = sb("top", [P, NT, 8]), sb("index", [P, NT, 8], U32), sb("indexf", [P, NT, 8])
        anyon, mx, tot = sb("anyon", [P, NT]), sb("mx", [P, NT]), sb("tot", [P, NT])
        fb, fb2 = sb("fb", [P, NT, MIX]), sb("fb2", [P, NT, MIX])
        with net.block() as (block, sem):
            step, colsum_done, sim_done, raw_done, exped, sig_done = (sem("step"), sem("column sums"), sem("similarity"),
                                                                      sem("products"), sem("exp"), sem("sigmoid"))

            floor_done, root_done = sem("sums of squares kept above zero"), sem("1/norms")

            @block.gpsimd
            def _(pool):
                pool.wait_ge(floor_done, 1)
                pool.tensor_tensor(siminv[:, :], siminv[:, :], net.minus_half, ALU.pow).then_inc(root_done, 1)
                pool.tensor_tensor(ssum[:, :], ssum[:, :], net.minus_half[:, 0:NT], ALU.pow).then_inc(root_done, 1)

            @block.scalar
            def _(act):
                act.activation(sig[:, :], W["gates"], ACT.Sigmoid).then_inc(sig_done, 1)
                act.wait_ge(exped, 1)
                act.activation(e[:, :, :], e[:, :, :], ACT.Exp).then_inc(exped, 1)

            @block.tensor
            def _(pe):
                pe.wait_ge(step, 1)
                for c in range(NC):
                    mm = pe.matmul(net.psum[:, 0, 0:MIX], net.ones_pp, simsq[:, c * MIX:(c + 1) * MIX], start=c == 0, stop=c == 1)
                mm.then_inc(colsum_done, 1)
                pe.wait_ge(sim_done, 1)
                for t in range(NT):
                    for c in range(NC):
                        mm = pe.matmul(net.psum[:, 1, t * MIX:(t + 1) * MIX], xc[:, c, t * P:(t + 1) * P],
                                       simn[:, c * MIX:(c + 1) * MIX], start=c == 0, stop=c == 1)
                mm.then_inc(raw_done, 1)

            @block.vector
            def _(dve):
                n = 0

                def then(ins):
                    nonlocal n
                    n += 1
                    ins.then_inc(step, 1)
                    dve.wait_ge(step, n)

                then(dve.tensor_tensor(simsq[:, :], W["sim"], W["sim"], ALU.mult))
                for t in range(NT):
                    then(dve.tensor_tensor_reduce(xsq[:, :], xn[:, t, :], xn[:, t, :], 1.0, 0.0, ALU.mult, ALU.add,
                                                  ssum[:, t:t + 1]))
                then(dve.tensor_scalar(ssum[:, :], ssum[:, :], 1e-24, None, ALU.max))
                dve.wait_ge(colsum_done, 1)
                dve.tensor_scalar(siminv[:, :], net.psum[:, 0, 0:MIX], 1e-24, None, ALU.max).then_inc(floor_done, 1)
                dve.wait_ge(root_done, 2)
                for c in range(NC):
                    ins = dve.tensor_tensor(simn[:, c * MIX:(c + 1) * MIX], W["sim"][:, c * MIX:(c + 1) * MIX],
                                            siminv[:, :], ALU.mult)
                    if c == 0:
                        then(ins)
                ins.then_inc(sim_done, 1)
                dve.wait_ge(raw_done, 1)
                then(dve.tensor_tensor(raw[:, :, :], net.psum[:, 1, 0:NT * MIX].rearrange("p (t e) -> p t e", t=NT),
                                       ssum[:, :].unsqueeze(2).broadcast_to([P, NT, MIX]), ALU.mult))
                dve.wait_ge(sig_done, 1)
                then(dve.tensor_tensor(logit[:, :, :], raw[:, :, :],
                                       sig[:, :].unsqueeze(1).broadcast_to([P, NT, MIX]), ALU.subtract))
                then(dve.tensor_scalar(g[:, :, :], logit[:, :, :], 0.0, None, ALU.max))
                then(dve.tensor_scalar(a[:, :, :], logit[:, :, :], 0.0, None, ALU.is_gt))
                then(dve.tensor_reduce(anyon[:, :], a[:, :, :], AX.X, ALU.max))
                then(dve.tensor_reduce(mx[:, :], g[:, :, :], AX.X, ALU.max))
                for t in range(NT):
                    then(dve.max(top[:, t, :], logit[:, t, :]))
                    then(dve.max_index(index[:, t, :], top[:, t, :], logit[:, t, :]))
                then(dve.tensor_copy(indexf[:, :, :], index[:, :, :]))
                for dst, i in ((fb, 0), (fb2, 1)):
                    then(dve.tensor_tensor(dst[:, :, :], net.iota[:, 0:MIX].unsqueeze(1).broadcast_to([P, NT, MIX]),
                                           indexf[:, :, i:i + 1].broadcast_to([P, NT, MIX]), ALU.is_equal))
                then(dve.tensor_tensor(fb[:, :, :], fb[:, :, :], fb2[:, :, :], ALU.add))
                then(dve.tensor_scalar(anyon[:, :], anyon[:, :], -1.0, 1.0, ALU.mult, ALU.add))
                then(dve.tensor_tensor(fb[:, :, :], fb[:, :, :], anyon[:, :].unsqueeze(2).broadcast_to([P, NT, MIX]), ALU.mult))
                then(dve.tensor_tensor(a[:, :, :], a[:, :, :], fb[:, :, :], ALU.add))
                dve.tensor_tensor(e[:, :, :], g[:, :, :], mx[:, :].unsqueeze(2).broadcast_to([P, NT, MIX]),
                                  ALU.subtract).then_inc(exped, 1)
                dve.wait_ge(exped, 2)
                then(dve.tensor_tensor(e[:, :, :], e[:, :, :], a[:, :, :], ALU.mult))
                then(dve.tensor_reduce(tot[:, :], e[:, :, :], AX.X, ALU.add))
                then(dve.reciprocal(tot[:, :], tot[:, :]))
                then(dve.tensor_tensor(gate[:, :, :], e[:, :, :], tot[:, :].unsqueeze(2).broadcast_to([P, NT, MIX]), ALU.mult))

        qkv = sb("qkv", [P, NT, 3, MIXD])
        weighed = sb("weighed", [P, 2, MIX, MIXD])
        half = MIX // 2
        with net.block() as (block, sem):
            product_done, weighed_done, summed_done = sem("products"), sem("weighed"), sem("summed")
            jobs = [(t, j) for t in range(NT) for j in range(3)]

            @block.tensor
            def _(pe):
                for n, (t, j) in enumerate(jobs):
                    if n >= 4:
                        pe.wait_ge(weighed_done, 2 * (n - 3))
                    for h in range(2):
                        for c in range(NC):
                            at = c * MIX * MIXD + h * half * MIXD
                            mm = pe.matmul(net.psum[:, 2 * (n % 4) + h, :], xc[:, c, t * P:(t + 1) * P],
                                           W["qkv"[j]][:, at:at + half * MIXD], start=c == 0, stop=c == 1)
                        mm.then_inc(product_done, 1)

            @block.vector
            def _(dve):
                for n, (t, j) in enumerate(jobs):
                    for h in range(2):
                        dve.wait_ge(product_done, 2 * n + h + 1)
                        dve.tensor_tensor(weighed[:, n % 2, h * half:(h + 1) * half, :],
                                          net.psum[:, 2 * (n % 4) + h, :].rearrange("p (e d) -> p e d", d=MIXD),
                                          gate[:, t, h * half:(h + 1) * half].unsqueeze(2).broadcast_to([P, half, MIXD]),
                                          ALU.mult).then_inc(weighed_done, 1)
                    dve.wait_ge(weighed_done, 2 * n + 2)
                    dve.tensor_reduce(qkv[:, t, j, :], weighed[:, n % 2, :, :].rearrange("p e d -> p d e"), AX.X, ALU.add)\
                       .then_inc(summed_done, 1)
        qk = sb("qk", [MIXD, 2, T])
        products(net, [Product("act", MIXD, T, turned([qkv[:, t, j, :] for t in range(NT)], net.ident), qk[:, j, :],
                               ("act", ACT.Copy, None, MIXD ** -0.5 if j == 0 else 1.0)) for j in range(2)])
        attn = sb("attn", [P, NT, MIXD])

        def finish(dve, t, ps, inverse):
            return dve.tensor_scalar(attn[:, t, :], ps, inverse, None, ALU.mult)
        wide_attention(net, [qk[:, 0, :]], [qk[:, 1, :]], lambda c: qkv[:, c, 2, :], MIXD, True, finish)
        mixed = sb("mixed", [P, 2, MIX, MIXD])
        mixed_c = sb("mixed_c", [P, 8, T])
        with net.block() as (block, sem):
            mixed_done, turned_done, copied_done = sem("mixed"), sem("transposed"), sem("copied")

            @block.vector
            def _(dve):
                for t in range(NT):
                    if t >= 2:
                        dve.wait_ge(turned_done, 2 * (t - 1))
                    dve.tensor_tensor(mixed[:, t % 2, :, :], attn[:, t, :].unsqueeze(1).broadcast_to([P, MIX, MIXD]),
                                      gate[:, t, :].unsqueeze(2).broadcast_to([P, MIX, MIXD]), ALU.mult).then_inc(mixed_done, 1)

            @block.tensor
            def _(pe):
                for t in range(NT):
                    pe.wait_ge(mixed_done, t + 1)
                    flat = mixed[:, t % 2, :, :].rearrange("p e d -> p (e d)")
                    for h in range(2):
                        for c in range(4):
                            mm = pe.transpose(net.psum[:, 2 * t + h, c * P:(c + 1) * P],
                                              flat[:, (4 * h + c) * P:(4 * h + c + 1) * P], net.ident)
                        mm.then_inc(turned_done, 1)

            @block.scalar
            def _(act):
                for t in range(NT):
                    for h in range(2):
                        act.wait_ge(turned_done, 2 * t + h + 1)
                        act.activation(mixed_c[:, 4 * h:4 * h + 4, t * P:(t + 1) * P],
                                       net.psum[:, 2 * t + h, :].rearrange("p (c n) -> p c n", c=4), ACT.Copy)\
                           .then_inc(copied_done, 1)
        add_output(net, x, mixed_c, 8, P, W["o"])


def L1_attn(net, W, x, xn, xc, **_):
    narrow_attention(net, W, x, xc, xc, HD ** -0.5, True, net.guard8)


def L1_xattn(net, W, x, xn, xc, cc, **_):
    with ExitStack() as ctx:
        q = net.sbuf("q", [P, NC, T], ctx=ctx)
        k = net.sbuf("k", [P, NC, T], ctx=ctx)
        v = net.sbuf("v", [P, NT, D], ctx=ctx)
        o = net.sbuf("o", [P, NC, D, 2], ctx=ctx)
        table = []
        for c in range(NC):
            table.append(cols_out("dve", W["wq"], D, xc, c * P, q[:, c, :], ("scalar", W["bq"][:, c:c + 1], D ** -0.5, ALU.add, ALU.mult)))
            table.append(cols_out("act", W["wk"], D, cc, c * P, k[:, c, :], ("act", ACT.Identity, W["bk"][:, c:c + 1], 1.0)))
        table += [rows_out(alternate(t), cc, t, W["wv"], D, 0, D, v[:, t, :], copied(alternate(t)), W["bv"]) for t in range(NT)]
        products(net, table)

        def finish(dve, t, ps, inverse):
            return dve.tensor_scalar(o[:, t % 2, :, t // 2], ps, inverse, None, ALU.mult)
        wide_attention(net, [q[:, c, :] for c in range(NC)], [k[:, c, :] for c in range(NC)],
                       lambda c: v[:, c, :], D, False, finish)
        add_output(net, x, o[:, :, :, :].rearrange("p c f r -> p c (f r)"), NC, P, W["wo"])


def ternary(net, W):
    with ExitStack() as ctx:
        part = net.sbuf("part", [P, 2], ctx=ctx)
        gamma = net.sbuf("gamma", [P, 2], ctx=ctx)
        edge = net.sbuf("edge", [P, 2, 2], ctx=ctx)
        low = net.sbuf("low", [P, F * D // P], ctx=ctx)
        with net.block() as (block, sem):
            step, sum_done = sem("step"), sem("sum over partitions")

            @block.tensor
            def _(pe):
                pe.wait_ge(step, 2)
                pe.matmul(net.psum[:, 0, 0:2], net.ones_pp, part[:, :], start=True, stop=True).then_inc(sum_done, 1)

            @block.vector
            def _(dve):
                n = 0

                def then(ins):
                    nonlocal n
                    n += 1
                    ins.then_inc(step, 1)
                    dve.wait_ge(step, n)
                for i, w in enumerate((W["fc"], W["proj"])):
                    then(dve.tensor_reduce(part[:, i:i + 1], w, AX.X, ALU.add, apply_absolute_value=True))
                dve.wait_ge(sum_done, 1)
                then(dve.tensor_scalar(gamma[:, :], net.psum[:, 0, 0:2], 1.0 / (F * D), 1e-6, ALU.mult, ALU.add))
                then(dve.tensor_scalar(edge[:, 0, :], gamma[:, :], 0.5, None, ALU.mult))
                then(dve.tensor_scalar(edge[:, 1, :], gamma[:, :], -0.5, None, ALU.mult))
                for i, w in enumerate((W["fc"], W["proj"])):
                    then(dve.tensor_scalar(low[:, :], w, edge[:, 1, i:i + 1], None, ALU.is_lt))
                    then(dve.scalar_tensor_tensor(out=w, in0=w, scalar=edge[:, 0, i:i + 1], in1=low[:, :],
                                                  op0=ALU.is_gt, op1=ALU.subtract))


def L1_ffn(net, W, x, xn, xc, **_):
    ternary(net, W)
    with ExitStack() as ctx:
        h = net.sbuf("h", [P, NT, F], ctx=ctx)
        hc = net.sbuf("hc", [P, F // P, T], ctx=ctx)
        table = []
        for t in range(NT):
            for half in range(2):
                table.append(rows_out("act", xc, t, W["fc"], F, half * BANK, BANK, h[:, t, half * BANK:(half + 1) * BANK],
                                      ("act", ACT.Gelu, None, 1.0)))
        products(net, table)
        stats = net.sbuf("stats", [P, NT, 2, 6], ctx=ctx)
        mv = net.sbuf("mean_var", [P, NT, 2], ctx=ctx)
        rstd = net.sbuf("rstd", [P, NT], ctx=ctx)
        with net.block() as (block, sem):
            stats_done, mv_done, rstd_done, guarded = sem("stats"), sem("mean and variance"), sem("1/std"), sem("variance + eps")

            @block.gpsimd
            def _(pool):
                pool.wait_ge(mv_done, NT)
                pool.tensor_scalar(rstd[:, :], mv[:, :, 1], LN_EPS, None, ALU.add, ALU.bypass).then_inc(guarded, 1)
                pool.wait_ge(guarded, 1)
                pool.tensor_tensor(rstd[:, :], rstd[:, :], net.minus_half[:, 0:NT], ALU.pow).then_inc(rstd_done, 1)

            @block.vector
            def _(dve):
                for t in range(NT):
                    for half in range(2):
                        dve.bn_stats(stats[:, t, half, :], h[:, t, half * BANK:(half + 1) * BANK]).then_inc(stats_done, 1)
                for t in range(NT):
                    dve.wait_ge(stats_done, 2 * t + 2)
                    dve.bn_aggr(mv[:, t, :], stats[:, t, :, :].rearrange("p a b -> p (a b)")).then_inc(mv_done, 1)
                dve.wait_ge(rstd_done, 1)
                for t in range(NT):
                    dve.tensor_scalar(h[:, t, :], h[:, t, :], mv[:, t, 0:1], rstd[:, t:t + 1], ALU.subtract, ALU.mult)
        table = []
        for c in range(F // P):
            w, b = W["ln_w"][:, c:c + 1], W["ln_b"][:, c:c + 1]
            fin = ("act", ACT.Identity, b, w) if c % 2 == 0 else ("scalar", w, b, ALU.mult, ALU.add)
            table.append(Product(alternate(c), P, T, turned([h[:, t, c * P:(c + 1) * P] for t in range(NT)], net.ident),
                                 hc[:, c, :], fin))
        products(net, table)
        add_output(net, x, hc, F // P, P, W["proj"])


def L2_attn(net, W, x, xn, xc, **_):
    with ExitStack() as ctx:
        wide = net.sbuf("wide", [P, NT, 2, D], ctx=ctx)
        stats = net.sbuf("stats", [P, NT, 2, 6], ctx=ctx)
        mv = net.sbuf("mean_var", [P, NT, 2, 2], ctx=ctx)
        rstd = net.sbuf("rstd", [P, NT, 2], ctx=ctx)
        products(net, [rows_out(alternate(t), xc, t, W["wqkv"], 3 * D, 0, 2 * D, wide[:, t, :, :].rearrange("p a b -> p (a b)"),
                                copied(alternate(t)), W["bqkv"]) for t in range(NT)])
        with net.block() as (block, sem):
            stats_done, mv_done, rstd_done, scaled = sem("stats"), sem("mean and variance"), sem("1/std"), sem("variance scaled")

            @block.gpsimd
            def _(pool):
                pool.wait_ge(mv_done, 2 * NT)
                pool.tensor_scalar(rstd[:, :, :], mv[:, :, :, 1], D / (D - 1), None, ALU.mult, ALU.bypass).then_inc(scaled, 1)
                pool.wait_ge(scaled, 1)
                pool.tensor_tensor(rstd[:, :, :], rstd[:, :, :], net.half[:, 0:2 * NT].rearrange("p (t j) -> p t j", j=2),
                                   ALU.pow).then_inc(rstd_done, 1)

            @block.vector
            def _(dve):
                for t in range(NT):
                    for j in range(2):
                        dve.bn_stats(stats[:, t, j, :], wide[:, t, j, :]).then_inc(stats_done, 1)
                for t in range(NT):
                    for j in range(2):
                        dve.wait_ge(stats_done, 2 * t + j + 1)
                        dve.bn_aggr(mv[:, t, j, :], stats[:, t, j, :]).then_inc(mv_done, 1)
                dve.wait_ge(rstd_done, 1)
                dve.tensor_scalar(rstd[:, :, :], rstd[:, :, :], 1e-6, None, ALU.add).then_inc(rstd_done, 1)
                dve.wait_ge(rstd_done, 2)
                dve.reciprocal(rstd[:, :, :], rstd[:, :, :]).then_inc(rstd_done, 1)
                dve.wait_ge(rstd_done, 3)

        def spread(j, fourfold):
            with net.block() as (block, sem):
                @block.vector
                def _(dve):
                    for t in range(NT):
                        dve.tensor_scalar(fourfold[:, t, :, :, :], wide[:, t, j, :].rearrange("p (h d) -> p h d", h=H)
                                          .unsqueeze(2).broadcast_to([P, H, 4, HD]),
                                          mv[:, t, j, 0:1], rstd[:, t, j:j + 1], ALU.subtract, ALU.mult)

        def jobs(j, p, fourfold):
            gain, offset = (W["gk"], W["hk"]) if j else (W["gq"], W["hq"])
            cols = [(slice(t * P, (t + 1) * P), fourfold[:, t, 2 * p:2 * p + 2, :, :].rearrange("p h r d -> p (h r d)"),
                     net.ident, True, True, True) for t in range(NT)]
            return cols, None, (gain[:, p:p + 1], offset[:, p:p + 1])
        narrow_attention(net, W, x, xc, xc, 1.0, True, net.guard6, linear=True, jobs=jobs, before=spread, vbias=W["bqkv"],
                         vwidth=3 * D, vat=2 * D)


def L2_xattn(net, W, x, xn, xc, cc, mask, mask_t, b, **_):
    with ExitStack() as ctx:
        sb = lambda name, shape, dt=F32: net.sbuf(name, shape, dt, ctx=ctx)
        mrows, mcols = sb("mrows", [P, NT, T], BF16), sb("mcols", [P, NT, T], BF16)
        qa, ka = sb("qa", [P, 4, T], F32R), sb("ka", [P, 4, T], F32R)
        qb, kb = sb("qb", [P, 4, T], F32R), sb("kb", [P, 4, T], F32R)
        v, o = sb("v", [P, NT, 4, DK + 1]), sb("o", [P, NT, H, DK])
        low, up = slice(0, DK), slice(DK, P)
        with net.block() as (block, sem):
            zeroed = sem("zeroed")

            @block.gpsimd
            def _(pool):
                pool.memset(v[:, :, :, DK:DK + 1], 1.0)

            @block.vector
            def _(dve):
                for j, extra in enumerate((up, low)):
                    dve.memset(kb[extra, j:4:2, :].bitcast(F32), 0.0).then_inc(zeroed, 1)
                for j, extra in enumerate((up, low)):
                    dve.wait_ge(zeroed, j + 1)
                    dve.memset(kb[extra.start:extra.start + 2, j:4:2, :].bitcast(F32), 1.0)
        for four in range(4):
            with ExitStack() as inner:
                raw = net.sbuf("raw", [P, 2, NT, T], I32, ctx=inner) if four == 0 else None
                with net.block() as (block, sem):
                    product_done, loaded, zeroed = sem("product"), sem("mask"), sem("partitions for -max zeroed")
                    high_done = sem("a head's high part")

                    if four == 0:
                        @block.sync
                        def _(sp):
                            for i, source in enumerate((mask, mask_t)):
                                sp.dma_start(raw[:, i, :, :], source[b].rearrange("(t p) k -> p t k", p=P)).then_inc(loaded, 16)

                    @block.gpsimd
                    def _(pool):
                        for j, extra in enumerate((up, low)):
                            pool.memset(qb[extra, j:4:2, :].bitcast(F32), 0.0).then_inc(zeroed, 1)
                        if four == 0:
                            pool.wait_ge(loaded, 32)
                            for i, to in enumerate((mrows, mcols)):
                                pool.wait_ge(zeroed, 2 + i)
                                pool.tensor_scalar(to[:, :, :], raw[:, i, :, :], 0, MASKED, ALU.is_equal, ALU.mult)\
                                    .then_inc(zeroed, 1)

                    @block.tensor
                    def _(pe):
                        for n in range(4):
                            p, is_k = 2 * four + n // 2, n % 2
                            w, src = (W["wk"], cc) if is_k else (W["wq"], xc)
                            for c in range(NC):
                                at = c * F + p * P
                                mm = pe.matmul(net.psum[:, n, :], w[:, at:at + P], src[:, c, :], start=c == 0, stop=c == 1)
                            mm.then_inc(product_done, 1)

                    @block.scalar
                    def _(act):
                        for n in range(4):
                            is_k = n % 2
                            bias = (W["bk"] if is_k else W["bq"])[:, 2 * four + n // 2:2 * four + n // 2 + 1]
                            act.wait_ge(product_done, n + 1)
                            for j, (own, other) in enumerate(((low, up), (up, low))):
                                u = 2 * (n // 2) + j
                                if is_k:
                                    act.activation(ka[other, u, :], net.psum[own, n, :], ACT.Identity, bias=bias[own, :])
                                act.activation((ka if is_k else qb)[own, u, :], net.psum[own, n, :], ACT.Identity,
                                               bias=bias[own, :]).then_inc(high_done, 1)

                    @block.vector
                    def _(dve):
                        for n in range(4):
                            is_k = n % 2
                            bias = (W["bk"] if is_k else W["bq"])[:, 2 * four + n // 2:2 * four + n // 2 + 1]
                            dve.wait_ge(product_done, n + 1)
                            for j, (own, other) in enumerate(((low, up), (up, low))):
                                u = 2 * (n // 2) + j
                                high, to = (ka, kb[own, u, :]) if is_k else (qb, qa[other, u, :])
                                dve.wait_ge(high_done, 2 * n + j + 1)
                                dve.scalar_tensor_tensor(out=to, in0=net.psum[own, n, :], scalar=bias[own, :],
                                                         in1=high[own, u, :].bitcast(F32), op0=ALU.add, op1=ALU.subtract)
                                if not is_k:
                                    dve.tensor_copy(qa[own, u, :], qb[own, u, :].bitcast(F32))
            products(net, [rows_out(alternate(t), cc, t, W["wv"], F, four * D, D, v[:, t, :, 0:DK], copied(alternate(t)),
                                    W["bv"], split=4) for t in range(NT)])
            many_heads(net, lambda h: [(ka[:, h, :], qa[:, h, :]), (kb[:, h, :], qb[:, h, :])],
                       lambda i: (qb[:, i, :], low if i % 2 else up), lambda kt, u: v[:, kt, u, :], DK,
                       o[:, :, 4 * four:4 * four + 4, :], 2, DK ** -0.5, mask_rows=mrows, mask_cols=mcols)
        flat = o[:, :, :, :].rearrange("p t h d -> p t (h d)")
        oc = sb("oc", [P, F // P, T])
        products(net, [Product(alternate(c), P, T, turned([flat[:, t, c * P:(c + 1) * P] for t in range(NT)], net.ident),
                               oc[:, c, :], copied(alternate(c))) for c in range(F // P)])
        add_output(net, x, oc, F // P, P, W["wo"])


def L2_ffn(net, W, x, xn, xc, w1, w2, arena, **_):
    with ExitStack() as ctx:
        sb = lambda name, shape, dt=F32: net.sbuf(name, shape, dt, ctx=ctx)
        xr, xrc = sb("xr", [P, NT, D]), sb("xrc", [P, NC, T])
        sq, ms = sb("sq", [P, D]), sb("ms", [P, NT])
        logit, top, index, indexf = sb("logit", [P, NT, 8]), sb("top", [P, NT, 8]), sb("index", [P, NT, 8], U32), sb("indexf", [P, NT])
        e, tot, gate, gate_c = sb("e", [P, NT, 8]), sb("tot", [P, NT]), sb("gate", [P, NT, 8]), sb("gate_c", [EXPERTS, T])
        with net.block() as (block, sem):
            step, mean_done, root_done = sem("step"), sem("mean square"), sem("1/root")

            @block.gpsimd
            def _(pool):
                pool.wait_ge(mean_done, 1)
                pool.tensor_tensor(ms[:, :], ms[:, :], net.minus_half[:, 0:NT], ALU.pow).then_inc(root_done, 1)

            @block.vector
            def _(dve):
                n = 0

                def then(ins):
                    nonlocal n
                    n += 1
                    ins.then_inc(step, 1)
                    dve.wait_ge(step, n)
                for t in range(NT):
                    then(dve.tensor_tensor_reduce(sq[:, :], xn[:, t, :], xn[:, t, :], 1.0, 0.0, ALU.mult, ALU.add, ms[:, t:t + 1]))
                dve.tensor_scalar(ms[:, :], ms[:, :], 1.0 / D, 1e-6, ALU.mult, ALU.add).then_inc(mean_done, 1)
                dve.wait_ge(root_done, 1)
                for t in range(NT):
                    then(dve.tensor_scalar(xr[:, t, :], xn[:, t, :], ms[:, t:t + 1], None, ALU.mult))
        products(net, [Product("dve", P, T, turned([xr[:, t, c * P:(c + 1) * P] for t in range(NT)], net.ident), xrc[:, c, :],
                               ("scalar", W["rms"][:, c:c + 1], None, ALU.mult, ALU.bypass)) for c in range(NC)])
        products(net, [rows_out("dve", xrc, t, W["gate"], 8, 0, 8, logit[:, t, :], VCOPY) for t in range(NT)])
        with net.block() as (block, sem):
            step, shifted, exped, ready, turned_done = (sem("step"), sem("logits - max"), sem("exp"), sem("gates"),
                                                        sem("gates transposed"))

            @block.vector
            def _(dve):
                n = 0

                def then(ins):
                    nonlocal n
                    n += 1
                    ins.then_inc(step, 1)
                    dve.wait_ge(step, n)
                for t in range(NT):
                    then(dve.max(top[:, t, :], logit[:, t, :]))
                    then(dve.max_index(index[:, t, :], top[:, t, :], logit[:, t, :]))
                dve.tensor_tensor(e[:, :, :], logit[:, :, :], top[:, :, 0:1].broadcast_to([P, NT, 8]),
                                  ALU.subtract).then_inc(shifted, 1)
                then(dve.tensor_copy(indexf[:, :], index[:, :, 0]))
                dve.wait_ge(exped, 1)
                then(dve.tensor_reduce(tot[:, :], e[:, :, :], AX.X, ALU.add))
                then(dve.reciprocal(tot[:, :], tot[:, :]))
                then(dve.tensor_tensor(gate[:, :, :], net.iota[:, 0:8].unsqueeze(1).broadcast_to([P, NT, 8]),
                                       indexf[:, :].unsqueeze(2).broadcast_to([P, NT, 8]), ALU.is_equal))
                dve.tensor_tensor(gate[:, :, :], gate[:, :, :], tot[:, :].unsqueeze(2).broadcast_to([P, NT, 8]), ALU.mult)\
                   .then_inc(ready, 1)
                dve.wait_ge(turned_done, 1)
                dve.tensor_copy(gate_c[:, :], net.psum[0:EXPERTS, 0, :])

            @block.scalar
            def _(act):
                act.wait_ge(shifted, 1)
                act.activation(e[:, :, :], e[:, :, :], ACT.Exp).then_inc(exped, 1)

            @block.tensor
            def _(pe):
                pe.wait_ge(ready, 1)
                for t in range(NT):
                    mm = pe.transpose(net.psum[0:EXPERTS, 0, t * P:(t + 1) * P], gate[:, t, :], net.ident)
                mm.then_inc(turned_done, 1)
        products(net, [Product("dve", P, D, summed([(gate_c[:, t * P:(t + 1) * P], W["b2"][0:EXPERTS, :])]), x[:, t, :],
                               ("tensor", x[:, t, :], ALU.add)) for t in range(NT)])
        hidden = sb("hidden", [P, 2, HIDDEN_CHUNKS, T])
        base = ARENA - 8192
        slot = [arena[:, base + 4096 * i:base + 4096 * (i + 1)] for i in range(2)]
        with net.block() as (block, sem):
            loaded = [sem("expert's weights in slot 0"), sem("expert's weights in slot 1")]
            up_done, act_done, down_done, added = sem("up product"), sem("silu"), sem("down product"), sem("added to x")

            @block.sync
            def _(sp):
                for n in range(EXPERTS):
                    if n >= 2:
                        sp.wait_ge(down_done, NT * (n - 1))
                    sp.dma_start(slot[n % 2][:, 0:2048], w1[n]).then_inc(loaded[n % 2], 16)
                    sp.dma_start(slot[n % 2][:, 2048:4096], w2[n]).then_inc(loaded[n % 2], 16)

            @block.tensor
            def _(pe):
                def up(n):
                    pe.wait_ge(loaded[n % 2], 32 * (n // 2 + 1))
                    for f in range(HIDDEN_CHUNKS):
                        m = n * HIDDEN_CHUNKS + f
                        if m >= 4:
                            pe.wait_ge(act_done, m - 3)
                        for c in range(NC):
                            at = c * F + f * P
                            mm = pe.matmul(net.psum[:, m % 4, :], slot[n % 2][:, at:at + P], xrc[:, c, :],
                                           start=c == 0, stop=c == 1)
                        mm.then_inc(up_done, 1)

                def down(n):
                    pe.wait_ge(act_done, HIDDEN_CHUNKS * (n + 1))
                    for t in range(NT):
                        m = n * NT + t
                        if m >= 4:
                            pe.wait_ge(added, m - 3)
                        for f in range(HIDDEN_CHUNKS):
                            at = 2048 + f * D
                            mm = pe.matmul(net.psum[:, 4 + m % 4, 0:D], hidden[:, n % 2, f, t * P:(t + 1) * P],
                                           slot[n % 2][:, at:at + D], start=f == 0, stop=f == HIDDEN_CHUNKS - 1)
                        mm.then_inc(down_done, 1)
                up(0)
                for n in range(EXPERTS):
                    if n + 1 < EXPERTS:
                        up(n + 1)
                    down(n)

            @block.scalar
            def _(act):
                for n in range(EXPERTS):
                    if n >= 2:
                        act.wait_ge(down_done, NT * (n - 1))
                    for f in range(HIDDEN_CHUNKS):
                        m = n * HIDDEN_CHUNKS + f
                        act.wait_ge(up_done, m + 1)
                        act.activation(hidden[:, n % 2, f, :], net.psum[:, m % 4, :], ACT.Silu,
                                       bias=W["b1"][:, m:m + 1]).then_inc(act_done, 1)

            @block.vector
            def _(dve):
                for n in range(EXPERTS):
                    for t in range(NT):
                        m = n * NT + t
                        dve.wait_ge(down_done, m + 1)
                        if m >= NT:
                            dve.wait_ge(added, m - NT + 1)
                        dve.scalar_tensor_tensor(out=x[:, t, :], in0=net.psum[:, 4 + m % 4, 0:D], scalar=gate[:, t, n:n + 1],
                                                 in1=x[:, t, :], op0=ALU.mult, op1=ALU.add).then_inc(added, 1)


def L3_attn(net, W, x, xn, xc, **_):
    def jobs(j, p, _):
        w, wr = (W["wk"], W["wkr"]) if j else (W["wq"], W["wqr"])
        return stacked_terms(w, xc, p), stacked_terms(wr, xc, p), None
    narrow_attention(net, W, x, xc, xc, HD ** -0.5, True, None, jobs=jobs)


def L3_xattn(net, W, x, xn, xc, ct, cc, kmask, b, **_):
    with ExitStack() as ctx:
        sb = lambda name, shape, dt=F32: net.sbuf(name, shape, dt, ctx=ctx)
        q, k = sb("q", [P, NC, T]), sb("k", [P, NC, T])
        raw, keep, gone = sb("raw", [P, T // 4], I32), sb("keep", [P, T]), sb("gone", [P, T])
        table = []
        for c in range(NC):
            table.append(cols_out("act", W["w"], D, xc, c * P, q[:, c, :], ("act", ACT.Relu, W["b"][:, c:c + 1], 1.0)))
            table.append(cols_out("dve", W["w"], D, cc, c * P, k[:, c, :], ("scalar", W["b"][:, c:c + 1], 0.0, ALU.add, ALU.max)))
        products(net, table)
        with net.block() as (block, sem):
            loaded = sem("mask")

            @block.sync
            def _(sp):
                sp.dma_start(raw[:, :], kmask[b].partition_broadcast(P)).then_inc(loaded, 16)

            @block.vector
            def _(dve):
                for c in range(NC):
                    dve.tensor_scalar(k[:, c, :], k[:, c, :], W["d"][:, c:c + 1], None, ALU.mult)
                dve.wait_ge(loaded, 16)
                dve.tensor_scalar(keep[:, :], raw[:, :].bitcast(U8), 0, None, ALU.is_equal)
                dve.tensor_scalar(gone[:, :], raw[:, :].bitcast(U8), 0, MASKED, ALU.not_equal, ALU.mult)

        def finish(dve, t, ps, inverse):
            return dve.scalar_tensor_tensor(out=x[:, t, :], in0=ps, scalar=inverse, in1=x[:, t, :],
                                            op0=ALU.mult, op1=ALU.add)
        wide_attention(net, [q[:, c, :] for c in range(NC)], [k[:, c, :] for c in range(NC)],
                       lambda c: ct[:, c, :], D, False, finish, keep=keep[:, :], gone=gone[:, :])


def L3_ffn(net, W, x, xn, xc, **_):
    with ExitStack() as ctx:
        sb = lambda name, shape, dt=F32: net.sbuf(name, shape, dt, ctx=ctx)
        hc, sim = sb("hc", [SLOTD, 1, T]), sb("sim", [P, NT, SLOTS])
        top, index, indexf = sb("top", [P, NT, 8]), sb("index", [P, NT, 8], U32), sb("indexf", [P, NT, 8])
        e, tot, gate, hit = sb("e", [P, NT, 4]), sb("tot", [P, NT]), sb("gate", [P, NT, SLOTS]), sb("hit", [P, NT, SLOTS])
        gate_c = sb("gate_c", [SLOTS, T])
        products(net, [Product("act", SLOTD, T, summed([(W["hash"][:, c * SLOTD:(c + 1) * SLOTD], xc[:, c, :]) for c in range(NC)]),
                               hc[:, 0, :], COPY)])
        products(net, [Product("act", P, SLOTS, summed([(hc[:, 0, t * P:(t + 1) * P], W["keys"][0:SLOTD, :])]), sim[:, t, :], COPY)
                       for t in range(NT)])
        with net.block() as (block, sem):
            step, shifted, exped, ready, turned_done = (sem("step"), sem("values - max"), sem("exp"), sem("gates"),
                                                        sem("gates transposed"))

            @block.vector
            def _(dve):
                n = 0

                def then(ins):
                    nonlocal n
                    n += 1
                    ins.then_inc(step, 1)
                    dve.wait_ge(step, n)
                for t in range(NT):
                    then(dve.max(top[:, t, :], sim[:, t, :]))
                    then(dve.max_index(index[:, t, :], top[:, t, :], sim[:, t, :]))
                dve.tensor_tensor(e[:, :, :], top[:, :, 0:4], top[:, :, 0:1].broadcast_to([P, NT, 4]),
                                  ALU.subtract).then_inc(shifted, 1)
                then(dve.tensor_copy(indexf[:, :, :], index[:, :, :]))
                dve.wait_ge(exped, 1)
                then(dve.tensor_reduce(tot[:, :], e[:, :, :], AX.X, ALU.add))
                then(dve.reciprocal(tot[:, :], tot[:, :]))
                then(dve.tensor_tensor(e[:, :, :], e[:, :, :], tot[:, :].unsqueeze(2).broadcast_to([P, NT, 4]), ALU.mult))
                iota = net.iota[:, :].unsqueeze(1).broadcast_to([P, NT, SLOTS])
                for i in range(4):
                    dst = gate if i == 0 else hit
                    then(dve.tensor_tensor(dst[:, :, :], iota, indexf[:, :, i:i + 1].broadcast_to([P, NT, SLOTS]), ALU.is_equal))
                    then(dve.tensor_tensor(dst[:, :, :], dst[:, :, :], e[:, :, i:i + 1].broadcast_to([P, NT, SLOTS]), ALU.mult))
                    if i:
                        ins = dve.tensor_tensor(gate[:, :, :], gate[:, :, :], hit[:, :, :], ALU.add)
                        if i < 3:
                            then(ins)
                ins.then_inc(ready, 1)
                dve.wait_ge(turned_done, 1)
                dve.tensor_copy(gate_c[:, :], net.psum[0:SLOTS, 0, :])

            @block.scalar
            def _(act):
                act.wait_ge(shifted, 1)
                act.activation(e[:, :, :], e[:, :, :], ACT.Exp).then_inc(exped, 1)

            @block.tensor
            def _(pe):
                pe.wait_ge(ready, 1)
                for t in range(NT):
                    mm = pe.transpose(net.psum[0:SLOTS, 0, t * P:(t + 1) * P], gate[:, t, :], net.ident)
                mm.then_inc(turned_done, 1)
        silu = sb("silu", [P, 2, T])
        proj = sb("proj", [P, SLOTS * SLOTD // P, T])
        chunks = SLOTS * SLOTD // P
        with net.block() as (block, sem):
            down_done, spread_done, silu_done, weighed = sem("down product"), sem("gates spread"), sem("silu"), sem("weighed")

            @block.tensor
            def _(pe):
                for n in range(chunks):
                    if n >= 2:
                        pe.wait_ge(weighed, n - 1)
                    for c in range(NC):
                        at = c * SLOTS * SLOTD + n * P
                        mm = pe.matmul(net.psum[:, n % 2, :], W["down"][:, at:at + P], xc[:, c, :], start=c == 0, stop=c == 1)
                    mm.then_inc(down_done, 1)
                    pe.matmul(net.psum[:, 2 + n % 2, :], W["spread"][0:SLOTS, n * P:(n + 1) * P], gate_c[:, :],
                              start=True, stop=True).then_inc(spread_done, 1)

            @block.scalar
            def _(act):
                for n in range(chunks):
                    act.wait_ge(down_done, n + 1)
                    if n >= 2:
                        act.wait_ge(weighed, n - 1)
                    act.activation(silu[:, n % 2, :], net.psum[:, n % 2, :], ACT.Silu).then_inc(silu_done, 1)

            @block.vector
            def _(dve):
                for n in range(chunks):
                    dve.wait_ge(silu_done, n + 1)
                    dve.wait_ge(spread_done, n + 1)
                    dve.tensor_tensor(proj[:, n, :], silu[:, n % 2, :], net.psum[:, 2 + n % 2, :], ALU.mult).then_inc(weighed, 1)
        out = sb("out", [P, NT, D])
        table = []
        for t in range(NT):
            terms = [(proj[:, c, t * P:(t + 1) * P], W["up"][:, c * D:(c + 1) * D]) for c in range(chunks)]
            table.append(Product("dve", P, D, summed(terms), out[:, t, :], ("stt", W["scale"], xn[:, t, :], ALU.mult, ALU.add)))
        products(net, table)
        with net.block() as (block, sem):
            @block.vector
            def _(dve):
                dve.tensor_tensor(x[:, :, :], x[:, :, :], out[:, :, :], ALU.add)


BODIES = dict(L0_attn=L0_attn, L0_xattn=L0_xattn, L0_ffn=L0_ffn, L1_attn=L1_attn, L1_xattn=L1_xattn, L1_ffn=L1_ffn,
              L2_attn=L2_attn, L2_xattn=L2_xattn, L2_ffn=L2_ffn, L3_attn=L3_attn, L3_xattn=L3_xattn, L3_ffn=L3_ffn)


def decoder(nc, x_d, ctx_d, mask_d, mask_t_d, kmask_d, w1_d, w2_d, consts_d, packs_d, out_d, batches=B, sublayers=SUBLAYERS):
    with ExitStack() as ctx:
        net = Net(nc, ctx)
        spots, width = offsets(CONSTS)
        consts = net.sbuf("consts", [P, width])
        (net.ident, net.causal, net.den16, net.guard8, net.guard6, net.ones_k, net.parts_q, net.parts_k, net.iota, net.ones, net.half, net.minus_half,
         net.causal_cols) = (consts[:, at:at + n] for at, n in spots.values())
        net.ones_pp = net.ones
        narrow = net.sbuf("narrow", [P, 3, P], BF16)
        net.ident16, net.causal16, net.causal_cols16 = (narrow[:, i, :] for i in range(3))
        arenas = [net.sbuf("arena0", [P, ARENA]), net.sbuf("arena1", [P, ARENA])]
        x, xn, xc = net.sbuf("x", [P, NT, D]), net.sbuf("xn", [P, NT, D]), net.sbuf("xc", [P, NC, T])
        ct, cc = net.sbuf("ct", [P, NT, D]), net.sbuf("cc", [P, NC, T])
        with net.block() as (block, sem):
            loaded = sem("constants")

            @block.sync
            def _(sp):
                sp.dma_start(consts[:, :], consts_d).then_inc(loaded, 16)
                sp.wait_ge(loaded, 16)

            @block.vector
            def _(dve):
                dve.wait_ge(loaded, 16)
                dve.tensor_copy(net.ident16, net.ident)
                dve.tensor_copy(net.causal16, net.causal[:, BANK - P:BANK])
                dve.tensor_copy(net.causal_cols16, net.causal_cols)
        first, first_loaded = packs_d[sublayers[0]], ctx.enter_context(nc.semaphore("first_weights_loaded"))
        loaded = [ctx.enter_context(nc.semaphore(f"weights_loaded_{i}")) for i in range(2)]
        with net.block() as (block, sem):
            @block.sync
            def _(sp):
                sp.dma_start(arenas[0][:, 0:first.shape[1]], first).then_inc(first_loaded, 16)
        blocks_start = net.turn
        with nc.Fori(0, batches) as b:
            with net.block() as (block, sem):
                x_loaded, ctx_loaded = sem("x"), sem("context")

                @block.sync
                def _(sp):
                    sp.dma_start(x[:, :, :], x_d[b].rearrange("(t p) d -> p t d", p=P)).then_inc(x_loaded, 16)
                    sp.dma_start(ct[:, :, :], ctx_d[b].rearrange("(t p) d -> p t d", p=P)).then_inc(ctx_loaded, 16)
                    sp.wait_ge(first_loaded, 16)
                    sp.wait_ge(x_loaded, 16)
                    sp.wait_ge(ctx_loaded, 16)
            with net.block() as (block, sem):
                @block.gpsimd
                def _(pool):
                    pool.sem_clear(range(first_loaded.num, loaded[-1].num + 1))
            products(net, [Product(alternate(c), P, T, turned([ct[:, t, c * P:(c + 1) * P] for t in range(NT)], net.ident),
                                   cc[:, c, :], copied(alternate(c))) for c in range(NC)])
            for s, name in enumerate(sublayers):
                arena = arenas[s % 2]
                W = {field: arena[:, at:at + n] for field, (at, n) in offsets(WIDTHS[name])[0].items()}
                if s + 1 < len(sublayers):
                    nxt, signal = packs_d[sublayers[s + 1]], loaded[(s + 1) % 2]
                else:
                    nxt, signal = first, first_loaded
                layernorm(net, x, xn, xc, W.get("bo"), fetch=(signal, arenas[(s + 1) % 2][:, 0:nxt.shape[1]], nxt),
                          need=(loaded[s % 2], 16 * ((s + 1) // 2)) if s else None)
                BODIES[name](net, W, x=x, xn=xn, xc=xc, ct=ct, cc=cc, mask=mask_d, mask_t=mask_t_d, kmask=kmask_d,
                             w1=w1_d, w2=w2_d, arena=arena, b=b)
            with net.block() as (block, sem):
                stored = sem("output")

                @block.sync
                def _(sp):
                    sp.dma_start(out_d[b].rearrange("(t p) d -> p t d", p=P), x[:, :, :]).then_inc(stored, 16)
                    sp.wait_ge(stored, 16)
            if net.turn != blocks_start:
                with net.block() as (block, sem):
                    pass
        with net.block() as (block, sem):
            @block.sync
            def _(sp):
                sp.wait_ge(first_loaded, 16)



def by_chunk(w):
    k, n = w.shape
    return w.reshape(k // P, P, n).transpose(1, 0, 2).reshape(P, -1)


def on_rows(a, rows=P):
    out = np.zeros((P, a.shape[-1]), np.float32)
    out[:a.shape[0]] = a
    return out


def on_every_row(a):
    return np.tile(a[None], (P, 1))


def apart(w):
    out = np.zeros((w.shape[0], H, PITCH), np.float32)
    out[:, :, :HD] = w.reshape(w.shape[0], H, HD)
    return out.reshape(w.shape[0], H * PITCH)


def thrice(w):
    out = np.zeros((w.shape[0], H, 4, HD), np.float32)
    out[:, :, :3] = w.reshape(w.shape[0], H, 1, HD)
    return out.reshape(w.shape[0], H * STACK)


def apart_rows(w):
    return np.ascontiguousarray(apart(np.ascontiguousarray(w.T)).T)


def blocks_of(w):
    out = np.zeros((H, HD, H, HD), np.float32)
    for h in range(H):
        out[h, :, h, :] = w
    return out.reshape(D, D)


def by_head(w):
    out = np.zeros((HD, H, HD, H), np.float32)
    for h in range(H):
        out[:, h, :, h] = w[:, :, h]
    return out.reshape(D, D)


def pack(i):
    f32 = np.float32
    evens = np.r_[0:D:2, 1:D:2]
    half = D // 2
    inv = (1.0 / 10000.0 ** (np.arange(half, dtype=f32) / f32(half))).astype(f32)
    ang = (np.arange(T, dtype=f32)[None, :] * inv[:, None]).astype(f32)
    inv3 = (1.0 / 10000.0 ** (np.arange(0, HD, 2, dtype=f32) / f32(HD))).astype(f32)
    ang3 = np.repeat((np.arange(T, dtype=f32)[None, :] * inv3[:, None]).astype(f32), 2, axis=0)
    sign = np.tile(np.array([-1.0, 1.0], f32), HD // 2)[:, None]
    cos3, sin3 = np.zeros((2, 4, HD, T), f32), np.zeros((2, 4, HD, T), f32)
    cos3[:, :3], sin3[:, :3] = np.cos(ang3), np.sin(ang3) * sign
    swap = np.arange(D).reshape(-1, 2)[:, ::-1].reshape(-1)
    qkv3 = i["L3_attn_Wqkv"]
    cols = lambda v: np.ascontiguousarray(v.reshape(-1, P).T)
    heads = lambda v: np.ascontiguousarray(thrice(v.reshape(1, D)).reshape(PAIRS, P).T)
    spread = np.zeros((SLOTS, SLOTS * SLOTD), f32)
    for s in range(SLOTS):
        spread[s, s * SLOTD:(s + 1) * SLOTD] = 1.0
    packs = {
        "L0_attn": dict(wq=by_chunk(by_head(i["L0_attn_w_q"])[:, evens]), wk=by_chunk(by_head(i["L0_attn_w_k"])[:, evens]),
                        wv=by_chunk(by_head(i["L0_attn_w_v"])), cos=np.cos(ang), sin=np.sin(ang)),
        "L0_xattn": dict(wq=by_chunk(thrice(blocks_of(i["L0_xattn_Wq"].T))), wk=by_chunk(thrice(blocks_of(i["L0_xattn_Wk"].T))),
                         wv=by_chunk(blocks_of(i["L0_xattn_Wv"].T)), wo=by_chunk(apart_rows(i["L0_xattn_Wo"].T)),
                         bo=on_every_row(i["L0_xattn_bo"])),
        "L0_ffn": dict(sim=by_chunk(i["L0_ffn_sim_matrix"]), gates=np.tile(i["L0_ffn_gates"][None], (P, 1)),
                       **{j: by_chunk(i[f"L0_ffn_{j}_proj"].transpose(1, 0, 2).reshape(D, MIX * MIXD)) for j in "qkv"},
                       o=by_chunk(i["L0_ffn_o_proj"].reshape(MIX * MIXD, D))),
        "L1_attn": dict(wq=by_chunk(thrice(i["L1_attn_Wq"].T)), wk=by_chunk(thrice(i["L1_attn_Wkv"][:D].T)),
                        wv=by_chunk(i["L1_attn_Wkv"][D:].T), wo=by_chunk(apart_rows(i["L1_attn_Wo"].T))),
        "L1_xattn": dict(**{f"w{j}": by_chunk(i[f"L1_xattn_W{j}"]) for j in "qkvo"}, bq=cols(i["L1_xattn_bq"]),
                         bk=cols(i["L1_xattn_bk"]), bv=on_every_row(i["L1_xattn_bv"]), bo=on_every_row(i["L1_xattn_bo"])),
        "L1_ffn": dict(fc=by_chunk(i["L1_ffn_W_fc"].T), proj=by_chunk(i["L1_ffn_W_proj"].T), ln_w=cols(i["L1_ffn_ln_w"]),
                       ln_b=cols(i["L1_ffn_ln_b"])),
        "L2_attn": dict(wqkv=by_chunk(i["L2_attn_Wqkv"]), bqkv=on_every_row(i["L2_attn_bqkv"]), gq=heads(i["L2_attn_gamma_q"]),
                        hq=heads(i["L2_attn_beta_q"]), gk=heads(i["L2_attn_gamma_k"]), hk=heads(i["L2_attn_beta_k"]),
                        wo=by_chunk(apart_rows(i["L2_attn_Wo"])), bo=on_every_row(i["L2_attn_bo"])),
        "L2_xattn": dict(wq=by_chunk(i["L2_xattn_Wq"].T), wk=by_chunk(i["L2_xattn_Wk"].T), wv=by_chunk(i["L2_xattn_Wv"].T),
                         wo=by_chunk(i["L2_xattn_Wo"].T),
                         bq=cols(i["L2_xattn_bq"]), bk=cols(i["L2_xattn_bk"]), bv=on_every_row(i["L2_xattn_bv"]),
                         bo=on_every_row(i["L2_xattn_bo"])),
        "L2_ffn": dict(rms=cols(i["L2_ffn_rms_w"]), gate=by_chunk(i["L2_ffn_gate_w"].T),
                       b1=np.ascontiguousarray(i["L2_ffn_b1"].reshape(EXPERTS * HIDDEN_CHUNKS, P).T), b2=on_rows(i["L2_ffn_b2"])),
        "L3_attn": dict(wq=by_chunk(thrice(qkv3[:, :D])), wqr=by_chunk(thrice(qkv3[:, :D][:, swap])),
                        wk=by_chunk(thrice(qkv3[:, D:2 * D])), wkr=by_chunk(thrice(qkv3[:, D:2 * D][:, swap])),
                        wv=by_chunk(qkv3[:, 2 * D:]), wo=by_chunk(apart_rows(i["L3_attn_Wout"])),
                        cos=cos3.reshape(P, T), sin=sin3.reshape(P, T), bo=on_every_row(i["L3_attn_bout"])),
        "L3_xattn": dict(w=by_chunk(i["L3_xattn_W"].T), b=cols(i["L3_xattn_b"]), d=cols(i["L3_xattn_D"][0])),
        "L3_ffn": dict(hash=by_chunk(i["L3_ffn_hasher_w"].T), keys=on_rows(i["L3_ffn_keys"].T),
                       down=by_chunk(i["L3_ffn_values_down"].transpose(1, 0, 2).reshape(D, SLOTS * SLOTD)),
                       up=by_chunk(i["L3_ffn_values_up"].reshape(SLOTS * SLOTD, D)), spread=on_rows(spread),
                       scale=np.tile(i["L3_ffn_scale"][None], (P, 1))),
    }
    out = {}
    for name, fields in WIDTHS.items():
        parts = [packs[name][field] for field, _ in fields]
        assert [p.shape for p in parts] == [(P, n) for _, n in fields], (name, [p.shape for p in parts])
        out[name] = np.ascontiguousarray(np.concatenate(parts, 1), dtype=f32)
    return out


def constants():
    f32 = np.float32
    causal = np.zeros((P, BANK), f32)
    causal[:, BANK - P:] = np.where(np.arange(P)[None, :] > np.arange(P)[:, None], f32(MASKED), f32(0))
    den16 = np.zeros((P, P), f32)
    for h in range(4):
        den16[h * PITCH + HD, h * PITCH:(h + 1) * PITCH] = 1.0
    guard8, guard6 = (np.zeros((P, 1), f32) for _ in range(2))
    guard8[HD::PITCH], guard6[HD::PITCH] = 1e-8, 1e-6
    ones_k, parts_q, parts_k = (np.zeros((P, 1), f32) for _ in range(3))
    for h in range(2):
        ones_k[h * STACK + SPARE:h * STACK + SPARE + 2] = 1.0
        parts_q[h * STACK + HD:h * STACK + 2 * HD] = -1.0
        parts_k[h * STACK + 2 * HD:h * STACK + 3 * HD] = -1.0
        parts_k[h * STACK + SPARE:h * STACK + SPARE + 2] = 1.0
    fields = dict(ident=np.eye(P, dtype=f32), causal=causal, den16=den16, guard8=guard8, guard6=guard6, ones_k=ones_k, parts_q=parts_q, parts_k=parts_k,
                  iota=np.tile(np.arange(64, dtype=f32)[None], (P, 1)), ones=np.ones((P, P), f32),
                  half=np.full((P, 16), 0.5, f32), minus_half=np.full((P, 16), -0.5, f32),
                  causal_cols=np.ascontiguousarray(causal[:, BANK - P:].T))
    return np.concatenate([fields[name] for name, _ in CONSTS], 1)


def host_arrays(inputs):
    i = {name: np.asarray(a) for name, a in inputs.items()}
    arrays = {
        "x": i["x"], "context": i["ctx_1024"], "mask": i["mask_BxSxS2_ik1"],
        "mask_t": np.ascontiguousarray(i["mask_BxSxS2_ik1"].transpose(0, 2, 1)),
        "key_mask": np.ascontiguousarray(i["mask_BxS2_bf0"]).view(np.int32),
        "w1": np.stack([by_chunk(w) for w in i["L2_ffn_W1"]]), "w2": np.stack([by_chunk(w) for w in i["L2_ffn_W2"]]),
        "consts": constants(),
    }
    return arrays, pack(i)


def kernel(**inputs):
    import concourse.bacc as _bacc
    from concourse.bass_utils import run_bass_kernel_spmd as _run

    arrays, packs = host_arrays(inputs)
    nc = _bacc.Bacc("TRN2", target_bir_lowering=False, num_devices=1)
    feed, aps = {}, {}
    for name, a in {**arrays, **{f"pack_{k}": v for k, v in packs.items()}}.items():
        feed[f"in_{name}"] = np.ascontiguousarray(a)
        aps[name] = nc.dram_tensor(f"in_{name}", a.shape, mybir.dt.from_np(a.dtype), kind="ExternalInput").ap()
    out = nc.dram_tensor("out", (B, T, D), F32, kind="ExternalOutput").ap()
    decoder(nc, aps["x"], aps["context"], aps["mask"], aps["mask_t"], aps["key_mask"], aps["w1"], aps["w2"],
            aps["consts"], {k: aps[f"pack_{k}"] for k in packs}, out)
    r = _run(nc, [feed], core_ids=[0])
    return r.results[0]["out"]
```

```python
from contextlib import ExitStack, contextmanager

import concourse.bass as bass
import numpy as np
from concourse import mybir

F32 = mybir.dt.float32
BF16 = mybir.dt.bfloat16
F32R = mybir.dt.float32r
I32 = mybir.dt.int32
U32 = mybir.dt.uint32
U8 = mybir.dt.uint8
ALU = mybir.AluOpType
ACT = mybir.ActivationFunctionType
AX = mybir.AxisListType

B, T, D, P = 4, 512, 256, 128
NT, NC = T // P, D // P
H, HD, PITCH = 16, D // 16, 32
GROUPS = H * PITCH // P
PAIRS = H // 2
STACK = 4 * HD
SPARE = 3 * HD
ROUND = 8
DK = 64
F = 1024
EXPERTS, HIDDEN_CHUNKS = 8, F // P
MIX, MIXD = 16, 64
SLOTS, SLOTD = 64, 32
BANK = 512
BANKS = 8
WARM_LAYERNORM, WARM_RECIPROCAL, WARM_ROUTER = 12, 10, 12
PUT_AT = 6
LN_EPS = 1e-5
MASKED = -1e30
SEMS = 16

WIDTHS = {
    "L0_attn": [("wq", 512), ("wk", 512), ("wv", 512), ("cos", 512), ("sin", 512)],
    "L0_xattn": [("wq", 512), ("wk", 512), ("wv", 512), ("wo", 1024), ("bo", 256)],
    "L0_ffn": [("sim", 32), ("gates", 16), ("q", 2048), ("k", 2048), ("v", 2048), ("o", 2048)],
    "L1_attn": [("wq", 512), ("wk", 512), ("wv", 512), ("wo", 1024)],
    "L1_xattn": [("wq", 512), ("wk", 512), ("wv", 512), ("wo", 512), ("bq", 2), ("bk", 2),
                 ("bv", 256), ("bo", 256)],
    "L1_ffn": [("fc", 2048), ("proj", 2048), ("ln_w", 8), ("ln_b", 8)],
    "L2_attn": [("wqkv", 1536), ("bqkv", 768), ("gq", 2), ("hq", 2), ("gk", 2), ("hk", 2),
                ("wo", 1024), ("bo", 256)],
    "L2_xattn": [("wq", 2048), ("wk", 2048), ("wv", 2048), ("wo", 2048), ("bq", 8), ("bk", 8),
                 ("bv", 1024), ("bo", 256)],
    "L2_ffn": [("rms", 2), ("gate", 16), ("b1", 64), ("b2", 256)],
    "L3_attn": [("wq", 512), ("wqr", 512), ("wk", 512), ("wkr", 512), ("wv", 512), ("wo", 1024),
                ("cos", 512), ("sin", 512), ("bo", 256)],
    "L3_xattn": [("w", 512), ("b", 2), ("d", 2)],
    "L3_ffn": [("hash", 64), ("keys", 64), ("down", 4096), ("up", 4096), ("spread", 2048), ("scale", 1)],
}
CONSTS = [("ident", P), ("causal", BANK), ("gather", PITCH), ("scatter", GROUPS * P), ("guard8", 1), ("guard6", 1), ("ones_k", 1), ("iota", 64), ("ones", P),
          ("half", 16), ("minus_half", 16), ("causal_cols", P)]
SUBLAYERS = list(WIDTHS)
EXPERT = 2 * D * F // P


def offsets(fields):
    at, out = 0, {}
    for name, width in fields:
        out[name] = (at, width)
        at += width
    return out, at


def pack_width(name):
    return sum(width for _, width in WIDTHS[name])


ARENAS = [max(*(pack_width(n) for n in SUBLAYERS[0::2]), pack_width("L2_ffn") + 2 * EXPERT),
          max(pack_width(n) for n in SUBLAYERS[1::2])]


class Net:

    def __init__(self, nc, ctx):
        self.nc, self.ctx = nc, ctx
        self.banks = [[ctx.enter_context(nc.semaphore(f"sem_{half}_{i}")) for i in range(SEMS)] for half in range(2)]
        self.turn = 0
        self.tensors = 0
        self.psum = ctx.enter_context(nc.psum_tensor("psum", [P, BANKS, BANK], F32))

    def keep_warm(self, pe, products):
        for _ in range(products):
            pe.matmul(self.psum[:, BANKS - 1, :], self.select[:, 0, :], self.select[:, 0:BANK // P, :], start=True, stop=True)

    def sbuf(self, name, shape, dt=F32, ctx=None):
        self.tensors += 1
        return (ctx or self.ctx).enter_context(self.nc.sbuf_tensor(f"{name}_{self.tensors}", shape, dt))

    @contextmanager
    def block(self):
        mine, other = self.banks[self.turn], self.banks[1 - self.turn]
        self.turn = 1 - self.turn
        free = iter(mine)
        with self.nc.Block() as block:
            @block.gpsimd
            def _(pool):
                pool.sem_clear(range(other[0].num, other[-1].num + 1))
            yield block, lambda signals: next(free)



class Product:

    def __init__(self, engine, rows, cols, mms, out, finish, split=None):
        self.engine, self.rows, self.cols, self.mms = engine, rows, cols, mms
        self.out, self.finish, self.split = out, finish, split


def summed(terms):
    n = len(terms)
    return [(None, a, b, i == 0, i == n - 1, False) for i, (a, b) in enumerate(terms)]


def turned(tiles, ident):
    return [(slice(i * P, i * P + t.shape[0]), t, ident[0:t.shape[0], 0:t.shape[0]], True, True, True)
            for i, t in enumerate(tiles)]


def finished(eng, p, ps):
    src = ps[0:p.rows, 0:p.cols]
    if p.split:
        src = src.rearrange("p (a b) -> p a b", a=p.split)
    kind, *args = p.finish
    if kind == "act":
        func, bias, scale = args
        kw = {} if bias is None else {"bias": bias}
        return eng.activation(p.out, src, func, scale=scale, **kw)
    if kind == "copy":
        return eng.tensor_copy(p.out, src)
    if kind == "scalar":
        s1, s2, op0, op1 = args
        return eng.tensor_scalar(p.out, src, s1, s2, op0, op1)
    if kind == "twice":
        table, other_out, other_table = args
        eng.tensor_tensor(other_out, src, other_table, ALU.mult)
        return eng.tensor_tensor(p.out, src, table, ALU.mult)
    if kind == "tensor":
        other, op = args
        return eng.tensor_tensor(p.out, src, other, op)
    scalar, other, op0, op1 = args
    return eng.scalar_tensor_tensor(out=p.out, in0=src, scalar=scalar, in1=other, op0=op0, op1=op1)


COPY = ("act", ACT.Copy, None, 1.0)
VCOPY = ("copy",)


def products(net, table, name="products"):
    owner = [p.engine for p in table]
    with net.block() as (block, sem):
        product_done, act_done, dve_done = sem("product"), sem("finished"), sem("finished")

        @block.tensor
        def _(pe):
            for n, p in enumerate(table):
                if n >= BANKS:
                    last = n - BANKS
                    pe.wait_ge(act_done if owner[last] == "act" else dve_done, owner[:last + 1].count(owner[last]))
                bank = net.psum[:, n % BANKS, :]
                for where, lhsT, rhs, start, stop, turn in p.mms:
                    dst = bank[0:p.rows, where] if where is not None else bank[0:p.rows, 0:p.cols]
                    if turn:
                        mm = pe.transpose(dst, lhsT, rhs)
                    else:
                        mm = pe.matmul(dst, lhsT, rhs, start=start, stop=stop)
                mm.then_inc(product_done, 1)

        @block.scalar
        def _(act):
            for n, p in enumerate(table):
                if p.engine == "act":
                    act.wait_ge(product_done, n + 1)
                    finished(act, p, net.psum[:, n % BANKS, :]).then_inc(act_done, 1)

        @block.vector
        def _(dve):
            done = 0
            for n, p in enumerate(table):
                if p.engine == "dve":
                    dve.wait_ge(product_done, n + 1)
                    if p.finish[0] == "stt" and done:
                        dve.wait_ge(dve_done, done)
                    finished(dve, p, net.psum[:, n % BANKS, :]).then_inc(dve_done, 1)
                    done += 1


def cols_out(engine, w, width, src, m, out, finish=COPY, rows=P, n=T, bias=None):
    chunks = src.shape[1]
    terms = [(w[:, k * width + m:k * width + m + rows], src[:, k, :]) for k in range(chunks)]
    return Product(engine, rows, n, summed(terms), out, finish)


def rows_out(engine, src, t, w, width, at, n, out, finish=COPY, bias=None, split=None):
    terms = [(src[:, k, t * P:(t + 1) * P], w[:, k * width + at:k * width + at + n]) for k in range(src.shape[1])]
    if bias is not None:
        row = bias[:, at:at + n]
        engine, finish = "dve", ("tensor", row.rearrange("p (a b) -> p a b", a=split) if split else row, ALU.add)
    return Product(engine, P, n, summed(terms), out, finish, split)



def layernorm(net, x, xn, xc, bias=None, fetches=(), need=None, parts=None):
    with ExitStack() as ctx:
        stats = net.sbuf("stats", [P, NT, 6], ctx=ctx)
        mv = net.sbuf("mean_var", [P, NT, 2], ctx=ctx)
        rstd = net.sbuf("rstd", [P, NT], ctx=ctx)
        with net.block() as (block, sem):
            stats_done, mv_done, rstd_done = sem("stats"), sem("mean and variance"), sem("1/std")
            xn_done, turned_done, guarded = sem("normalised tile"), sem("transposed chunk"), sem("variance + eps")
            high_done, bias_done = sem("tile copied, with its high part"), sem("bias added to a tile")

            def turned_tile(t):
                return net.psum[:, t, 0:D].rearrange("p (c n) -> p c n", c=NC)

            def of_tile(cols, t):
                return cols[:, :, t * P:(t + 1) * P]

            @block.gpsimd
            def _(pool):
                pool.wait_ge(mv_done, NT)
                pool.tensor_scalar(rstd[:, :], mv[:, :, 1], LN_EPS, None, ALU.add, ALU.bypass).then_inc(guarded, 1)
                pool.wait_ge(guarded, 1)
                pool.tensor_tensor(rstd[:, :], rstd[:, :], net.minus_half[:, 0:NT], ALU.pow).then_inc(rstd_done, 1)
                if bias is not None:
                    if need is not None:
                        pool.wait_ge(need[0], need[1])
                    for t in range(NT):
                        pool.wait_ge(xn_done, t + 1)
                        if t:
                            pool.wait_ge(bias_done, t)
                        pool.tensor_tensor(x[:, t, :], x[:, t, :], bias, ALU.add).then_inc(bias_done, 1)

            @block.sync
            def _(sp):
                for signal, to, source in fetches:
                    sp.dma_start(to, source).then_inc(signal, 16)
                if need is not None:
                    sp.wait_ge(need[0], need[1])

            @block.vector
            def _(dve):
                for t in range(NT):
                    dve.bn_stats(stats[:, t, :], x[:, t, :]).then_inc(stats_done, 1)
                for t in range(NT):
                    dve.wait_ge(stats_done, t + 1)
                    dve.bn_aggr(mv[:, t, :], stats[:, t, :]).then_inc(mv_done, 1)
                dve.wait_ge(rstd_done, 1)
                for t in range(NT):
                    dve.tensor_scalar(xn[:, t, :], x[:, t, :], mv[:, t, 0:1], rstd[:, t:t + 1],
                                      ALU.subtract, ALU.mult).then_inc(xn_done, 1)
                if parts is None:
                    dve.wait_ge(turned_done, NT)
                    dve.tensor_copy(of_tile(xc, NT - 1), turned_tile(NT - 1))
                else:
                    for t in range(NT):
                        dve.wait_ge(high_done, t + 1)
                        dve.tensor_tensor(of_tile(parts[1], t), turned_tile(t), of_tile(parts[0], t).bitcast(F32), ALU.subtract)

            @block.tensor
            def _(pe):
                net.keep_warm(pe, WARM_LAYERNORM)
                for t in range(NT):
                    pe.wait_ge(xn_done, t + 1)
                    for c in range(NC):
                        mm = pe.transpose(net.psum[:, t, c * P:(c + 1) * P], xn[:, t, c * P:(c + 1) * P], net.ident)
                    mm.then_inc(turned_done, 1)

            @block.scalar
            def _(act):
                for t in range(NT if parts else NT - 1):
                    act.wait_ge(turned_done, t + 1)
                    ins = act.activation(of_tile(xc, t), turned_tile(t), ACT.Copy)
                    if parts:
                        ins = act.activation(of_tile(parts[0], t), turned_tile(t), ACT.Copy)
                    ins.then_inc(high_done, 1)



def wide_attention(net, q, k, values, width, causal, finish, keep=None, gone=None):
    masked = causal or keep is not None
    with ExitStack() as ctx:
        probs = net.sbuf("probs", [P, 2, T], ctx=ctx)
        scores = net.sbuf("scores", [P, 2, T], ctx=ctx) if masked else None
        kept = net.sbuf("kept", [P, 2, T], ctx=ctx) if keep is not None else None
        probs_t = net.sbuf("probs_t", [P, 2, T], ctx=ctx)
        nmax = net.sbuf("nmax", [P, NT], ctx=ctx)
        total = net.sbuf("total", [P, NT], ctx=ctx)
        inverse = net.sbuf("inverse", [P, NT], ctx=ctx)
        span = [(t + 1) * P if causal else T for t in range(NT)]
        with net.block() as (block, sem):
            scores_done, kept_done, max_done, probs_done = sem("scores"), sem("kept"), sem("maximum"), sem("exp")
            turned_done, copied_done, out_done = sem("transposed"), sem("transpose copied"), sem("p @ v")
            inverse_done, tile_done = sem("1/sum"), sem("tile written")

            @block.tensor
            def _(pe):
                def score(t):
                    if t >= 2:
                        if masked:
                            pe.wait_ge(max_done, t - 1)
                        else:
                            pe.wait_ge(probs_done, t - 1)
                    for i, (a, b) in enumerate(zip(q, k)):
                        mm = pe.matmul(net.psum[:, t % 2, 0:span[t]], a[:, t * P:(t + 1) * P], b[:, 0:span[t]],
                                       start=i == 0, stop=i == len(q) - 1)
                    mm.then_inc(scores_done, 1)

                score(0)
                for t in range(NT):
                    if t + 1 < NT:
                        score(t + 1)
                    pe.wait_ge(probs_done, t + 1)
                    if t >= 2:
                        pe.wait_ge(copied_done, t - 1)
                    for c in range(span[t] // P):
                        mm = pe.transpose(net.psum[:, 2 + t % 2, c * P:(c + 1) * P],
                                          probs[:, t % 2, c * P:(c + 1) * P], net.ident)
                    mm.then_inc(turned_done, 1)
                    pe.wait_ge(copied_done, t + 1)
                    if t >= 2:
                        pe.wait_ge(tile_done, t - 1)
                    n = span[t] // P
                    for c in range(n):
                        mm = pe.matmul(net.psum[:, 4 + t % 2, 0:width], probs_t[:, t % 2, c * P:(c + 1) * P],
                                       values(c), start=c == 0, stop=c == n - 1)
                    mm.then_inc(out_done, 1)

            @block.vector
            def _(dve):
                def maximum(t):
                    dve.wait_ge(scores_done, t + 1)
                    src = net.psum[:, t % 2, 0:span[t]]
                    if not masked:
                        dve.tensor_reduce(nmax[:, t:t + 1], src, AX.X, ALU.max, negate=True).then_inc(max_done, 1)
                        return
                    if t >= 2:
                        dve.wait_ge(probs_done, t - 1)
                    if keep is not None:
                        dve.tensor_tensor(kept[:, t % 2, :], src, keep, ALU.mult).then_inc(kept_done, 1)
                        dve.wait_ge(kept_done, t + 1)
                        src, mask = kept[:, t % 2, :], gone
                    else:
                        mask = net.causal[:, BANK - span[t]:BANK]
                    dve.tensor_tensor_reduce(scores[:, t % 2, 0:span[t]], src, mask, -1.0, 3e38, ALU.add, ALU.min,
                                             nmax[:, t:t + 1]).then_inc(max_done, 1)

                maximum(0)
                for t in range(NT):
                    if t + 1 < NT:
                        maximum(t + 1)
                    dve.wait_ge(turned_done, t + 1)
                    if t >= 2:
                        dve.wait_ge(out_done, t - 1)
                    dve.tensor_copy(probs_t[:, t % 2, 0:span[t]], net.psum[:, 2 + t % 2, 0:span[t]])\
                       .then_inc(copied_done, 1)
                    dve.wait_ge(probs_done, t + 1)
                    dve.reciprocal(inverse[:, t:t + 1], total[:, t:t + 1]).then_inc(inverse_done, 1)
                    dve.wait_ge(inverse_done, t + 1)
                    dve.wait_ge(out_done, t + 1)
                    finish(dve, t, net.psum[:, 4 + t % 2, 0:width], inverse[:, t:t + 1]).then_inc(tile_done, 1)

            @block.scalar
            def _(act):
                for t in range(NT):
                    act.wait_ge(max_done, t + 1)
                    if t >= 2:
                        act.wait_ge(turned_done, t - 1)
                    src = scores[:, t % 2, 0:span[t]] if masked else net.psum[:, t % 2, 0:span[t]]
                    act.activation(probs[:, t % 2, 0:span[t]], src, ACT.Exp, bias=nmax[:, t:t + 1],
                                   scale=-1.0 if masked else 1.0, accum_out=total[:, t:t + 1]).then_inc(probs_done, 1)



def many_heads(net, passes, put_in, v, hd, o, pairs, scale, guard=None, causal=False, linear=False, mask_rows=None, mask_cols=None):
    packed = hd == HD
    future = causal and not linear
    cut = causal and linear
    lag = 2
    turns = 1 if packed else 2
    at = SPARE
    tiles, steps = 2 * NT, NT
    width = hd + 1
    ring = (0, 1, 7) if packed else (0, 1)

    def slot(p, n):
        return tiles * p + n + (turns * (p - 1 + (n >= PUT_AT)) if p else 0)

    def put_slot(p):
        return tiles * (p + 1) + turns * p + (PUT_AT if p + 1 < pairs else 0)

    with ExitStack() as ctx:
        if not linear:
            nmax = net.sbuf("nmax", [P, pairs, NT, 2], ctx=ctx)
            spread = net.sbuf("spread", [P, 2, turns, NT, P], ctx=ctx)
        masked = net.sbuf("masked", [P, T], ctx=ctx) if mask_rows is not None else None
        if not packed:
            inverse = net.sbuf("inverse", [P, 2, NT], ctx=ctx)
        buffers = 3 if packed else 2
        probs = net.sbuf("probs", [P, buffers, 2, T], ctx=ctx)
        with net.block() as (block, sem):
            cleared, scores_done = sem("spread zeroed"), sem("scores")
            row_read = sem("a turn's bank read: maximum taken, or -max put into q")
            high_done, split_done = sem("high part of -max"), sem("low part of -max")
            turned_done = sem("-max transposed")
            colscores_done, probs_done, cut_done = sem("transposed scores"), sem("exp"), sem("future cut off")
            second_done = sem("linear: scores of a step's second head copied")
            pv_done, o_done = sem("p @ v of a step"), sem("output copied")
            sums_read, inverted = sem("sums kept above zero"), sem("1/sum")

            @block.gpsimd
            def _(pool):
                if not linear:
                    pool.memset(spread[:, :, :, :, :], 0.0).then_inc(cleared, 1)
                if cut:
                    for n in range(pairs * steps):
                        pool.wait_ge(probs_done, n + 1)
                        pool.wait_ge(second_done, n + 1)
                        kt = n % steps
                        d = probs[:, n % buffers, :, kt * P:(kt + 1) * P]
                        pool.affine_select(out=d, in_=d, compare_op=ALU.is_ge, fill=0.0, base=0,
                                           pattern=[[0, 2], [1, P]], channel_multiplier=-1).then_inc(cut_done, 1)

            @block.tensor
            def _(pe):
                def score(p, n):
                    qt, s = n // 2, slot(p, n)
                    if s >= len(ring):
                        pe.wait_ge(row_read, s - len(ring) + 1)
                    w = (qt + 1) * P if causal else T
                    bank = net.psum[:, ring[s % len(ring)], 0:w]
                    terms = passes(2 * p + n % 2)
                    last = len(terms) - 1
                    for i, (k, q) in enumerate(terms):
                        mm = pe.matmul(bank, q[:, qt * P:(qt + 1) * P], k[:, 0:w], start=i == 0, stop=i == last and not causal)
                    if causal:
                        mm = pe.matmul(bank[:, qt * P:w], net.ident16, net.causal16, start=False, stop=True)
                    mm.then_inc(scores_done, 1)

                def put(p):
                    pe.wait_ge(split_done, p + 1)
                    for i in range(turns):
                        s = put_slot(p) + i
                        pe.wait_ge(row_read, s - len(ring) + 1)
                        for t in range(NT):
                            mm = pe.transpose(net.psum[:, ring[s % len(ring)], t * P:(t + 1) * P], spread[:, p % 2, i, t, :],
                                              net.ident)
                        mm.then_inc(turned_done, 1)

                def col_scores(n):
                    p, kt = n // steps, n % steps
                    if not linear and kt == 0:
                        pe.wait_ge(row_read, put_slot(p) + turns)
                    if n >= 2:
                        pe.wait_ge(probs_done, n - 1)
                        if linear:
                            pe.wait_ge(second_done, n - 1)
                    lo = kt * P if causal else 0
                    for j in range(2):
                        bank = net.psum[:, 2 + 2 * (n % 2) + j, lo:T]
                        terms = passes(2 * p + j)
                        last = len(terms) - 1
                        for i, (k, q) in enumerate(terms):
                            mm = pe.matmul(bank, k[:, kt * P:(kt + 1) * P], q[:, lo:T], start=i == 0,
                                           stop=i == last and mask_cols is None and not future)
                        if future:
                            mm = pe.matmul(bank[:, 0:P], net.ident16, net.causal_cols16, start=False, stop=True)
                        if mask_cols is not None:
                            mm = pe.matmul(bank, net.ident16, mask_cols[:, kt, :], start=False, stop=True)
                    mm.then_inc(colscores_done, 1)

                def weigh(n):
                    p, kt = n // steps, n % steps
                    pe.wait_ge(cut_done if cut else probs_done, n + 1)
                    if packed and kt == 0 and p % 2 == 0 and p:
                        pe.wait_ge(o_done, p // 2)
                    if not packed and kt == 0 and p:
                        pe.wait_ge(o_done, 2 * p)
                    lo = kt * P if causal else 0
                    for j in range(2):
                        if packed:
                            u = (2 * p + j) % 4
                            mm = pe.matmul(net.psum[u * PITCH:(u + 1) * PITCH, 6, lo:T], v(kt, 2 * p + j), probs[:, n % buffers, j, lo:T],
                                           start=kt == 0, stop=kt == steps - 1, tile_position=(0, u * PITCH))
                        else:
                            for t in range(NT):
                                mm = pe.matmul(net.psum[:, 6 + j, t * width:(t + 1) * width], probs[:, n % buffers, j, t * P:(t + 1) * P],
                                               v(kt, 2 * p + j), start=kt == 0 and t == 0, stop=kt == steps - 1 and t == NT - 1)
                    mm.then_inc(pv_done, 1)

                behind = buffers - 1
                if linear:
                    for n in range(pairs * steps):
                        col_scores(n)
                        if n >= behind:
                            weigh(n - behind)
                else:
                    for p in range(pairs + lag):
                        for i in range(steps):
                            if p < pairs:
                                score(p, 2 * i)
                            if p >= lag:
                                col_scores((p - lag) * steps + i)
                            if p < pairs:
                                score(p, 2 * i + 1)
                            if (p - lag) * steps + i >= behind:
                                weigh((p - lag) * steps + i - behind)
                            if 1 <= p <= pairs and i == (PUT_AT // 2 - 1 if p < pairs else 0):
                                put(p - 1)
                for n in range(pairs * steps - behind, pairs * steps):
                    weigh(n)

            @block.vector
            def _(dve):
                def maximum(p, n):
                    qt, s = n // 2, slot(p, n)
                    w = (qt + 1) * P if causal else T
                    dve.wait_ge(scores_done, tiles * p + n + 1)
                    bank, out = net.psum[:, ring[s % len(ring)], 0:w], nmax[:, p, qt, n % 2:n % 2 + 1]
                    if mask_rows is None:
                        dve.tensor_reduce(out, bank, AX.X, ALU.max, negate=True).then_inc(row_read, 1)
                    else:
                        dve.wait_ge(row_read, s)
                        dve.tensor_tensor_reduce(masked[:, :], bank, mask_rows[:, qt, :], -1.0, 3e38, ALU.add, ALU.min, out)\
                           .then_inc(row_read, 1)

                def split(p):
                    dve.wait_ge(row_read, slot(p, tiles - 1) + 1)
                    m = nmax[:, p, :, :]
                    if not packed:
                        dve.tensor_scalar(m, m, 1e20, None, ALU.min).then_inc(high_done, 1)
                        dve.wait_ge(high_done, 3 * p + 1)
                    if p >= 2:
                        dve.wait_ge(turned_done, turns * (p - 1))
                    if packed:
                        both = spread[:, p % 2, 0, :, :].rearrange("p t (j c) -> p t j c", j=2)
                        dve.tensor_copy(both[:, :, :, at].bitcast(F32R), m).then_inc(high_done, 1)
                        dve.wait_ge(high_done, p + 1)
                        dve.tensor_tensor(both[:, :, :, at + 1], m, both[:, :, :, at], ALU.subtract).then_inc(split_done, 1)
                        return
                    for j in range(2):
                        c = (1 - j) * hd
                        dve.tensor_copy(spread[:, p % 2, j, :, c].bitcast(F32R), m[:, :, j]).then_inc(high_done, 1)
                    dve.wait_ge(high_done, 3 * (p + 1))
                    for j in range(2):
                        c = (1 - j) * hd
                        ins = dve.tensor_tensor(spread[:, p % 2, j, :, c + 1], m[:, :, j], spread[:, p % 2, j, :, c], ALU.subtract)
                    ins.then_inc(split_done, 1)

                def put(p):
                    for i in range(turns):
                        dve.wait_ge(turned_done, turns * p + i + 1)
                        tile, where = put_in(p * turns + i)
                        bank = ring[(put_slot(p) + i) % len(ring)]
                        dve.tensor_tensor(tile[where, :], tile[where, :].bitcast(F32), net.psum[where, bank, :],
                                          ALU.add).then_inc(row_read, 1)

                def copy_out(p):
                    dve.wait_ge(pv_done, steps * (p + 1))
                    if packed:
                        if guard is None:
                            ins = dve.tensor_copy(o[:, p // 2, :], net.psum[:, 6, :])
                        else:
                            ins = dve.tensor_scalar(o[:, p // 2, :], net.psum[:, 6, :], guard, None, ALU.add)
                        ins.then_inc(o_done, 1)
                    else:
                        if p:
                            dve.wait_ge(o_done, 2 * p)
                        out = net.psum[:, 6:8, 0:NT * width].rearrange("p j (t d) -> p j t d", t=NT)
                        dve.tensor_scalar(inverse[:, :, :], out[:, :, :, hd], 1e-30, None, ALU.max).then_inc(sums_read, 1)
                        dve.wait_ge(sums_read, p + 1)
                        dve.reciprocal(inverse[:, :, :], inverse[:, :, :]).then_inc(inverted, 1)
                        dve.wait_ge(inverted, p + 1)
                        for j in range(2):
                            dve.tensor_tensor(o[:, :, 2 * p + j, :], out[:, j, :, 0:hd],
                                              inverse[:, j, :].unsqueeze(2).broadcast_to([P, NT, hd]), ALU.mult).then_inc(o_done, 1)

                if linear:
                    for n in range(pairs * steps):
                        lo = n % steps * P if causal else 0
                        dve.wait_ge(colscores_done, n + 1)
                        if n >= buffers:
                            dve.wait_ge(pv_done, n - buffers + 1)
                        dve.tensor_copy(probs[:, n % buffers, 1, lo:T], net.psum[:, 3 + 2 * (n % 2), lo:T]).then_inc(second_done, 1)
                        if n % (2 * steps) == 1 and n > 1:
                            copy_out(n // steps - 1)
                else:
                    dve.wait_ge(cleared, 1)
                    for p in range(pairs + lag):
                        for n in range(tiles):
                            if p < pairs:
                                maximum(p, n)
                            if not packed and n == 1 and p >= lag + 1:
                                copy_out(p - lag - 1)
                            if n == PUT_AT - 1 and 1 <= p <= pairs:
                                put(p - 1)
                        if p < pairs:
                            split(p)
                if linear or not packed:
                    copy_out(pairs - 1)

            @block.scalar
            def _(act):
                def copy_out(p):
                    act.wait_ge(pv_done, steps * (p + 1))
                    bias = {} if guard is None else {"bias": guard}
                    act.activation(o[:, p // 2, :], net.psum[:, 6, :], ACT.Identity, **bias).then_inc(o_done, 1)

                for n in range(pairs * steps):
                    kt = n % steps
                    lo = kt * P if causal else 0
                    act.wait_ge(colscores_done, n + 1)
                    if n >= buffers:
                        act.wait_ge(pv_done, n - buffers + 1)
                    first = 2 + 2 * (n % 2)
                    if linear:
                        act.activation(probs[:, n % buffers, 0, lo:T], net.psum[:, first, lo:T], ACT.Copy).then_inc(probs_done, 1)
                    else:
                        act.activation(probs[:, n % buffers, :, lo:T], net.psum[:, first:first + 2, lo:T], ACT.Exp, scale=scale)\
                           .then_inc(probs_done, 1)
                    if packed and not linear and n % (2 * steps) == 0 and n > 0:
                        copy_out(n // steps - 1)
                if packed and not linear:
                    copy_out(pairs - 1)


def stack_parts(net, jobs, qs, ks, v, values, vbias, rope=None):
    v_engine = ["dve" if vbias is not None else alternate(t) for t in range(NT)]
    square = jobs[0][2] is not None
    outputs = 2 * PAIRS
    by_act = [m % 2 or m // 2 % 2 == 0 for m in range(outputs)]
    by_dve = [m % 2 or m // 2 % 2 == 1 for m in range(outputs)]
    halves = [slice(j * STACK, (j + 1) * STACK) for j in range(2)]
    with ExitStack() as ctx:
        high = net.sbuf("high", [P, 4, T], F32R, ctx=ctx)
        low = net.sbuf("low", [P, 4, T], F32R, ctx=ctx)
        value = net.sbuf("value", [P, 4, T], ctx=ctx) if rope or square else None
        rotated = net.sbuf("rotated", [P, 4, T], ctx=ctx) if rope else None
        with net.block() as (block, sem):
            product_done, value_done, high_done, low_done = sem("product"), sem("value"), sem("high"), sem("low")
            cos_done, sin_done, zeroed = sem("times cosine"), sem("times sine"), sem("zeroed")
            placed, act_done, dve_done = sem("parts in place"), sem("copied by ScalarE"), sem("copied by VectorE")
            v_done, v_by_act, v_by_dve = sem("values product"), sem("values by ScalarE"), sem("values by VectorE")

            def heads_of(t):
                return net.psum[:, 4 + t, 0:D].rearrange("p (h d) -> p h d", h=H)

            @block.tensor
            def _(pe):
                for t, terms in enumerate(values):
                    for where, lhsT, rhs, start, stop, turn in terms:
                        mm = pe.matmul(net.psum[:, 4 + t, 0:D], lhsT, rhs, start=start, stop=stop)
                    mm.then_inc(v_done, 1)
                for n, (terms, turned_terms, sq) in enumerate(jobs):
                    if n == 2:
                        if "act" in v_engine:
                            pe.wait_ge(v_by_act, v_engine.count("act"))
                        pe.wait_ge(v_by_dve, v_engine.count("dve"))
                    for which, group in enumerate((terms, turned_terms)):
                        for where, lhsT, rhs, start, stop, turn in group or ():
                            bank = net.psum[:, 2 * n + which, :]
                            if turn:
                                mm = pe.transpose(bank[:, where], lhsT, rhs)
                            else:
                                mm = pe.matmul(bank, lhsT, rhs, start=start, stop=stop)
                    mm.then_inc(product_done, 1)
                for m in range(outputs):
                    p, is_k = m // 2, m % 2
                    src = 2 * (p // 4) + is_k
                    if p % 4 == 0:
                        pe.wait_ge(high_done, src + 1)
                        pe.wait_ge(low_done, max(src, 1) + 1)
                    if m >= 4:
                        pe.wait_ge(act_done, sum(by_act[:m - 3]))
                        pe.wait_ge(dve_done, sum(by_dve[:m - 3]))
                    for part, parts in enumerate((high, low)):
                        mm = pe.matmul(net.psum[:, m % 4, :], net.select[:, 4 * (2 * is_k + part) + p % 4, :], parts[:, src, :],
                                       start=part == 0, stop=part == 1)
                    mm.then_inc(placed, 1)

            def source(n):
                return value[:, n, :] if rope or square else net.psum[:, 2 * n, :]

            @block.gpsimd
            def _(pool):
                if rope:
                    for n in range(len(jobs)):
                        pool.wait_ge(cos_done, n + 1)
                        pool.wait_ge(sin_done, n + 1)
                        if n:
                            pool.wait_ge(value_done, n)
                        pool.tensor_tensor(value[:, n, :], value[:, n, :], rotated[:, n, :], ALU.add).then_inc(value_done, 1)
                    pool.wait_ge(value_done, len(jobs))
                for j in range(2):
                    pool.memset(ks[halves[1 - j], j:H:2, :].bitcast(F32), 0.0).then_inc(zeroed, 1)
                pool.wait_ge(zeroed, 2)
                pool.memset(v[:, :, :, HD + 1:], 0.0).then_inc(zeroed, 1)
                pool.wait_ge(zeroed, 3)
                pool.memset(v[:, :, :, HD:HD + 1], 1.0)

            @block.scalar
            def _(act):
                for t in range(NT):
                    if v_engine[t] == "act":
                        act.wait_ge(v_done, t + 1)
                        act.activation(v[:, t, :, 0:HD], heads_of(t), ACT.Copy).then_inc(v_by_act, 1)
                for n, (terms, turned_terms, sq) in enumerate(jobs):
                    if square:
                        act.wait_ge(product_done, n + 1)
                        act.activation(value[:, n, :], net.psum[:, 2 * n, :], ACT.Square, bias=sq[1], scale=sq[0])\
                           .then_inc(value_done, 1)
                    act.wait_ge(value_done if rope or square else product_done, n + 1)
                    act.activation(high[:, n, :], source(n), ACT.Identity).then_inc(high_done, 1)
                for m in range(outputs):
                    if by_act[m]:
                        act.wait_ge(placed, m + 1)
                        if m % 2:
                            act.activation(ks[halves[0], m - 1, :], net.psum[halves[0], m % 4, :], ACT.Identity,
                                           bias=net.ones_k[halves[0], :]).then_inc(act_done, 1)
                        else:
                            act.activation(qs[:, m // 2, :], net.psum[:, m % 4, :], ACT.Identity).then_inc(act_done, 1)

            @block.vector
            def _(dve):
                for t in range(NT):
                    if v_engine[t] == "dve":
                        dve.wait_ge(v_done, t + 1)
                        if vbias is None:
                            ins = dve.tensor_copy(v[:, t, :, 0:HD], heads_of(t))
                        else:
                            ins = dve.tensor_tensor(v[:, t, :, 0:HD], heads_of(t), vbias.rearrange("p (h d) -> p h d", h=H), ALU.add)
                        ins.then_inc(v_by_dve, 1)
                if rope:
                    for n in range(len(jobs)):
                        dve.wait_ge(product_done, n + 1)
                        dve.tensor_tensor(value[:, n, :], net.psum[:, 2 * n, :], rope[0], ALU.mult).then_inc(cos_done, 1)
                        dve.tensor_tensor(rotated[:, n, :], net.psum[:, 2 * n + 1, :], rope[1], ALU.mult).then_inc(sin_done, 1)
                for n in range(len(jobs)):
                    dve.wait_ge(high_done, n + 1)
                    dve.tensor_tensor(low[:, n, :], source(n), high[:, n, :].bitcast(F32), ALU.subtract).then_inc(low_done, 1)
                for m in range(outputs):
                    if by_dve[m]:
                        dve.wait_ge(placed, m + 1)
                        if m % 2:
                            dve.tensor_scalar(ks[halves[1], m, :], net.psum[halves[1], m % 4, :], net.ones_k[halves[1], :], None,
                                              ALU.add).then_inc(dve_done, 1)
                        else:
                            dve.tensor_copy(qs[:, m // 2, :], net.psum[:, m % 4, :]).then_inc(dve_done, 1)


def divide_and_add(net, x, o, w):
    with ExitStack() as ctx:
        inv = net.sbuf("inv", [P, T], ctx=ctx)
        scaled = net.sbuf("scaled", [P, GROUPS, T], ctx=ctx)
        with net.block() as (block, sem):
            sums_done, inverse_done, spread_done = sem("sums gathered"), sem("1/sum"), sem("1/sum on the heads' partitions")
            scaled_done, out_done = sem("heads scaled"), sem("output product")

            @block.tensor
            def _(pe):
                for c in range(GROUPS):
                    mm = pe.matmul(net.psum[c * PITCH:(c + 1) * PITCH, 0, :], net.gather, o[:, c, :], start=True, stop=True,
                                   tile_position=(0, c * PITCH))
                mm.then_inc(sums_done, 1)
                net.keep_warm(pe, WARM_RECIPROCAL)
                pe.wait_ge(inverse_done, 1)

                def spread(c):
                    if c >= 2:
                        pe.wait_ge(scaled_done, c - 1)
                    pe.matmul(net.psum[:, 1 + c % 2, :], net.scatter[:, c * P:(c + 1) * P], inv[:, :], start=True, stop=True)\
                      .then_inc(spread_done, 1)
                spread(0)
                for c in range(GROUPS):
                    if c + 1 < GROUPS:
                        spread(c + 1)
                    pe.wait_ge(scaled_done, c + 1)
                    for t in range(NT):
                        mm = pe.matmul(net.psum[:, 4 + t, 0:D], scaled[:, c, t * P:(t + 1) * P], w[:, c * D:(c + 1) * D],
                                       start=c == 0, stop=c == GROUPS - 1)
                        if c == GROUPS - 1:
                            mm.then_inc(out_done, 1)

            @block.vector
            def _(dve):
                dve.wait_ge(sums_done, 1)
                dve.reciprocal(inv[:, :], net.psum[:, 0, :]).then_inc(inverse_done, 1)
                for c in range(GROUPS):
                    dve.wait_ge(spread_done, c + 1)
                    dve.tensor_tensor(scaled[:, c, :], o[:, c, :], net.psum[:, 1 + c % 2, :], ALU.mult).then_inc(scaled_done, 1)
                for t in range(NT):
                    dve.wait_ge(out_done, t + 1)
                    dve.tensor_tensor(x[:, t, :], x[:, t, :], net.psum[:, 4 + t, 0:D], ALU.add)


def add_output(net, x, src, chunks, rows, w):
    table = []
    for t in range(NT):
        terms = [(src[0:rows, c, t * P:(t + 1) * P], w[0:rows, c * D:(c + 1) * D]) for c in range(chunks)]
        table.append(Product("dve", P, D, summed(terms), x[:, t, :], ("tensor", x[:, t, :], ALU.add)))
    products(net, table)


def alternate(n):
    return "dve" if n % 2 else "act"


def copied(engine):
    return COPY if engine == "act" else VCOPY



def narrow_attention(net, W, x, qsrc, ksrc, scale, causal, guard, linear=False, jobs=None, rope=None):
    with ExitStack() as ctx:
        qs = net.sbuf("qs", [P, PAIRS, T], F32R, ctx=ctx)
        ks = net.sbuf("ks", [P, H, T], F32R, ctx=ctx)
        v = net.sbuf("v", [P, NT, H, PITCH], ctx=ctx)
        wv, width, at, bias = (W["wqkv"], 3 * D, 2 * D, W["bqkv"]) if "wqkv" in W else (W["wv"], D, 0, None)
        values = [summed([(ksrc[:, c, t * P:(t + 1) * P], wv[:, c * width + at:c * width + at + D]) for c in range(NC)])
                  for t in range(NT)]
        if jobs is None:
            def jobs(j, c):
                return (chunk_terms(*((W["wk"], ksrc) if j else (W["wq"], qsrc)), c), None, None)
        stack_parts(net, [jobs(j, c) for c in range(NC) for j in range(2)], qs, ks, v, values,
                    None if bias is None else bias[:, at:at + D], rope)
        o = net.sbuf("o", [P, GROUPS, T], ctx=ctx)
        many_heads(net, lambda h: [(ks[:, h, :], qs[:, h // 2, :])], lambda i: (qs[:, i, :], slice(0, P)),
                   lambda kt, h: v[:, kt, h, :], HD, o, PAIRS, scale, guard=guard, causal=causal, linear=linear)
        divide_and_add(net, x, o, W["wo"])


def chunk_terms(w, src, c):
    return summed([(w[:, i * D + c * P:i * D + (c + 1) * P], src[:, i, :]) for i in range(NC)])


def L0_attn(net, W, x, xn, xc, **_):
    with ExitStack() as ctx:
        q = net.sbuf("q", [P, NC, T], ctx=ctx)
        k = net.sbuf("k", [P, NC, T], ctx=ctx)
        v = net.sbuf("v", [P, NT, D], ctx=ctx)
        tmp = net.sbuf("tmp", [P, 8, T], ctx=ctx)
        table = []
        for i, (dst, w) in enumerate(((q, W["wq"]), (k, W["wk"]))):
            for c in range(NC):
                at = 4 * i + 2 * c
                table.append(cols_out("dve", w, D, xc, c * P, tmp[:, at, :], ("twice", W["cos"], tmp[:, at + 1, :], W["sin"])))
        table += [rows_out("act", xc, t, W["wv"], D, 0, D, v[:, t, :]) for t in range(NT)]
        products(net, table)
        with net.block() as (block, sem):
            rotated = sem("rotated")

            @block.vector
            def _(dve):
                for i, dst in enumerate((q, k)):
                    a = tmp[:, 4 * i:4 * i + 4, :]
                    dve.tensor_tensor(dst[:, 0, :], a[:, 0, :], a[:, 3, :], ALU.subtract).then_inc(rotated, 1)
                    dve.tensor_tensor(dst[:, 1, :], a[:, 1, :], a[:, 2, :], ALU.add).then_inc(rotated, 1)

            @block.scalar
            def _(act):
                act.wait_ge(rotated, 2)
                act.activation(q[:, :, :], q[:, :, :], ACT.Copy, scale=D ** -0.5)

        def finish(dve, t, ps, inverse):
            return dve.scalar_tensor_tensor(out=x[:, t, :], in0=ps, scalar=inverse, in1=x[:, t, :],
                                            op0=ALU.mult, op1=ALU.add)
        wide_attention(net, [q[:, c, :] for c in range(NC)], [k[:, c, :] for c in range(NC)],
                       lambda c: v[:, c, :], D, True, finish)


def L0_xattn(net, W, x, xn, xc, cc, **_):
    narrow_attention(net, W, x, xc, cc, D ** -0.5, False, None)


def L0_ffn(net, W, x, xn, xc, parts, **_):
    with ExitStack() as ctx:
        lasting = lambda name, shape: net.sbuf(name, shape, ctx=ctx)
        gate, qkv = lasting("gate", [P, NT, MIX]), lasting("qkv", [P, NT, 3, MIXD])
        projecting = ctx.enter_context(ExitStack())
        sb = lambda name, shape, dt=F32: net.sbuf(name, shape, dt, ctx=projecting)
        wh, wl = (sb(f"qkv_{part}", [P, 3, 2 * MIX * MIXD], F32R) for part in ("high", "low"))
        xsq, ssum = sb("xsq", [P, D]), sb("ssum", [P, NT])
        simsq, simn, siminv = sb("simsq", [P, 2 * MIX]), sb("simn", [P, 2 * MIX]), sb("siminv", [P, MIX])
        sig, raw, logit = sb("sig", [P, MIX]), sb("raw", [P, NT, MIX]), sb("logit", [P, NT, MIX])
        g, a, e = sb("g", [P, NT, MIX]), sb("a", [P, NT, MIX]), sb("e", [P, NT, MIX])
        top, index, indexf = sb("top", [P, NT, 8]), sb("index", [P, NT, 8], U32), sb("indexf", [P, NT, 8])
        anyon, mx, tot = sb("anyon", [P, NT]), sb("mx", [P, NT]), sb("tot", [P, NT])
        fb, fb2 = sb("fb", [P, NT, MIX]), sb("fb2", [P, NT, MIX])
        with net.block() as (block, sem):
            step, colsum_done, sim_done, raw_done, exped, sig_done = (sem("step"), sem("column sums"), sem("similarity"),
                                                                      sem("products"), sem("exp"), sem("sigmoid"))

            floor_done, root_done = sem("sums of squares kept above zero"), sem("1/norms")
            high_done = sem("high part of a matrix")

            @block.gpsimd
            def _(pool):
                pool.wait_ge(floor_done, 1)
                pool.tensor_tensor(siminv[:, :], siminv[:, :], net.minus_half, ALU.pow).then_inc(root_done, 1)
                pool.tensor_tensor(ssum[:, :], ssum[:, :], net.minus_half[:, 0:NT], ALU.pow).then_inc(root_done, 1)
                pool.wait_ge(high_done, 1)
                pool.wait_ge(root_done, 2)
                pool.tensor_tensor(wl[:, 0, :], W["q"], wh[:, 0, :].bitcast(F32), ALU.subtract)

            @block.scalar
            def _(act):
                act.activation(sig[:, :], W["gates"], ACT.Sigmoid).then_inc(sig_done, 1)
                for j in range(3):
                    act.activation(wh[:, j, :], W["qkv"[j]], ACT.Copy).then_inc(high_done, 1)
                act.wait_ge(exped, 1)
                act.activation(e[:, :, :], e[:, :, :], ACT.Exp).then_inc(exped, 1)

            @block.tensor
            def _(pe):
                pe.wait_ge(step, 1)
                for c in range(NC):
                    mm = pe.matmul(net.psum[:, 0, 0:MIX], net.ones_pp, simsq[:, c * MIX:(c + 1) * MIX], start=c == 0, stop=c == 1)
                mm.then_inc(colsum_done, 1)
                pe.wait_ge(sim_done, 1)
                for t in range(NT):
                    for c in range(NC):
                        mm = pe.matmul(net.psum[:, 1, t * MIX:(t + 1) * MIX], xc[:, c, t * P:(t + 1) * P],
                                       simn[:, c * MIX:(c + 1) * MIX], start=c == 0, stop=c == 1)
                mm.then_inc(raw_done, 1)
                net.keep_warm(pe, 2 * WARM_ROUTER)

            @block.vector
            def _(dve):
                n = 0

                def then(ins):
                    nonlocal n
                    n += 1
                    ins.then_inc(step, 1)
                    dve.wait_ge(step, n)

                then(dve.tensor_tensor(simsq[:, :], W["sim"], W["sim"], ALU.mult))
                for t in range(NT):
                    then(dve.tensor_tensor_reduce(xsq[:, :], xn[:, t, :], xn[:, t, :], 1.0, 0.0, ALU.mult, ALU.add,
                                                  ssum[:, t:t + 1]))
                then(dve.tensor_scalar(ssum[:, :], ssum[:, :], 1e-24, None, ALU.max))
                dve.wait_ge(colsum_done, 1)
                dve.tensor_scalar(siminv[:, :], net.psum[:, 0, 0:MIX], 1e-24, None, ALU.max).then_inc(floor_done, 1)
                dve.wait_ge(root_done, 2)
                for c in range(NC):
                    ins = dve.tensor_tensor(simn[:, c * MIX:(c + 1) * MIX], W["sim"][:, c * MIX:(c + 1) * MIX],
                                            siminv[:, :], ALU.mult)
                    if c == 0:
                        then(ins)
                ins.then_inc(sim_done, 1)
                dve.wait_ge(raw_done, 1)
                then(dve.tensor_tensor(raw[:, :, :], net.psum[:, 1, 0:NT * MIX].rearrange("p (t e) -> p t e", t=NT),
                                       ssum[:, :].unsqueeze(2).broadcast_to([P, NT, MIX]), ALU.mult))
                dve.wait_ge(sig_done, 1)
                then(dve.tensor_tensor(logit[:, :, :], raw[:, :, :],
                                       sig[:, :].unsqueeze(1).broadcast_to([P, NT, MIX]), ALU.subtract))
                then(dve.tensor_scalar(g[:, :, :], logit[:, :, :], 0.0, None, ALU.max))
                then(dve.tensor_scalar(a[:, :, :], logit[:, :, :], 0.0, None, ALU.is_gt))
                then(dve.tensor_reduce(anyon[:, :], a[:, :, :], AX.X, ALU.max))
                then(dve.tensor_reduce(mx[:, :], g[:, :, :], AX.X, ALU.max))
                for t in range(NT):
                    then(dve.max(top[:, t, :], logit[:, t, :]))
                    then(dve.max_index(index[:, t, :], top[:, t, :], logit[:, t, :]))
                then(dve.tensor_copy(indexf[:, :, :], index[:, :, :]))
                for dst, i in ((fb, 0), (fb2, 1)):
                    then(dve.tensor_tensor(dst[:, :, :], net.iota[:, 0:MIX].unsqueeze(1).broadcast_to([P, NT, MIX]),
                                           indexf[:, :, i:i + 1].broadcast_to([P, NT, MIX]), ALU.is_equal))
                then(dve.tensor_tensor(fb[:, :, :], fb[:, :, :], fb2[:, :, :], ALU.add))
                then(dve.tensor_scalar(anyon[:, :], anyon[:, :], -1.0, 1.0, ALU.mult, ALU.add))
                then(dve.tensor_tensor(fb[:, :, :], fb[:, :, :], anyon[:, :].unsqueeze(2).broadcast_to([P, NT, MIX]), ALU.mult))
                then(dve.tensor_tensor(a[:, :, :], a[:, :, :], fb[:, :, :], ALU.add))
                dve.tensor_tensor(e[:, :, :], g[:, :, :], mx[:, :].unsqueeze(2).broadcast_to([P, NT, MIX]),
                                  ALU.subtract).then_inc(exped, 1)
                dve.wait_ge(exped, 2)
                then(dve.tensor_tensor(e[:, :, :], e[:, :, :], a[:, :, :], ALU.mult))
                then(dve.tensor_reduce(tot[:, :], e[:, :, :], AX.X, ALU.add))
                then(dve.reciprocal(tot[:, :], tot[:, :]))
                then(dve.tensor_tensor(gate[:, :, :], e[:, :, :], tot[:, :].unsqueeze(2).broadcast_to([P, NT, MIX]), ALU.mult))

        weighed = sb("weighed", [P, 2, MIX, MIXD])
        half = MIX // 2
        with net.block() as (block, sem):
            product_done, weighed_done, summed_done = sem("products"), sem("weighed"), sem("summed")
            low_done = sem("low parts of the keys' and the values' matrix")
            jobs = [(t, j) for j in range(3) for t in range(NT)]

            @block.gpsimd
            def _(pool):
                for j in (1, 2):
                    if j == 2:
                        pool.wait_ge(low_done, 1)
                    pool.tensor_tensor(wl[:, j, :], W["qkv"[j]], wh[:, j, :].bitcast(F32), ALU.subtract).then_inc(low_done, 1)

            @block.tensor
            def _(pe):
                for n, (t, j) in enumerate(jobs):
                    if n >= 4:
                        pe.wait_ge(weighed_done, 2 * (n - 3))
                    if j and t == 0:
                        pe.wait_ge(low_done, j)
                    for h in range(2):
                        for c in range(NC):
                            at = c * MIX * MIXD + h * half * MIXD
                            for i, (src, w) in enumerate(((0, wh), (0, wl), (1, wh))):
                                mm = pe.matmul(net.psum[:, 2 * (n % 4) + h, :], parts[src][:, c, t * P:(t + 1) * P],
                                               w[:, j, at:at + half * MIXD], start=c == 0 and i == 0, stop=c == 1 and i == 2)
                        mm.then_inc(product_done, 1)

            @block.vector
            def _(dve):
                for n, (t, j) in enumerate(jobs):
                    for h in range(2):
                        dve.wait_ge(product_done, 2 * n + h + 1)
                        dve.tensor_tensor(weighed[:, n % 2, h * half:(h + 1) * half, :],
                                          net.psum[:, 2 * (n % 4) + h, :].rearrange("p (e d) -> p e d", d=MIXD),
                                          gate[:, t, h * half:(h + 1) * half].unsqueeze(2).broadcast_to([P, half, MIXD]),
                                          ALU.mult).then_inc(weighed_done, 1)
                    dve.wait_ge(weighed_done, 2 * n + 2)
                    dve.tensor_reduce(qkv[:, t, j, :], weighed[:, n % 2, :, :].rearrange("p e d -> p d e"), AX.X, ALU.add)\
                       .then_inc(summed_done, 1)
        projecting.close()
        qk = lasting("qk", [MIXD, 2, T])
        products(net, [Product("act", MIXD, T, turned([qkv[:, t, j, :] for t in range(NT)], net.ident), qk[:, j, :],
                               ("act", ACT.Copy, None, MIXD ** -0.5 if j == 0 else 1.0)) for j in range(2)])
        attn = lasting("attn", [P, NT, MIXD])

        def finish(dve, t, ps, inverse):
            return dve.tensor_scalar(attn[:, t, :], ps, inverse, None, ALU.mult)
        wide_attention(net, [qk[:, 0, :]], [qk[:, 1, :]], lambda c: qkv[:, c, 2, :], MIXD, True, finish)
        mixed = lasting("mixed", [P, 2, MIX, MIXD])
        mixed_c = lasting("mixed_c", [P, 8, T])
        with net.block() as (block, sem):
            mixed_done, turned_done, copied_done = sem("mixed"), sem("transposed"), sem("copied")

            @block.vector
            def _(dve):
                for t in range(NT):
                    if t >= 2:
                        dve.wait_ge(turned_done, 2 * (t - 1))
                    dve.tensor_tensor(mixed[:, t % 2, :, :], attn[:, t, :].unsqueeze(1).broadcast_to([P, MIX, MIXD]),
                                      gate[:, t, :].unsqueeze(2).broadcast_to([P, MIX, MIXD]), ALU.mult).then_inc(mixed_done, 1)

            @block.tensor
            def _(pe):
                for t in range(NT):
                    pe.wait_ge(mixed_done, t + 1)
                    flat = mixed[:, t % 2, :, :].rearrange("p e d -> p (e d)")
                    for h in range(2):
                        for c in range(4):
                            mm = pe.transpose(net.psum[:, 2 * t + h, c * P:(c + 1) * P],
                                              flat[:, (4 * h + c) * P:(4 * h + c + 1) * P], net.ident)
                        mm.then_inc(turned_done, 1)

            @block.scalar
            def _(act):
                for t in range(NT):
                    for h in range(2):
                        act.wait_ge(turned_done, 2 * t + h + 1)
                        act.activation(mixed_c[:, 4 * h:4 * h + 4, t * P:(t + 1) * P],
                                       net.psum[:, 2 * t + h, :].rearrange("p (c n) -> p c n", c=4), ACT.Copy)\
                           .then_inc(copied_done, 1)
        add_output(net, x, mixed_c, 8, P, W["o"])


def L1_attn(net, W, x, xn, xc, **_):
    narrow_attention(net, W, x, xc, xc, HD ** -0.5, True, net.guard8)


def L1_xattn(net, W, x, xn, xc, cc, **_):
    with ExitStack() as ctx:
        q = net.sbuf("q", [P, NC, T], ctx=ctx)
        k = net.sbuf("k", [P, NC, T], ctx=ctx)
        v = net.sbuf("v", [P, NT, D], ctx=ctx)
        o = net.sbuf("o", [P, NC, D, 2], ctx=ctx)
        table = []
        for c in range(NC):
            table.append(cols_out("dve", W["wq"], D, xc, c * P, q[:, c, :], ("scalar", W["bq"][:, c:c + 1], D ** -0.5, ALU.add, ALU.mult)))
            table.append(cols_out("act", W["wk"], D, cc, c * P, k[:, c, :], ("act", ACT.Identity, W["bk"][:, c:c + 1], 1.0)))
        table += [rows_out(alternate(t), cc, t, W["wv"], D, 0, D, v[:, t, :], copied(alternate(t)), W["bv"]) for t in range(NT)]
        products(net, table)

        def finish(dve, t, ps, inverse):
            return dve.tensor_scalar(o[:, t % 2, :, t // 2], ps, inverse, None, ALU.mult)
        wide_attention(net, [q[:, c, :] for c in range(NC)], [k[:, c, :] for c in range(NC)],
                       lambda c: v[:, c, :], D, False, finish)
        add_output(net, x, o[:, :, :, :].rearrange("p c f r -> p c (f r)"), NC, P, W["wo"])


def ternary(net, W):
    with ExitStack() as ctx:
        part = net.sbuf("part", [P, 2], ctx=ctx)
        gamma = net.sbuf("gamma", [P, 2], ctx=ctx)
        edge = net.sbuf("edge", [P, 2, 2], ctx=ctx)
        low = net.sbuf("low", [P, F * D // P], ctx=ctx)
        with net.block() as (block, sem):
            step, sum_done = sem("step"), sem("sum over partitions")

            @block.tensor
            def _(pe):
                pe.wait_ge(step, 2)
                pe.matmul(net.psum[:, 0, 0:2], net.ones_pp, part[:, :], start=True, stop=True).then_inc(sum_done, 1)

            @block.vector
            def _(dve):
                n = 0

                def then(ins):
                    nonlocal n
                    n += 1
                    ins.then_inc(step, 1)
                    dve.wait_ge(step, n)
                for i, w in enumerate((W["fc"], W["proj"])):
                    then(dve.tensor_reduce(part[:, i:i + 1], w, AX.X, ALU.add, apply_absolute_value=True))
                dve.wait_ge(sum_done, 1)
                then(dve.tensor_scalar(gamma[:, :], net.psum[:, 0, 0:2], 1.0 / (F * D), 1e-6, ALU.mult, ALU.add))
                then(dve.tensor_scalar(edge[:, 0, :], gamma[:, :], 0.5, None, ALU.mult))
                then(dve.tensor_scalar(edge[:, 1, :], gamma[:, :], -0.5, None, ALU.mult))
                for i, w in enumerate((W["fc"], W["proj"])):
                    then(dve.tensor_scalar(low[:, :], w, edge[:, 1, i:i + 1], None, ALU.is_lt))
                    then(dve.scalar_tensor_tensor(out=w, in0=w, scalar=edge[:, 0, i:i + 1], in1=low[:, :],
                                                  op0=ALU.is_gt, op1=ALU.subtract))


def L1_ffn(net, W, x, xn, parts, **_):
    with ExitStack() as ctx:
        fc, proj = (net.sbuf(name, [P, F * D // P], F32R, ctx=ctx) for name in ("fc", "proj"))
        with net.block() as (block, sem):
            @block.scalar
            def _(act):
                for to, w in ((fc, W["fc"]), (proj, W["proj"])):
                    act.activation(to[:, 0:F], w[:, 0:F], ACT.Copy)

            @block.vector
            def _(dve):
                for to, w in ((fc, W["fc"]), (proj, W["proj"])):
                    dve.tensor_copy(to[:, F:], w[:, F:])
        h = net.sbuf("h", [P, NT, F], ctx=ctx)
        hc = net.sbuf("hc", [P, F // P, T], ctx=ctx)
        hh, hl = (net.sbuf(f"hc_{part}", [P, F // P, T], F32R, ctx=ctx) for part in ("high", "low"))
        table = []
        for t in range(NT):
            for half in range(2):
                terms = [(part[:, k, t * P:(t + 1) * P], fc[:, k * F + half * BANK:k * F + (half + 1) * BANK])
                         for k in range(NC) for part in parts]
                table.append(Product("act", P, BANK, summed(terms), h[:, t, half * BANK:(half + 1) * BANK],
                                     ("act", ACT.Gelu, None, 1.0)))
        products(net, table)
        stats = net.sbuf("stats", [P, NT, 2, 6], ctx=ctx)
        mv = net.sbuf("mean_var", [P, NT, 2], ctx=ctx)
        rstd = net.sbuf("rstd", [P, NT], ctx=ctx)
        with net.block() as (block, sem):
            stats_done, mv_done, rstd_done, guarded = sem("stats"), sem("mean and variance"), sem("1/std"), sem("variance + eps")

            @block.gpsimd
            def _(pool):
                pool.wait_ge(mv_done, NT)
                pool.tensor_scalar(rstd[:, :], mv[:, :, 1], LN_EPS, None, ALU.add, ALU.bypass).then_inc(guarded, 1)
                pool.wait_ge(guarded, 1)
                pool.tensor_tensor(rstd[:, :], rstd[:, :], net.minus_half[:, 0:NT], ALU.pow).then_inc(rstd_done, 1)

            @block.vector
            def _(dve):
                for t in range(NT):
                    for half in range(2):
                        dve.bn_stats(stats[:, t, half, :], h[:, t, half * BANK:(half + 1) * BANK]).then_inc(stats_done, 1)
                for t in range(NT):
                    dve.wait_ge(stats_done, 2 * t + 2)
                    dve.bn_aggr(mv[:, t, :], stats[:, t, :, :].rearrange("p a b -> p (a b)")).then_inc(mv_done, 1)
                dve.wait_ge(rstd_done, 1)
                for t in range(NT):
                    dve.tensor_scalar(h[:, t, :], h[:, t, :], mv[:, t, 0:1], rstd[:, t:t + 1], ALU.subtract, ALU.mult)
        chunks = F // P
        with net.block() as (block, sem):
            turned_done, value_done, high_done = sem("transposed"), sem("value"), sem("high part")

            @block.tensor
            def _(pe):
                for c in range(chunks):
                    for t in range(NT):
                        mm = pe.transpose(net.psum[:, c, t * P:(t + 1) * P], h[:, t, c * P:(c + 1) * P], net.ident)
                    mm.then_inc(turned_done, 1)

            @block.scalar
            def _(act):
                for c in range(chunks):
                    act.wait_ge(turned_done, c + 1)
                    act.activation(hc[:, c, :], net.psum[:, c, :], ACT.Identity, bias=W["ln_b"][:, c:c + 1],
                                   scale=W["ln_w"][:, c:c + 1]).then_inc(value_done, 1)

            @block.vector
            def _(dve):
                for c in range(chunks):
                    dve.wait_ge(value_done, c + 1)
                    dve.tensor_copy(hh[:, c, :], hc[:, c, :]).then_inc(high_done, 1)
                    if c % 2:
                        dve.wait_ge(high_done, c + 1)
                        dve.tensor_tensor(hl[:, c, :], hc[:, c, :], hh[:, c, :].bitcast(F32), ALU.subtract)

            @block.gpsimd
            def _(pool):
                for c in range(0, chunks, 2):
                    pool.wait_ge(high_done, c + 1)
                    pool.tensor_tensor(hl[:, c, :], hc[:, c, :], hh[:, c, :].bitcast(F32), ALU.subtract)
        table = []
        for t in range(NT):
            terms = [(part[:, c, t * P:(t + 1) * P], proj[:, c * D:(c + 1) * D]) for c in range(chunks) for part in (hh, hl)]
            table.append(Product("dve", P, D, summed(terms), x[:, t, :], ("tensor", x[:, t, :], ALU.add)))
        products(net, table)


def L2_attn(net, W, x, xn, xc, **_):
    with ExitStack() as ctx:
        wide = net.sbuf("wide", [P, NT, 2, D], ctx=ctx)
        stats = net.sbuf("stats", [P, NT, 2, 6], ctx=ctx)
        mv = net.sbuf("mean_var", [P, NT, 2, 2], ctx=ctx)
        rstd = net.sbuf("rstd", [P, NT, 2], ctx=ctx)
        products(net, [rows_out(alternate(t), xc, t, W["wqkv"], 3 * D, 0, 2 * D, wide[:, t, :, :].rearrange("p a b -> p (a b)"),
                                copied(alternate(t)), W["bqkv"]) for t in range(NT)])
        with net.block() as (block, sem):
            stats_done, mv_done, rstd_done, scaled = sem("stats"), sem("mean and variance"), sem("1/std"), sem("variance scaled")

            @block.gpsimd
            def _(pool):
                pool.wait_ge(mv_done, 2 * NT)
                pool.tensor_scalar(rstd[:, :, :], mv[:, :, :, 1], D / (D - 1), None, ALU.mult, ALU.bypass).then_inc(scaled, 1)
                pool.wait_ge(scaled, 1)
                pool.tensor_tensor(rstd[:, :, :], rstd[:, :, :], net.half[:, 0:2 * NT].rearrange("p (t j) -> p t j", j=2),
                                   ALU.pow).then_inc(rstd_done, 1)

            @block.vector
            def _(dve):
                for t in range(NT):
                    for j in range(2):
                        dve.bn_stats(stats[:, t, j, :], wide[:, t, j, :]).then_inc(stats_done, 1)
                for t in range(NT):
                    for j in range(2):
                        dve.wait_ge(stats_done, 2 * t + j + 1)
                        dve.bn_aggr(mv[:, t, j, :], stats[:, t, j, :]).then_inc(mv_done, 1)
                dve.wait_ge(rstd_done, 1)
                dve.tensor_scalar(rstd[:, :, :], rstd[:, :, :], 1e-6, None, ALU.add).then_inc(rstd_done, 1)
                dve.wait_ge(rstd_done, 2)
                dve.reciprocal(rstd[:, :, :], rstd[:, :, :]).then_inc(rstd_done, 1)
                dve.wait_ge(rstd_done, 3)
                for t in range(NT):
                    for j in range(2):
                        dve.tensor_scalar(wide[:, t, j, :], wide[:, t, j, :], mv[:, t, j, 0:1], rstd[:, t, j:j + 1],
                                          ALU.subtract, ALU.mult)

        def jobs(j, c):
            gain, offset = (W["gk"], W["hk"]) if j else (W["gq"], W["hq"])
            cols = turned([wide[:, t, j, c * P:(c + 1) * P] for t in range(NT)], net.ident)
            return cols, None, (gain[:, c:c + 1], offset[:, c:c + 1])
        narrow_attention(net, W, x, xc, xc, 1.0, True, net.guard6, linear=True, jobs=jobs)


def L2_xattn(net, W, x, xn, xc, cc, raw_mask, mask_loaded, room, **_):
    with ExitStack() as ctx:
        sb = lambda name, shape, dt=F32: net.sbuf(name, shape, dt, ctx=ctx)
        mrows, mcols = sb("mrows", [P, NT, T], BF16), sb("mcols", [P, NT, T], BF16)
        qa, ka = sb("qa", [P, ROUND, T], F32R), sb("ka", [P, ROUND, T], F32R)
        qb, kb = sb("qb", [P, ROUND, T], F32R), sb("kb", [P, ROUND, T], F32R)
        v = sb("v", [P, NT, ROUND, DK + 1])
        o, oc = (room[:, i * NT * F:(i + 1) * NT * F] for i in (1, 0))
        o, oc = o.rearrange("p (t h d) -> p t h d", t=NT, h=H), oc.rearrange("p (c n) -> p c n", n=T)
        low, up = slice(0, DK), slice(DK, P)
        products_of_heads = ROUND
        for r in range(H // ROUND):
            first = r * ROUND
            with net.block() as (block, sem):
                product_done, high_done, low_done = sem("product"), sem("a head's high part"), sem("a pair's low parts")
                values_done, zeroed, extra_zeroed = sem("values product"), sem("partitions for -max zeroed"), sem("k's zeros")

                @block.gpsimd
                def _(pool):
                    for j, extra in enumerate((up, low)):
                        pool.memset(qb[extra, j:ROUND:2, :].bitcast(F32), 0.0).then_inc(zeroed, 1)
                    pool.wait_ge(zeroed, 2)
                    if r == 0:
                        for j, extra in enumerate((up, low)):
                            pool.memset(kb[extra, j:ROUND:2, :].bitcast(F32), 0.0).then_inc(extra_zeroed, 1)
                        pool.wait_ge(extra_zeroed, 2)
                        for j, extra in enumerate((up, low)):
                            pool.memset(kb[extra.start:extra.start + 2, j:ROUND:2, :].bitcast(F32), 1.0).then_inc(extra_zeroed, 1)
                        pool.wait_ge(extra_zeroed, 4)
                        pool.memset(v[:, :, :, DK:DK + 1], 1.0).then_inc(extra_zeroed, 1)
                        pool.wait_ge(mask_loaded, 32)
                        pool.wait_ge(extra_zeroed, 5)
                        pool.tensor_scalar(mcols[:, :, :], raw_mask[:, 1, :, :], 0, MASKED, ALU.is_equal, ALU.mult)

                @block.tensor
                def _(pe):
                    for n in range(products_of_heads):
                        p, is_k = first // 2 + n // 2, n % 2
                        w, src = (W["wk"], cc) if is_k else (W["wq"], xc)
                        for c in range(NC):
                            at = c * F + p * P
                            mm = pe.matmul(net.psum[:, n, :], w[:, at:at + P], src[:, c, :], start=c == 0, stop=c == 1)
                        mm.then_inc(product_done, 1)
                    for t in range(NT):
                        pe.wait_ge(low_done, t + 1)
                        for c in range(NC):
                            at = c * F + first * DK
                            mm = pe.matmul(net.psum[:, t, 0:ROUND * DK], cc[:, c, t * P:(t + 1) * P],
                                           W["wv"][:, at:at + ROUND * DK], start=c == 0, stop=c == 1)
                        mm.then_inc(values_done, 1)

                @block.scalar
                def _(act):
                    for n in range(products_of_heads):
                        is_k, p = n % 2, first // 2 + n // 2
                        bias = (W["bk"] if is_k else W["bq"])[:, p:p + 1]
                        act.wait_ge(product_done, n + 1)
                        for j, (own, other) in enumerate(((low, up), (up, low))):
                            u = n // 2 * 2 + j
                            if is_k:
                                act.activation(ka[other, u, :], net.psum[own, n, :], ACT.Identity, bias=bias[own, :])
                            act.activation((ka if is_k else qb)[own, u, :], net.psum[own, n, :], ACT.Identity,
                                           bias=bias[own, :]).then_inc(high_done, 1)

                @block.vector
                def _(dve):
                    for n in range(products_of_heads):
                        is_k, p = n % 2, first // 2 + n // 2
                        bias = (W["bk"] if is_k else W["bq"])[:, p:p + 1]
                        dve.wait_ge(product_done, n + 1)
                        for j, (own, other) in enumerate(((low, up), (up, low))):
                            u = n // 2 * 2 + j
                            high, to = (ka, kb[own, u, :]) if is_k else (qb, qa[other, u, :])
                            dve.wait_ge(high_done, 2 * n + j + 1)
                            if not is_k:
                                dve.tensor_copy(qa[own, u, :], qb[own, u, :].bitcast(F32))
                            ins = dve.scalar_tensor_tensor(out=to, in0=net.psum[own, n, :], scalar=bias[own, :],
                                                           in1=high[own, u, :].bitcast(F32), op0=ALU.add, op1=ALU.subtract)
                        ins.then_inc(low_done, 1)
                    bias = W["bv"][:, first * DK:(first + ROUND) * DK].rearrange("p (h d) -> p h d", h=ROUND)
                    for t in range(NT):
                        dve.wait_ge(values_done, t + 1)
                        dve.tensor_tensor(v[:, t, :, 0:DK], net.psum[:, t, 0:ROUND * DK].rearrange("p (h d) -> p h d", h=ROUND),
                                          bias, ALU.add)
                    if r == 0:
                        dve.wait_ge(mask_loaded, 32)
                        dve.tensor_scalar(mrows[:, :, :], raw_mask[:, 0, :, :], 0, MASKED, ALU.is_equal, ALU.mult)
            many_heads(net, lambda h: [(ka[:, h, :], qa[:, h, :]), (kb[:, h, :], qb[:, h, :])],
                       lambda i: (qb[:, i, :], low if i % 2 else up), lambda kt, u: v[:, kt, u, :], DK,
                       o[:, :, first:first + ROUND, :], ROUND // 2, DK ** -0.5, mask_rows=mrows, mask_cols=mcols)
        flat = o.rearrange("p t h d -> p t (h d)")
        products(net, [Product(alternate(c), P, T, turned([flat[:, t, c * P:(c + 1) * P] for t in range(NT)], net.ident),
                               oc[:, c, :], copied(alternate(c))) for c in range(F // P)])
        add_output(net, x, oc, F // P, P, W["wo"])


def L2_ffn(net, W, x, xn, xc, w1, w2, arena, **_):
    with ExitStack() as ctx:
        sb = lambda name, shape, dt=F32: net.sbuf(name, shape, dt, ctx=ctx)
        base, half = pack_width("L2_ffn"), EXPERT // 2
        up_w, down_w = ([arena[:, at + half * i:at + half * (i + 1)] for i in range(2)] for at in (base, base + EXPERT))
        xr, xrc = sb("xr", [P, NT, D]), sb("xrc", [P, NC, T])
        sq, ms = sb("sq", [P, D]), sb("ms", [P, NT])
        logit, top, index, indexf = sb("logit", [P, NT, 8]), sb("top", [P, NT, 8]), sb("index", [P, NT, 8], U32), sb("indexf", [P, NT])
        e, tot, gate, gate_c = sb("e", [P, NT, 8]), sb("tot", [P, NT]), sb("gate", [P, NT, 8]), sb("gate_c", [EXPERTS, T])
        with net.block() as (block, sem):
            step, mean_done, root_done = sem("step"), sem("mean square"), sem("1/root")

            @block.sync
            def _(sp):
                for n in range(2):
                    sp.dma_start(up_w[n], w1[n]).then_inc(net.up_loaded[n], 16)
                    sp.dma_start(down_w[n], w2[n]).then_inc(net.down_loaded[n], 16)

            @block.gpsimd
            def _(pool):
                pool.wait_ge(mean_done, 1)
                pool.tensor_tensor(ms[:, :], ms[:, :], net.minus_half[:, 0:NT], ALU.pow).then_inc(root_done, 1)

            @block.vector
            def _(dve):
                n = 0

                def then(ins):
                    nonlocal n
                    n += 1
                    ins.then_inc(step, 1)
                    dve.wait_ge(step, n)
                for t in range(NT):
                    then(dve.tensor_tensor_reduce(sq[:, :], xn[:, t, :], xn[:, t, :], 1.0, 0.0, ALU.mult, ALU.add, ms[:, t:t + 1]))
                dve.tensor_scalar(ms[:, :], ms[:, :], 1.0 / D, 1e-6, ALU.mult, ALU.add).then_inc(mean_done, 1)
                dve.wait_ge(root_done, 1)
                for t in range(NT):
                    then(dve.tensor_scalar(xr[:, t, :], xn[:, t, :], ms[:, t:t + 1], None, ALU.mult))
        products(net, [Product("dve", P, T, turned([xr[:, t, c * P:(c + 1) * P] for t in range(NT)], net.ident), xrc[:, c, :],
                               ("scalar", W["rms"][:, c:c + 1], None, ALU.mult, ALU.bypass)) for c in range(NC)])
        products(net, [rows_out("dve", xrc, t, W["gate"], 8, 0, 8, logit[:, t, :], VCOPY) for t in range(NT)])
        with net.block() as (block, sem):
            step, shifted, exped, ready, turned_done = (sem("step"), sem("logits - max"), sem("exp"), sem("gates"),
                                                        sem("gates transposed"))

            @block.vector
            def _(dve):
                n = 0

                def then(ins):
                    nonlocal n
                    n += 1
                    ins.then_inc(step, 1)
                    dve.wait_ge(step, n)
                for t in range(NT):
                    then(dve.max(top[:, t, :], logit[:, t, :]))
                    then(dve.max_index(index[:, t, :], top[:, t, :], logit[:, t, :]))
                dve.tensor_tensor(e[:, :, :], logit[:, :, :], top[:, :, 0:1].broadcast_to([P, NT, 8]),
                                  ALU.subtract).then_inc(shifted, 1)
                then(dve.tensor_copy(indexf[:, :], index[:, :, 0]))
                dve.wait_ge(exped, 1)
                then(dve.tensor_reduce(tot[:, :], e[:, :, :], AX.X, ALU.add))
                then(dve.reciprocal(tot[:, :], tot[:, :]))
                then(dve.tensor_tensor(gate[:, :, :], net.iota[:, 0:8].unsqueeze(1).broadcast_to([P, NT, 8]),
                                       indexf[:, :].unsqueeze(2).broadcast_to([P, NT, 8]), ALU.is_equal))
                dve.tensor_tensor(gate[:, :, :], gate[:, :, :], tot[:, :].unsqueeze(2).broadcast_to([P, NT, 8]), ALU.mult)\
                   .then_inc(ready, 1)
                dve.wait_ge(turned_done, 1)
                dve.tensor_copy(gate_c[:, :], net.psum[0:EXPERTS, 0, :])

            @block.scalar
            def _(act):
                act.wait_ge(shifted, 1)
                act.activation(e[:, :, :], e[:, :, :], ACT.Exp).then_inc(exped, 1)

            @block.tensor
            def _(pe):
                pe.wait_ge(ready, 1)
                for t in range(NT):
                    mm = pe.transpose(net.psum[0:EXPERTS, 0, t * P:(t + 1) * P], gate[:, t, :], net.ident)
                mm.then_inc(turned_done, 1)
        products(net, [Product("dve", P, D, summed([(gate_c[:, t * P:(t + 1) * P], W["b2"][0:EXPERTS, :])]), x[:, t, :],
                               ("tensor", x[:, t, :], ALU.add)) for t in range(NT)])
        experts(net, x, xrc, gate, W["b1"], w1, w2, up_w, down_w)


def experts(net, x, xrc, gate, b1, w1, w2, up_w, down_w):
    units, chunks = 2 * EXPERTS, HIDDEN_CHUNKS // 2
    size = chunks * D
    with ExitStack() as ctx:
        sb = lambda name, shape, dt=F32: net.sbuf(name, shape, dt, ctx=ctx)
        xh, xl = sb("x_high", [P, NC, T], F32R), sb("x_low", [P, NC, T], F32R)
        uh, ul = sb("up_high", [P, 2, size], F32R), sb("up_low", [P, 2, size], F32R)
        dh, dl = sb("down_high", [P, 2, size], F32R), sb("down_low", [P, 2, size], F32R)
        hidden = sb("hidden", [P, chunks, T])
        hh, hl = sb("hidden_high", [P, 2, chunks, T], F32R), sb("hidden_low", [P, 2, chunks, T], F32R)

        def raw_up(u):
            return up_w[u // 2 % 2].rearrange("p (c f) -> p c f", c=NC)[:, :, u % 2 * F // 2:(u % 2 + 1) * F // 2]

        def raw_down(u):
            return down_w[u // 2 % 2][:, u % 2 * size:(u % 2 + 1) * size]

        def halves(part):
            return part.rearrange("p (c f) -> p c f", c=NC)

        with net.block() as (block, sem):
            xh_done, xl_done, up_done, silu_done = sem("x high"), sem("x low"), sem("up product"), sem("silu")
            hh_done, hl_done, down_done, added = sem("hidden high"), sem("hidden low"), sem("down product"), sem("added to x")
            uh_done, ul_done, dh_done, dl_done = sem("up high"), sem("up low"), sem("down high"), sem("down low")

            @block.sync
            def _(sp):
                for n in range(2, EXPERTS):
                    sp.wait_ge(ul_done, 2 * (n - 1))
                    sp.dma_start(up_w[n % 2], w1[n]).then_inc(net.up_loaded[n % 2], 16)
                    sp.wait_ge(dl_done, 2 * (n - 1))
                    sp.dma_start(down_w[n % 2], w2[n]).then_inc(net.down_loaded[n % 2], 16)

            @block.tensor
            def _(pe):
                def up(u):
                    pe.wait_ge(uh_done, u + 1)
                    pe.wait_ge(ul_done, u + 1)
                    for f in range(chunks):
                        m = u * chunks + f
                        if m >= 4:
                            pe.wait_ge(silu_done, m - 3)
                        for c in range(NC):
                            at = c * F // 2 + f * P
                            for i, (w, src) in enumerate(((uh, xh), (ul, xh), (uh, xl))):
                                mm = pe.matmul(net.psum[:, m % 4, :], w[:, u % 2, at:at + P], src[:, c, :],
                                               start=c == 0 and i == 0, stop=c == 1 and i == 2)
                        mm.then_inc(up_done, 1)

                def down(u):
                    pe.wait_ge(hh_done, u + 1)
                    pe.wait_ge(hl_done, u + 1)
                    pe.wait_ge(dh_done, u + 1)
                    pe.wait_ge(dl_done, u + 1)
                    for t in range(NT):
                        if u % 2 == 0 and u:
                            pe.wait_ge(added, (u // 2 - 1) * NT + t + 1)
                        for f in range(chunks):
                            for i, (h, w) in enumerate(((hh, dh), (hl, dh), (hh, dl))):
                                mm = pe.matmul(net.psum[:, 4 + t, 0:D], h[:, u % 2, f, t * P:(t + 1) * P],
                                               w[:, u % 2, f * D:(f + 1) * D], start=u % 2 == 0 and f == 0 and i == 0,
                                               stop=u % 2 == 1 and f == chunks - 1 and i == 2)
                        mm.then_inc(down_done, 1)
                pe.wait_ge(xh_done, 1)
                pe.wait_ge(xl_done, 1)
                up(0)
                for u in range(units):
                    if u + 1 < units:
                        up(u + 1)
                    down(u)

            @block.scalar
            def _(act):
                def up_high(u):
                    act.wait_ge(net.up_loaded[u // 2 % 2], 16 * (u // 4 + 1))
                    if u >= 2:
                        act.wait_ge(up_done, chunks * (u - 1))
                    act.activation(halves(uh[:, u % 2, :]), raw_up(u), ACT.Copy).then_inc(uh_done, 1)

                def down_high(u):
                    act.wait_ge(net.down_loaded[u // 2 % 2], 16 * (u // 4 + 1))
                    if u >= 2:
                        act.wait_ge(down_done, NT * (u - 1))
                    act.activation(dh[:, u % 2, :], raw_down(u), ACT.Copy).then_inc(dh_done, 1)
                up_high(0)
                up_high(1)
                down_high(0)
                for u in range(units):
                    if u:
                        act.wait_ge(hl_done, u)
                    for f in range(chunks):
                        m = u * chunks + f
                        act.wait_ge(up_done, m + 1)
                        act.activation(hidden[:, f, :], net.psum[:, m % 4, :], ACT.Silu,
                                       bias=b1[:, m:m + 1]).then_inc(silu_done, 1)
                    if u >= 2:
                        act.wait_ge(down_done, NT * (u - 1))
                    act.wait_ge(silu_done, chunks * (u + 1))
                    act.activation(hh[:, u % 2, :, :], hidden[:, :, :], ACT.Copy).then_inc(hh_done, 1)
                    if u + 2 < units:
                        up_high(u + 2)
                    if u + 1 < units:
                        down_high(u + 1)

            @block.gpsimd
            def _(pool):
                def up_low(u):
                    pool.wait_ge(uh_done, u + 1)
                    if u == 1:
                        pool.wait_ge(ul_done, 1)
                    if u >= 2:
                        pool.wait_ge(dl_done, u - 1)
                    pool.tensor_tensor(halves(ul[:, u % 2, :]), raw_up(u), halves(uh[:, u % 2, :]).bitcast(F32), ALU.subtract)\
                        .then_inc(ul_done, 1)

                def down_low(u):
                    pool.wait_ge(dh_done, u + 1)
                    pool.wait_ge(ul_done, min(u + 2, units))
                    pool.tensor_tensor(dl[:, u % 2, :], raw_down(u), dh[:, u % 2, :].bitcast(F32), ALU.subtract)\
                        .then_inc(dl_done, 1)
                up_low(0)
                for u in range(units):
                    if u + 1 < units:
                        up_low(u + 1)
                    down_low(u)

            def add(dve, n):
                for t in range(NT):
                    m = n * NT + t
                    dve.wait_ge(down_done, 2 * n * NT + NT + t + 1)
                    if n:
                        dve.wait_ge(added, m - NT + 1)
                    dve.scalar_tensor_tensor(out=x[:, t, :], in0=net.psum[:, 4 + t, 0:D], scalar=gate[:, t, n:n + 1],
                                             in1=x[:, t, :], op0=ALU.mult, op1=ALU.add).then_inc(added, 1)

            @block.vector
            def _(dve):
                dve.tensor_copy(xh[:, :, :], xrc[:, :, :]).then_inc(xh_done, 1)
                dve.wait_ge(xh_done, 1)
                dve.tensor_tensor(xl[:, :, :], xrc[:, :, :], xh[:, :, :].bitcast(F32), ALU.subtract).then_inc(xl_done, 1)
                for u in range(units):
                    dve.wait_ge(hh_done, u + 1)
                    if u >= 2:
                        dve.wait_ge(down_done, NT * (u - 1))
                    dve.tensor_tensor(hl[:, u % 2, :, :], hidden[:, :, :], hh[:, u % 2, :, :].bitcast(F32), ALU.subtract)\
                       .then_inc(hl_done, 1)
                    if u % 2 == 0 and u:
                        add(dve, u // 2 - 1)
                add(dve, EXPERTS - 1)


def L3_attn(net, W, x, xn, xc, **_):
    def jobs(j, c):
        w, wr = (W["wk"], W["wkr"]) if j else (W["wq"], W["wqr"])
        return chunk_terms(w, xc, c), chunk_terms(wr, xc, c), None
    narrow_attention(net, W, x, xc, xc, HD ** -0.5, True, None, jobs=jobs, rope=(W["cos"], W["sin"]))


def L3_xattn(net, W, x, xn, xc, ct, cc, kmask, b, **_):
    with ExitStack() as ctx:
        sb = lambda name, shape, dt=F32: net.sbuf(name, shape, dt, ctx=ctx)
        q, k = sb("q", [P, NC, T]), sb("k", [P, NC, T])
        raw, keep, gone = sb("raw", [P, T // 4], I32), sb("keep", [P, T]), sb("gone", [P, T])
        table = []
        for c in range(NC):
            table.append(cols_out("act", W["w"], D, xc, c * P, q[:, c, :], ("act", ACT.Relu, W["b"][:, c:c + 1], 1.0)))
            table.append(cols_out("dve", W["w"], D, cc, c * P, k[:, c, :], ("scalar", W["b"][:, c:c + 1], 0.0, ALU.add, ALU.max)))
        products(net, table)
        with net.block() as (block, sem):
            loaded = sem("mask")

            @block.sync
            def _(sp):
                sp.dma_start(raw[:, :], kmask[b].partition_broadcast(P)).then_inc(loaded, 16)

            @block.vector
            def _(dve):
                for c in range(NC):
                    dve.tensor_scalar(k[:, c, :], k[:, c, :], W["d"][:, c:c + 1], None, ALU.mult)
                dve.wait_ge(loaded, 16)
                dve.tensor_scalar(keep[:, :], raw[:, :].bitcast(U8), 0, None, ALU.is_equal)
                dve.tensor_scalar(gone[:, :], raw[:, :].bitcast(U8), 0, MASKED, ALU.not_equal, ALU.mult)

        def finish(dve, t, ps, inverse):
            return dve.scalar_tensor_tensor(out=x[:, t, :], in0=ps, scalar=inverse, in1=x[:, t, :],
                                            op0=ALU.mult, op1=ALU.add)
        wide_attention(net, [q[:, c, :] for c in range(NC)], [k[:, c, :] for c in range(NC)],
                       lambda c: ct[:, c, :], D, False, finish, keep=keep[:, :], gone=gone[:, :])


def L3_ffn(net, W, x, xn, xc, **_):
    with ExitStack() as ctx:
        sb = lambda name, shape, dt=F32: net.sbuf(name, shape, dt, ctx=ctx)
        hc, sim = sb("hc", [SLOTD, 1, T]), sb("sim", [P, NT, SLOTS])
        top, index, indexf = sb("top", [P, NT, 8]), sb("index", [P, NT, 8], U32), sb("indexf", [P, NT, 8])
        e, tot, gate, hit = sb("e", [P, NT, 4]), sb("tot", [P, NT]), sb("gate", [P, NT, SLOTS]), sb("hit", [P, NT, SLOTS])
        parts, gate_c, spread = sb("parts", [P, NT, 2, SLOTS]), sb("gate_c", [P, T], F32R), sb("spread", [P, SLOTS * SLOTD], F32R)
        products(net, [Product("act", SLOTD, T, summed([(W["hash"][:, c * SLOTD:(c + 1) * SLOTD], xc[:, c, :]) for c in range(NC)]),
                               hc[:, 0, :], COPY)])
        products(net, [Product("act", P, SLOTS, summed([(hc[:, 0, t * P:(t + 1) * P], W["keys"][0:SLOTD, :])]), sim[:, t, :], COPY)
                       for t in range(NT)])
        with net.block() as (block, sem):
            step, shifted, exped, ready, turned_done = (sem("step"), sem("values - max"), sem("exp"), sem("gates"),
                                                        sem("gates transposed"))
            spread_done = sem("the matrix that spreads the gates")

            @block.vector
            def _(dve):
                n = 0

                def then(ins):
                    nonlocal n
                    n += 1
                    ins.then_inc(step, 1)
                    dve.wait_ge(step, n)
                for t in range(NT):
                    then(dve.max(top[:, t, :], sim[:, t, :]))
                    then(dve.max_index(index[:, t, :], top[:, t, :], sim[:, t, :]))
                dve.tensor_tensor(e[:, :, :], top[:, :, 0:4], top[:, :, 0:1].broadcast_to([P, NT, 4]),
                                  ALU.subtract).then_inc(shifted, 1)
                then(dve.tensor_copy(indexf[:, :, :], index[:, :, :]))
                dve.wait_ge(exped, 1)
                then(dve.tensor_reduce(tot[:, :], e[:, :, :], AX.X, ALU.add))
                then(dve.reciprocal(tot[:, :], tot[:, :]))
                then(dve.tensor_tensor(e[:, :, :], e[:, :, :], tot[:, :].unsqueeze(2).broadcast_to([P, NT, 4]), ALU.mult))
                iota = net.iota[:, :].unsqueeze(1).broadcast_to([P, NT, SLOTS])
                for i in range(4):
                    dst = gate if i == 0 else hit
                    then(dve.tensor_tensor(dst[:, :, :], iota, indexf[:, :, i:i + 1].broadcast_to([P, NT, SLOTS]), ALU.is_equal))
                    then(dve.tensor_tensor(dst[:, :, :], dst[:, :, :], e[:, :, i:i + 1].broadcast_to([P, NT, SLOTS]), ALU.mult))
                    if i:
                        ins = dve.tensor_tensor(gate[:, :, :], gate[:, :, :], hit[:, :, :], ALU.add)
                        then(ins)
                then(dve.tensor_copy(parts[:, :, 0, :].bitcast(F32R), gate[:, :, :]))
                dve.tensor_tensor(parts[:, :, 1, :], gate[:, :, :], parts[:, :, 0, :], ALU.subtract).then_inc(ready, 1)
                dve.wait_ge(turned_done, 1)
                dve.tensor_copy(gate_c[:, :], net.psum[:, 0, :])

            @block.gpsimd
            def _(pool):
                pool.tensor_copy(spread[:, :], W["spread"]).then_inc(spread_done, 1)
                pool.wait_ge(spread_done, 1)
                pool.tensor_tensor(x[:, :, :], x[:, :, :], xn[:, :, :], ALU.add)

            @block.scalar
            def _(act):
                act.wait_ge(shifted, 1)
                act.activation(e[:, :, :], e[:, :, :], ACT.Exp).then_inc(exped, 1)

            @block.tensor
            def _(pe):
                net.keep_warm(pe, 3 * WARM_ROUTER)
                pe.wait_ge(ready, 1)
                for t in range(NT):
                    mm = pe.transpose(net.psum[:, 0, t * P:(t + 1) * P], parts[:, t, :, :].rearrange("p i s -> p (i s)"), net.ident)
                mm.then_inc(turned_done, 1)
        silu = sb("silu", [P, 2, T])
        proj = sb("proj", [P, SLOTS * SLOTD // P, T])
        chunks = SLOTS * SLOTD // P
        with net.block() as (block, sem):
            down_done, spread_done, silu_done, weighed = sem("down product"), sem("gates spread"), sem("silu"), sem("weighed")

            @block.tensor
            def _(pe):
                for n in range(chunks):
                    if n >= 2:
                        pe.wait_ge(weighed, n - 1)
                    for c in range(NC):
                        at = c * SLOTS * SLOTD + n * P
                        mm = pe.matmul(net.psum[:, n % 2, :], W["down"][:, at:at + P], xc[:, c, :], start=c == 0, stop=c == 1)
                    mm.then_inc(down_done, 1)
                    pe.matmul(net.psum[:, 2 + n % 2, :], spread[:, n * P:(n + 1) * P], gate_c[:, :],
                              start=True, stop=True).then_inc(spread_done, 1)

            @block.scalar
            def _(act):
                for n in range(chunks):
                    act.wait_ge(down_done, n + 1)
                    if n >= 2:
                        act.wait_ge(weighed, n - 1)
                    act.activation(silu[:, n % 2, :], net.psum[:, n % 2, :], ACT.Silu).then_inc(silu_done, 1)

            @block.vector
            def _(dve):
                for n in range(chunks):
                    dve.wait_ge(silu_done, n + 1)
                    dve.wait_ge(spread_done, n + 1)
                    dve.tensor_tensor(proj[:, n, :], silu[:, n % 2, :], net.psum[:, 2 + n % 2, :], ALU.mult).then_inc(weighed, 1)
        table = []
        for t in range(NT):
            terms = [(proj[:, c, t * P:(t + 1) * P], W["up"][:, c * D:(c + 1) * D]) for c in range(chunks)]
            table.append(Product("dve", P, D, summed(terms), x[:, t, :], ("stt", W["scale"], x[:, t, :], ALU.mult, ALU.add)))
        products(net, table)


BODIES = dict(L0_attn=L0_attn, L0_xattn=L0_xattn, L0_ffn=L0_ffn, L1_attn=L1_attn, L1_xattn=L1_xattn, L1_ffn=L1_ffn,
              L2_attn=L2_attn, L2_xattn=L2_xattn, L2_ffn=L2_ffn, L3_attn=L3_attn, L3_xattn=L3_xattn, L3_ffn=L3_ffn)


def decoder(nc, x_d, ctx_d, mask_d, mask_t_d, kmask_d, w1_d, w2_d, consts_d, select_d, packs_d, ternary_d, out_d, batches=B, sublayers=SUBLAYERS):
    with ExitStack() as ctx:
        net = Net(nc, ctx)
        spots, width = offsets(CONSTS)
        consts = net.sbuf("consts", [P, width])
        (net.ident, net.causal, net.gather, net.scatter, net.guard8, net.guard6, net.ones_k, net.iota, net.ones, net.half, net.minus_half,
         net.causal_cols) = (consts[:, at:at + n] for at, n in spots.values())
        net.ones_pp = net.ones
        narrow = net.sbuf("narrow", [P, 3, P], BF16)
        net.ident16, net.causal16, net.causal_cols16 = (narrow[:, i, :] for i in range(3))
        arenas = [net.sbuf(f"arena{i}", [P, ARENAS[i]]) for i in range(2)]
        x, xn, xc = net.sbuf("x", [P, NT, D]), net.sbuf("xn", [P, NT, D]), net.sbuf("xc", [P, NC, T])
        ct, cc = net.sbuf("ct", [P, NT, D]), net.sbuf("cc", [P, NC, T])
        net.select = net.sbuf("select", [P, 16, P], F32R)
        spots, width = offsets(WIDTHS["L1_ffn"])
        ternary_w = {name: arenas[1][:, at:at + n] for name, (at, n) in spots.items()}
        first_arena = arenas[SUBLAYERS.index(sublayers[0]) % 2]
        first, first_loaded = packs_d[sublayers[0]], ctx.enter_context(nc.semaphore("first_weights_loaded"))
        loaded = [ctx.enter_context(nc.semaphore(f"weights_loaded_{i}")) for i in range(2)]
        mask_loaded = ctx.enter_context(nc.semaphore("mask_loaded"))
        room = arenas[0][:, pack_width("L2_ffn"):pack_width("L2_ffn") + 2 * EXPERT]
        raw_mask = room[:, 0:2 * NT * T].bitcast(I32).rearrange("p (i t k) -> p i t k", i=2, t=NT)
        net.up_loaded = [ctx.enter_context(nc.semaphore(f"experts_up_loaded_{i}")) for i in range(2)]
        net.down_loaded = [ctx.enter_context(nc.semaphore(f"experts_down_loaded_{i}")) for i in range(2)]
        x_loaded, ctx_loaded = (ctx.enter_context(nc.semaphore(name)) for name in ("x_loaded", "context_loaded"))
        x_next = room[:, -NT * D:].rearrange("p (t d) -> p t d", t=NT)

        def start_fetches(b):
            return [(x_loaded, x_next, x_d[b].rearrange("(t p) d -> p t d", p=P)),
                    (ctx_loaded, ct[:, :, :], ctx_d[b].rearrange("(t p) d -> p t d", p=P))]

        with net.block() as (block, sem):
            loaded_consts, w_loaded = sem("constants"), sem("L1_ffn's weights")
            raw_select = arenas[1][:, -16 * P:].rearrange("p (i m) -> p i m", m=P)

            @block.sync
            def _(sp):
                sp.dma_start(consts[:, :], consts_d).then_inc(loaded_consts, 16)
                sp.dma_start(raw_select, select_d).then_inc(loaded_consts, 16)
                sp.dma_start(arenas[1][:, 0:width], packs_d["L1_ffn"]).then_inc(w_loaded, 16)
                sp.dma_start(first_arena[:, 0:first.shape[1]], first).then_inc(first_loaded, 16)
                for signal, to, source in start_fetches(0):
                    sp.dma_start(to, source).then_inc(signal, 16)
                sp.wait_ge(w_loaded, 16)

            @block.vector
            def _(dve):
                dve.wait_ge(loaded_consts, 32)
                dve.tensor_copy(net.select[:, :, :], raw_select)
                dve.tensor_copy(net.ident16, net.ident)
                dve.tensor_copy(net.causal16, net.causal[:, BANK - P:BANK])
                dve.tensor_copy(net.causal_cols16, net.causal_cols)
        ternary(net, ternary_w)
        packs_d = {**packs_d, "L1_ffn": ternary_d}

        def change_batch(to, source):
            output = source is xn
            with net.block() as (block, sem):
                out_ready, turned_done = sem("output copied"), sem("context transposed")
                stored = sem("output stored")

                @block.sync
                def _(sp):
                    if output:
                        sp.wait_ge(out_ready, 1)
                    sp.dma_start(to, source[:, :, :] if output else source).then_inc(stored, 16)
                    sp.wait_ge(stored, 16)
                    sp.wait_ge(first_loaded, 16)

                @block.tensor
                def _(pe):
                    pe.wait_ge(ctx_loaded, 16)
                    for c in range(NC):
                        for t in range(NT):
                            mm = pe.transpose(net.psum[:, c, t * P:(t + 1) * P], ct[:, t, c * P:(c + 1) * P], net.ident)
                        mm.then_inc(turned_done, 1)

                @block.scalar
                def _(act):
                    for c in range(NC):
                        act.wait_ge(turned_done, c + 1)
                        act.activation(cc[:, c, :], net.psum[:, c, :], ACT.Copy)

                @block.vector
                def _(dve):
                    if output:
                        dve.tensor_copy(xn[:, :, :], x[:, :, :]).then_inc(out_ready, 1)
                        dve.wait_ge(out_ready, 1)
                    dve.wait_ge(x_loaded, 16)
                    dve.tensor_copy(x[:, :, :], x_next)

        change_batch(ternary_d, arenas[1][:, 0:width])
        blocks_start = net.turn
        with nc.Fori(0, batches) as b:
            with net.block() as (block, sem):
                @block.gpsimd
                def _(pool):
                    pool.sem_clear(range(first_loaded.num, ctx_loaded.num + 1))
            for s, name in enumerate(sublayers):
                arena = arenas[SUBLAYERS.index(name) % 2]
                W = {field: arena[:, at:at + n] for field, (at, n) in offsets(WIDTHS[name])[0].items()}
                if s + 1 < len(sublayers):
                    nxt, signal = packs_d[sublayers[s + 1]], loaded[(s + 1) % 2]
                    to = arenas[SUBLAYERS.index(sublayers[s + 1]) % 2]
                else:
                    nxt, signal, to = first, first_loaded, first_arena
                fetches = [(signal, to[:, 0:nxt.shape[1]], nxt)]
                if s + 1 == len(sublayers):
                    fetches += start_fetches(b + 1)
                if name == "L2_xattn":
                    fetches += [(mask_loaded, raw_mask[:, i, :, :], m[b].rearrange("(t p) k -> p t k", p=P))
                                for i, m in enumerate((mask_d, mask_t_d))]
                with ExitStack() as around:
                    parts = None
                    if name in ("L0_ffn", "L1_ffn"):
                        parts = [net.sbuf(f"xc_{part}", [P, NC, T], F32R, ctx=around) for part in ("high", "low")]
                    layernorm(net, x, xn, xc, W.get("bo"), fetches=fetches,
                              need=(loaded[s % 2], 16 * ((s + 1) // 2)) if s else None, parts=parts)
                    BODIES[name](net, W, x=x, xn=xn, xc=xc, ct=ct, cc=cc, raw_mask=raw_mask, mask_loaded=mask_loaded, room=room,
                                 kmask=kmask_d, w1=w1_d, w2=w2_d, arena=arena, b=b, parts=parts)
            change_batch(out_d[b].rearrange("(t p) d -> p t d", p=P), xn)
            if net.turn != blocks_start:
                with net.block() as (block, sem):
                    pass



def by_chunk(w):
    k, n = w.shape
    return w.reshape(k // P, P, n).transpose(1, 0, 2).reshape(P, -1)


def on_rows(a, rows=P):
    out = np.zeros((P, a.shape[-1]), np.float32)
    out[:a.shape[0]] = a
    return out


def on_every_row(a):
    return np.tile(a[None], (P, 1))


def apart(w):
    out = np.zeros((w.shape[0], H, PITCH), np.float32)
    out[:, :, :HD] = w.reshape(w.shape[0], H, HD)
    return out.reshape(w.shape[0], H * PITCH)


def apart_rows(w):
    return np.ascontiguousarray(apart(np.ascontiguousarray(w.T)).T)


def blocks_of(w):
    out = np.zeros((H, HD, H, HD), np.float32)
    for h in range(H):
        out[h, :, h, :] = w
    return out.reshape(D, D)


def by_head(w):
    out = np.zeros((HD, H, HD, H), np.float32)
    for h in range(H):
        out[:, h, :, h] = w[:, :, h]
    return out.reshape(D, D)


def pack(i):
    f32 = np.float32
    evens = np.r_[0:D:2, 1:D:2]
    half = D // 2
    inv = (1.0 / 10000.0 ** (np.arange(half, dtype=f32) / f32(half))).astype(f32)
    ang = (np.arange(T, dtype=f32)[None, :] * inv[:, None]).astype(f32)
    inv3 = (1.0 / 10000.0 ** (np.arange(0, HD, 2, dtype=f32) / f32(HD))).astype(f32)
    ang3 = np.repeat((np.arange(T, dtype=f32)[None, :] * inv3[:, None]).astype(f32), 2, axis=0)
    sign = np.tile(np.array([-1.0, 1.0], f32), HD // 2)[:, None]
    cos3, sin3 = (np.tile(a, (P // HD, 1)) for a in (np.cos(ang3), np.sin(ang3) * sign))
    swap = np.arange(D).reshape(-1, 2)[:, ::-1].reshape(-1)
    qkv3 = i["L3_attn_Wqkv"]
    cols = lambda v: np.ascontiguousarray(v.reshape(-1, P).T)
    spread = np.zeros((2 * SLOTS, SLOTS * SLOTD), f32)
    for s in range(SLOTS):
        spread[[s, SLOTS + s], s * SLOTD:(s + 1) * SLOTD] = 1.0
    packs = {
        "L0_attn": dict(wq=by_chunk(by_head(i["L0_attn_w_q"])[:, evens]), wk=by_chunk(by_head(i["L0_attn_w_k"])[:, evens]),
                        wv=by_chunk(by_head(i["L0_attn_w_v"])), cos=np.cos(ang), sin=np.sin(ang)),
        "L0_xattn": dict(wq=by_chunk(blocks_of(i["L0_xattn_Wq"].T)), wk=by_chunk(blocks_of(i["L0_xattn_Wk"].T)),
                         wv=by_chunk(blocks_of(i["L0_xattn_Wv"].T)), wo=by_chunk(apart_rows(i["L0_xattn_Wo"].T)),
                         bo=on_every_row(i["L0_xattn_bo"])),
        "L0_ffn": dict(sim=by_chunk(i["L0_ffn_sim_matrix"]), gates=np.tile(i["L0_ffn_gates"][None], (P, 1)),
                       **{j: by_chunk(i[f"L0_ffn_{j}_proj"].transpose(1, 0, 2).reshape(D, MIX * MIXD)) for j in "qkv"},
                       o=by_chunk(i["L0_ffn_o_proj"].reshape(MIX * MIXD, D))),
        "L1_attn": dict(wq=by_chunk(i["L1_attn_Wq"].T), wk=by_chunk(i["L1_attn_Wkv"][:D].T),
                        wv=by_chunk(i["L1_attn_Wkv"][D:].T), wo=by_chunk(apart_rows(i["L1_attn_Wo"].T))),
        "L1_xattn": dict(**{f"w{j}": by_chunk(i[f"L1_xattn_W{j}"]) for j in "qkvo"}, bq=cols(i["L1_xattn_bq"]),
                         bk=cols(i["L1_xattn_bk"]), bv=on_every_row(i["L1_xattn_bv"]), bo=on_every_row(i["L1_xattn_bo"])),
        "L1_ffn": dict(fc=by_chunk(i["L1_ffn_W_fc"].T), proj=by_chunk(i["L1_ffn_W_proj"].T), ln_w=cols(i["L1_ffn_ln_w"]),
                       ln_b=cols(i["L1_ffn_ln_b"])),
        "L2_attn": dict(wqkv=by_chunk(i["L2_attn_Wqkv"]), bqkv=on_every_row(i["L2_attn_bqkv"]), gq=cols(i["L2_attn_gamma_q"]),
                        hq=cols(i["L2_attn_beta_q"]), gk=cols(i["L2_attn_gamma_k"]), hk=cols(i["L2_attn_beta_k"]),
                        wo=by_chunk(apart_rows(i["L2_attn_Wo"])), bo=on_every_row(i["L2_attn_bo"])),
        "L2_xattn": dict(wq=by_chunk(i["L2_xattn_Wq"].T), wk=by_chunk(i["L2_xattn_Wk"].T), wv=by_chunk(i["L2_xattn_Wv"].T),
                         wo=by_chunk(i["L2_xattn_Wo"].T),
                         bq=cols(i["L2_xattn_bq"]), bk=cols(i["L2_xattn_bk"]), bv=on_every_row(i["L2_xattn_bv"]),
                         bo=on_every_row(i["L2_xattn_bo"])),
        "L2_ffn": dict(rms=cols(i["L2_ffn_rms_w"]), gate=by_chunk(i["L2_ffn_gate_w"].T),
                       b1=np.ascontiguousarray(i["L2_ffn_b1"].reshape(EXPERTS * HIDDEN_CHUNKS, P).T), b2=on_rows(i["L2_ffn_b2"])),
        "L3_attn": dict(wq=by_chunk(qkv3[:, :D]), wqr=by_chunk(qkv3[:, :D][:, swap]),
                        wk=by_chunk(qkv3[:, D:2 * D]), wkr=by_chunk(qkv3[:, D:2 * D][:, swap]),
                        wv=by_chunk(qkv3[:, 2 * D:]), wo=by_chunk(apart_rows(i["L3_attn_Wout"])),
                        cos=cos3, sin=sin3, bo=on_every_row(i["L3_attn_bout"])),
        "L3_xattn": dict(w=by_chunk(i["L3_xattn_W"].T), b=cols(i["L3_xattn_b"]), d=cols(i["L3_xattn_D"][0])),
        "L3_ffn": dict(hash=by_chunk(i["L3_ffn_hasher_w"].T), keys=on_rows(i["L3_ffn_keys"].T),
                       down=by_chunk(i["L3_ffn_values_down"].transpose(1, 0, 2).reshape(D, SLOTS * SLOTD)),
                       up=by_chunk(i["L3_ffn_values_up"].reshape(SLOTS * SLOTD, D)), spread=spread,
                       scale=np.tile(i["L3_ffn_scale"][None], (P, 1))),
    }
    out = {}
    for name, fields in WIDTHS.items():
        parts = [packs[name][field] for field, _ in fields]
        assert [p.shape for p in parts] == [(P, n) for _, n in fields], (name, [p.shape for p in parts])
        out[name] = np.ascontiguousarray(np.concatenate(parts, 1), dtype=f32)
    return out


def constants():
    f32 = np.float32
    causal = np.zeros((P, BANK), f32)
    causal[:, BANK - P:] = np.where(np.arange(P)[None, :] > np.arange(P)[:, None], f32(MASKED), f32(0))
    gather, scatter = np.zeros((P, PITCH), f32), np.zeros((P, GROUPS, P), f32)
    for h in range(4):
        gather[h * PITCH + HD, h * 8:(h + 1) * 8] = 1.0
        for c in range(GROUPS):
            scatter[c * PITCH + h * 8, c, h * PITCH:(h + 1) * PITCH] = 1.0
    guard8, guard6 = (np.zeros((P, 1), f32) for _ in range(2))
    guard8[HD::PITCH], guard6[HD::PITCH] = 1e-8, 1e-6
    ones_k = np.zeros((P, 1), f32)
    for h in range(2):
        ones_k[h * STACK + SPARE:h * STACK + SPARE + 2] = 1.0
    fields = dict(ident=np.eye(P, dtype=f32), causal=causal, gather=gather, scatter=scatter.reshape(P, GROUPS * P), guard8=guard8, guard6=guard6, ones_k=ones_k,
                  iota=np.tile(np.arange(64, dtype=f32)[None], (P, 1)), ones=np.ones((P, P), f32),
                  half=np.full((P, 16), 0.5, f32), minus_half=np.full((P, 16), -0.5, f32),
                  causal_cols=np.ascontiguousarray(causal[:, BANK - P:].T))
    return np.concatenate([fields[name] for name, _ in CONSTS], 1)


def selection():
    out = np.zeros((P, 4, 4, 2, 4, HD), np.float32)
    for which, places in enumerate(((0, 2), (1,), (0, 1), (2,))):
        for place in places:
            for pair in range(4):
                for head in range(2):
                    at = (2 * pair + head) * HD
                    out[at:at + HD, which, pair, head, place, :] = np.eye(HD)
    return out.reshape(P, 16, P)


def spare(a):
    return np.concatenate([a, a[:1]])


def host_arrays(inputs):
    i = {name: np.asarray(a) for name, a in inputs.items()}
    arrays = {
        "x": spare(i["x"]), "context": spare(i["ctx_1024"]), "mask": i["mask_BxSxS2_ik1"],
        "mask_t": np.ascontiguousarray(i["mask_BxSxS2_ik1"].transpose(0, 2, 1)),
        "key_mask": np.ascontiguousarray(i["mask_BxS2_bf0"]).view(np.int32),
        "w1": np.stack([by_chunk(w) for w in i["L2_ffn_W1"]]), "w2": np.stack([by_chunk(w) for w in i["L2_ffn_W2"]]),
        "consts": constants(), "select": selection(),
    }
    return arrays, pack(i)


def kernel(**inputs):
    import concourse.bacc as _bacc
    from concourse.bass_utils import run_bass_kernel_spmd as _run

    arrays, packs = host_arrays(inputs)
    nc = _bacc.Bacc("TRN2", target_bir_lowering=False, num_devices=1)
    feed, aps = {}, {}
    for name, a in {**arrays, **{f"pack_{k}": v for k, v in packs.items()}}.items():
        feed[f"in_{name}"] = np.ascontiguousarray(a)
        aps[name] = nc.dram_tensor(f"in_{name}", a.shape, mybir.dt.from_np(a.dtype), kind="ExternalInput").ap()
    out = nc.dram_tensor("out", (B, T, D), F32, kind="ExternalOutput").ap()
    ternary = nc.dram_tensor("ternary", (P, pack_width("L1_ffn")), F32, kind="Internal").ap()
    decoder(nc, aps["x"], aps["context"], aps["mask"], aps["mask_t"], aps["key_mask"], aps["w1"], aps["w2"],
            aps["consts"], aps["select"], {k: aps[f"pack_{k}"] for k in packs}, ternary, out)
    r = _run(nc, [feed], core_ids=[0])
    return r.results[0]["out"]
```
